# Optimizing a Trainium2 kernel written in Bass

```python
import numpy as np
import jax
import jax.numpy as jnp

def _softmax(x, axis=-1):
    return jax.nn.softmax(x, axis=axis)

def _gelu(x):
    return jax.nn.gelu(x, approximate=True)

def _silu(x):
    return jax.nn.silu(x)

def _sigmoid(x):
    return jax.nn.sigmoid(x)

def _layernorm(x, axis=-1, eps=1e-05):
    m = jnp.mean(x, axis=axis, keepdims=True)
    v = jnp.var(x, axis=axis, keepdims=True)
    return (x - m) / jnp.sqrt(v + eps)

def _scatter_add(tgt, idx, src, axis=0):
    return tgt.at[idx].add(src)

def _segment_sum(src, seg, n):
    return jax.ops.segment_sum(src, seg, n)
kernel_name = 'mk_gnn_preln_d4_gnn_r32_642b5a'

def setup_inputs(seed: int=0):
    np.random.seed(seed)
    _w = jnp.asarray

    def _rec_inputs():
        import jax
        import jax.numpy as jnp
        _gk = jax.random.key(seed)
        x = -0.000202 + 1 * jax.random.normal(jax.random.fold_in(_gk, 1), (3125, 128), jnp.float32)
        _s = jax.random.randint(jax.random.fold_in(_gk, 2), (25000,), 0, 3125, jnp.int32)
        _d = jax.random.randint(jax.random.fold_in(_gk, 3), (25000,), 0, 3125, jnp.int32)
        _loop = jnp.arange(3125, dtype=jnp.int32)
        src = jnp.concatenate([_s, _d, _loop])
        dst = jnp.concatenate([_d, _s, _loop])
        _o = jnp.argsort(dst, stable=True)
        src = src[_o]
        dst = dst[_o]
        edge_attr_128 = 5.93493e-05 + 1.00006 * jax.random.normal(jax.random.fold_in(_gk, 12), (53125, 128), jnp.float32)
        return (x, src, dst, edge_attr_128)
    x, src, dst, edge_attr_128 = _rec_inputs()

    def _L0_gnn_setup():
        import jax, jax.numpy as jnp
        import numpy as np
        N = 50000
        E = 18750
        D = 128
        key = jax.random.key(seed)
        k_x, k_ei, k_ea, k_w1, k_b1, k_w2, k_b2 = jax.random.split(key, 7)
        x = jax.random.normal(k_x, (N, D), dtype=jnp.float32)
        edge_index = jax.random.randint(k_ei, (2, E), 0, N, dtype=jnp.int64)
        edge_attr = jax.random.normal(k_ea, (E, D), dtype=jnp.float32)
        s1 = 1.0 / np.sqrt(2 * D)
        s2 = 1.0 / np.sqrt(D)
        W1 = jax.random.uniform(k_w1, (2 * D, D), dtype=jnp.float32, minval=-s1, maxval=s1)
        b1 = jax.random.uniform(k_b1, (D,), dtype=jnp.float32, minval=-s1, maxval=s1)
        W2 = jax.random.uniform(k_w2, (D, D), dtype=jnp.float32, minval=-s2, maxval=s2)
        b2 = jax.random.uniform(k_b2, (D,), dtype=jnp.float32, minval=-s2, maxval=s2)
        return {'x': x, 'edge_index': edge_index, 'edge_attr': edge_attr, 'W1': W1, 'b1': b1, 'W2': W2, 'b2': b2}
    _L0_gnn_all = _L0_gnn_setup()
    _L0_gnn_in = {k: v for k, v in _L0_gnn_all.items() if k in ('W1', 'b1', 'W2', 'b2')}
    del _L0_gnn_all

    def _L1_gnn_setup():
        import jax, jax.numpy as jnp
        import numpy as np
        N_NODES = 50000
        N_EDGES = 18750
        HIDDEN = 128
        N_GRAPHS = 32
        key = jax.random.key(seed)
        ks = jax.random.split(key, 8)
        x = jax.random.normal(ks[0], (N_NODES, HIDDEN), dtype=jnp.float32)
        edge_index = jax.random.randint(ks[1], (2, N_EDGES), 0, N_NODES, dtype=jnp.int64)
        edge_attr = jax.random.normal(ks[2], (N_EDGES, HIDDEN), dtype=jnp.float32)
        u = jax.random.normal(ks[3], (N_GRAPHS, HIDDEN), dtype=jnp.float32)
        batch = jax.random.randint(ks[4], (N_NODES,), 0, N_GRAPHS, dtype=jnp.int64)
        s1 = 1.0 / np.sqrt(2 * HIDDEN)
        s2 = 1.0 / np.sqrt(HIDDEN)
        W1 = jax.random.uniform(ks[5], (2 * HIDDEN, HIDDEN), jnp.float32, -s1, s1)
        b1 = jnp.zeros((HIDDEN,), jnp.float32)
        W2 = jax.random.uniform(ks[6], (HIDDEN, HIDDEN), jnp.float32, -s2, s2)
        b2 = jnp.zeros((HIDDEN,), jnp.float32)
        return {'x': x, 'edge_index': edge_index, 'edge_attr': edge_attr, 'u': u, 'batch': batch, 'W1': W1, 'b1': b1, 'W2': W2, 'b2': b2}
    _L1_gnn_all = _L1_gnn_setup()
    _L1_gnn_in = {k: v for k, v in _L1_gnn_all.items() if k in ('u', 'W1', 'b1', 'W2', 'b2')}
    del _L1_gnn_all

    def _L2_gnn_setup():
        import jax, jax.numpy as jnp
        import numpy as np
        N_NODES = 50000
        N_EDGES = 25000
        IN_FEAT = 128
        HID = 64
        OUT = 128

        def gcn_conv(x, src, dst, W, b, n_nodes):
            h = x @ W
            ones = jnp.ones(src.shape[0], dtype=x.dtype)
            deg = jax.ops.segment_sum(ones, dst, num_segments=n_nodes)
            dinv = jax.lax.rsqrt(deg)
            norm = dinv[src] * dinv[dst]
            msg = norm[:, None] * h[src]
            out = jax.ops.segment_sum(msg, dst, num_segments=n_nodes)
            return out + b
        key = jax.random.key(seed)
        k1, k2, k3, k4, k5, k6 = jax.random.split(key, 6)
        x = jax.random.normal(k1, (N_NODES, IN_FEAT), dtype=jnp.float32)
        edge_index = jax.random.randint(k2, (2, N_EDGES), 0, N_NODES, dtype=jnp.int64)
        W1 = jax.random.normal(k3, (IN_FEAT, HID), dtype=jnp.float32) * (1.0 / np.sqrt(IN_FEAT))
        b1 = jnp.zeros((HID,), dtype=jnp.float32)
        W2 = jax.random.normal(k4, (HID, OUT), dtype=jnp.float32) * (1.0 / np.sqrt(HID))
        b2 = jnp.zeros((OUT,), dtype=jnp.float32)
        return {'x': x, 'edge_index': edge_index, 'W1': W1, 'b1': b1, 'W2': W2, 'b2': b2}
    _L2_gnn_all = _L2_gnn_setup()
    _L2_gnn_in = {k: v for k, v in _L2_gnn_all.items() if k in ('W1', 'b1', 'W2', 'b2')}
    del _L2_gnn_all

    def _L3_gnn_setup():
        import jax, jax.numpy as jnp
        import numpy as np
        N = 50000
        E = 20000
        D = 128

        def _lin_init(key, fan_in, fan_out):
            kw, kb = jax.random.split(key)
            bound = 1.0 / np.sqrt(fan_in)
            W = jax.random.uniform(kw, (fan_in, fan_out), jnp.float32, -bound, bound)
            b = jax.random.uniform(kb, (fan_out,), jnp.float32, -bound, bound)
            return (W, b)
        key = jax.random.key(seed)
        ks = jax.random.split(key, 7)
        x = jax.random.normal(ks[0], (N, D), jnp.float32)
        edge_index = jax.random.randint(ks[1], (2, E), 0, N, dtype=jnp.int64)
        edge_attr = jax.random.normal(ks[2], (E, D), jnp.float32)
        msg_w1, msg_b1 = _lin_init(ks[3], 3 * D, D)
        msg_w2, msg_b2 = _lin_init(ks[4], D, D)
        upd_w1, upd_b1 = _lin_init(ks[5], 2 * D, D)
        upd_w2, upd_b2 = _lin_init(ks[6], D, D)
        return {'x': x, 'edge_index': edge_index, 'edge_attr': edge_attr, 'msg_w1': msg_w1, 'msg_b1': msg_b1, 'msg_w2': msg_w2, 'msg_b2': msg_b2, 'upd_w1': upd_w1, 'upd_b1': upd_b1, 'upd_w2': upd_w2, 'upd_b2': upd_b2}
    _L3_gnn_all = _L3_gnn_setup()
    _L3_gnn_in = {k: v for k, v in _L3_gnn_all.items() if k in ('msg_w1', 'msg_b1', 'msg_w2', 'msg_b2', 'upd_w1', 'upd_b1', 'upd_w2', 'upd_b2')}
    del _L3_gnn_all
    return {'x': x, 'src': src, 'dst': dst, 'edge_attr_128': edge_attr_128, 'L0_gnn_W1': _L0_gnn_in['W1'], 'L0_gnn_b1': _L0_gnn_in['b1'], 'L0_gnn_W2': _L0_gnn_in['W2'], 'L0_gnn_b2': _L0_gnn_in['b2'], 'L1_gnn_u': _L1_gnn_in['u'], 'L1_gnn_W1': _L1_gnn_in['W1'], 'L1_gnn_b1': _L1_gnn_in['b1'], 'L1_gnn_W2': _L1_gnn_in['W2'], 'L1_gnn_b2': _L1_gnn_in['b2'], 'L2_gnn_W1': _L2_gnn_in['W1'], 'L2_gnn_b1': _L2_gnn_in['b1'], 'L2_gnn_W2': _L2_gnn_in['W2'], 'L2_gnn_b2': _L2_gnn_in['b2'], 'L3_gnn_msg_w1': _L3_gnn_in['msg_w1'], 'L3_gnn_msg_b1': _L3_gnn_in['msg_b1'], 'L3_gnn_msg_w2': _L3_gnn_in['msg_w2'], 'L3_gnn_msg_b2': _L3_gnn_in['msg_b2'], 'L3_gnn_upd_w1': _L3_gnn_in['upd_w1'], 'L3_gnn_upd_b1': _L3_gnn_in['upd_b1'], 'L3_gnn_upd_w2': _L3_gnn_in['upd_w2'], 'L3_gnn_upd_b2': _L3_gnn_in['upd_b2']}

def reference(x, src, dst, edge_attr_128, L0_gnn_W1, L0_gnn_b1, L0_gnn_W2, L0_gnn_b2, L1_gnn_u, L1_gnn_W1, L1_gnn_b1, L1_gnn_W2, L1_gnn_b2, L2_gnn_W1, L2_gnn_b1, L2_gnn_W2, L2_gnn_b2, L3_gnn_msg_w1, L3_gnn_msg_b1, L3_gnn_msg_w2, L3_gnn_msg_b2, L3_gnn_upd_w1, L3_gnn_upd_b1, L3_gnn_upd_w2, L3_gnn_upd_b2):
    import jax
    import jax.numpy as jnp

    def _L0_gnn_ref(x, edge_index, edge_attr, W1, b1, W2, b2):
        import jax, jax.numpy as jnp
        import numpy as np
        N = 50000
        E = 18750
        D = 128
        row, col = (edge_index[0], edge_index[1])
        edge_aggr = jnp.zeros((x.shape[0], edge_attr.shape[1]), dtype=x.dtype)
        edge_aggr = edge_aggr.at[row].add(edge_attr).at[col].add(edge_attr)
        node_features = jnp.concatenate([x, edge_aggr], axis=1)
        h = jax.nn.relu(node_features @ W1 + b1)
        return h @ W2 + b2

    def _L1_gnn_ref(x, edge_index, edge_attr, u, batch, W1, b1, W2, b2):
        import jax, jax.numpy as jnp
        import numpy as np
        N_NODES = 50000
        N_EDGES = 18750
        HIDDEN = 128
        N_GRAPHS = 32
        col = edge_index[1]
        agg = jax.ops.segment_sum(edge_attr, col, num_segments=x.shape[0])
        combined = jnp.concatenate([x, agg], axis=1)
        h = jax.nn.relu(combined @ W1 + b1)
        return h @ W2 + b2

    def _L2_gnn_ref(x, edge_index, W1, b1, W2, b2):
        import jax, jax.numpy as jnp
        import numpy as np
        N_NODES = 50000
        N_EDGES = 25000
        IN_FEAT = 128
        HID = 64
        OUT = 128

        def gcn_conv(x, src, dst, W, b, n_nodes):
            h = x @ W
            ones = jnp.ones(src.shape[0], dtype=x.dtype)
            deg = jax.ops.segment_sum(ones, dst, num_segments=n_nodes)
            dinv = jax.lax.rsqrt(deg)
            norm = dinv[src] * dinv[dst]
            msg = norm[:, None] * h[src]
            out = jax.ops.segment_sum(msg, dst, num_segments=n_nodes)
            return out + b
        n = x.shape[0]
        loops = jnp.arange(n, dtype=edge_index.dtype)
        src = jnp.concatenate([edge_index[0], loops])
        dst = jnp.concatenate([edge_index[1], loops])
        h = gcn_conv(x, src, dst, W1, b1, n)
        h = jax.nn.relu(h)
        out = gcn_conv(h, src, dst, W2, b2, n)
        return out

    def _L3_gnn_ref(x, edge_index, edge_attr, msg_w1, msg_b1, msg_w2, msg_b2, upd_w1, upd_b1, upd_w2, upd_b2):
        import jax, jax.numpy as jnp
        import numpy as np
        N = 50000
        E = 20000
        D = 128

        def _lin_init(key, fan_in, fan_out):
            kw, kb = jax.random.split(key)
            bound = 1.0 / np.sqrt(fan_in)
            W = jax.random.uniform(kw, (fan_in, fan_out), jnp.float32, -bound, bound)
            b = jax.random.uniform(kb, (fan_out,), jnp.float32, -bound, bound)
            return (W, b)
        row, col = (edge_index[0], edge_index[1])
        num_nodes = x.shape[0]
        m_in = jnp.concatenate([x[row], x[col], edge_attr], axis=-1)
        h = jax.nn.relu(m_in @ msg_w1 + msg_b1)
        messages = h @ msg_w2 + msg_b2
        summed = jax.ops.segment_sum(messages, col, num_segments=num_nodes)
        counts = jax.ops.segment_sum(jnp.ones((messages.shape[0],), messages.dtype), col, num_segments=num_nodes)
        aggregated = jnp.where(counts[:, None] > 0, summed / jnp.maximum(counts, 1.0)[:, None], jnp.zeros_like(summed))
        u_in = jnp.concatenate([x, aggregated], axis=-1)
        updated = jax.nn.relu(u_in @ upd_w1 + upd_b1) @ upd_w2 + upd_b2
        return updated
    edge_index = jnp.stack([src, dst])
    batch0 = jnp.zeros((3125,), jnp.int32)
    h = jnp.maximum(_layernorm(x, axis=-1), 0.0)
    x = x + _L0_gnn_ref(h, edge_index, edge_attr_128, L0_gnn_W1, L0_gnn_b1, L0_gnn_W2, L0_gnn_b2)
    h = jnp.maximum(_layernorm(x, axis=-1), 0.0)
    x = x + _L1_gnn_ref(h, edge_index, edge_attr_128, L1_gnn_u, batch0, L1_gnn_W1, L1_gnn_b1, L1_gnn_W2, L1_gnn_b2)
    h = jnp.maximum(_layernorm(x, axis=-1), 0.0)
    x = x + _L2_gnn_ref(h, edge_index, L2_gnn_W1, L2_gnn_b1, L2_gnn_W2, L2_gnn_b2)
    h = jnp.maximum(_layernorm(x, axis=-1), 0.0)
    x = x + _L3_gnn_ref(h, edge_index, edge_attr_128, L3_gnn_msg_w1, L3_gnn_msg_b1, L3_gnn_msg_w2, L3_gnn_msg_b2, L3_gnn_upd_w1, L3_gnn_upd_b1, L3_gnn_upd_w2, L3_gnn_upd_b2)
    return x

_drawn_inputs = setup_inputs


def setup_inputs(seed=0):
    import zlib

    import numpy as np

    out = dict(_drawn_inputs(seed))
    spreads = {'L1_gnn_b1': (0.0, 0.341),
     'L1_gnn_b2': (0.0, 0.1),
     'L2_gnn_b1': (0.0, 0.1),
     'L2_gnn_b2': (0.0, 0.1)}
    factors = {'L0_gnn_b1': 6.161,
     'L3_gnn_msg_w1': 6.214,
     'L3_gnn_msg_b1': 8.0,
     'L3_gnn_msg_w2': 3.745,
     'L3_gnn_msg_b2': 8.0,
     'L3_gnn_upd_b1': 6.422}
    for name, (base, spread) in spreads.items():
        noise = np.random.default_rng([zlib.crc32(name.encode()), seed]).standard_normal(out[name].shape)
        drawn = base * np.exp(spread * noise) if base else spread * noise
        out[name] = jnp.asarray(drawn.astype(out[name].dtype))
    for name, factor in factors.items():
        out[name] = (out[name] * factor).astype(out[name].dtype)
    return out
```

```python
import numpy as np
import concourse.bass as bass
from concourse import mybir
from contextlib import ExitStack

F32 = mybir.dt.float32
I32 = mybir.dt.int32
BF16 = mybir.dt.bfloat16
ALU = mybir.AluOpType
ACT = mybir.ActivationFunctionType
AX = mybir.AxisListType

P = 128
N, E, D, H2 = 3125, 53125, 128, 64
NB = -(-N // P)
NP = NB * P
NLAST = N - (NB - 1) * P
EC = -(-E // P)
EP = EC * P
ELAST = E - (EC - 1) * P
ET = -(-EC // P)
NK = NB + 1
G = 2
SLOT = G * P
SLOTS = (E + NB * (SLOT - 1)) // SLOT
BUF = 4
SLOTS = -(-SLOTS // BUF) * BUF
ST = -(-SLOTS // P)
RW = D + 2
BANK = 512
BANKS = -(-NP // BANK)
MASKED = 4096.0
EPS = 1e-5
KC = 4


class Signal:

    def __init__(self, handle):
        self.h, self.base = handle, 0

    def at(self, n):
        return self.base + n

    def passed(self, n):
        self.base += n


def banks():
    return [(k, BANK * k, min(BANK, NP - BANK * k)) for k in range(BANKS)]


def build(nc, x, src, dst, ea, l0, l1, l2, l3, out):
    ctx = ExitStack()
    with ctx:
        nc_ctx = ctx.enter_context(nc.allow_non_contiguous_dma(reason="small tables and bias columns"))

        def sb(name, shape, dt=F32):
            return ctx.enter_context(nc.sbuf_tensor(name, shape, dt))

        def signal(name):
            return Signal(ctx.enter_context(nc.semaphore(name)))

        def dram(name, shape, dt=F32):
            return nc.dram_tensor(name, shape, dt, kind="Internal").ap()

        rows_by_src = dram("rows_by_src", (EP, RW))
        rows_by_dst = dram("rows_by_dst", (EP, RW))
        tab_i_dram = [dram(f"tab_i{k}", (2, ST * P), I32) for k in range(2)]
        tab_f_dram = [dram(f"tab_f{k}", (2, ST * P)) for k in range(2)]
        z_table = [dram(f"z_table{k}", (NP, H2)) for k in range(2)]
        p_table = dram("p_table", (NP, D))
        deg_dram = dram("deg_dram", (3, NP))

        x_nm = sb("x_nm", [P, NB, D])
        agg_dst = sb("agg_dst", [P, NP])
        agg_sum = sb("agg_sum", [P, NP])
        node_bc = sb("node_bc", [P, 3, NP])
        stats = sb("stats", [P, NB, 6])
        mv = sb("mv", [P, NB, 2])
        rstd = sb("rstd", [P, NB])
        deg = sb("deg", [P, 3, NB])
        deg_root = sb("deg_root", [P, NB])
        std = sb("std", [P, NB])

        iota_i = sb("iota_i", [P, P], I32)
        part_i = sb("part_i", [P, 1], I32)
        slot_i = sb("slot_i", [P, ST], I32)
        place_i = sb("place_i", [P, G], I32)
        iota = sb("iota", [P, P])
        iota_b = sb("iota_b", [P, P], BF16)
        part = sb("part", [P, 1])
        slot_id = sb("slot_id", [P, ST])
        place = sb("place", [P, G])
        ident = sb("ident", [P, P])
        lower = sb("lower", [P, P])
        ones = sb("ones", [P, EC])
        zeros = sb("zeros", [1, BANK])

        w_l0 = sb("w_l0", [P, 2, D])
        w_l1 = sb("w_l1", [P, 2, D])
        w2_l0 = sb("w2_l0", [P, D])
        w2_l1 = sb("w2_l1", [P, D])
        w1_g = sb("w1_g", [P, H2])
        w2_g = sb("w2_g", [H2, D])
        w_msg = sb("w_msg", [P, 3, D])
        w2_msg = sb("w2_msg", [P, D])
        w_upd = sb("w_upd", [P, 2, D])
        w2_upd = sb("w2_upd", [P, D])
        b_cols = sb("b_cols", [P, 4])
        b_rows = sb("b_rows", [1, 6, D])

        tab_row = sb("tab_row", [1, 2, 2, ST * P], I32)
        tab_bc = sb("tab_bc", [P, 2, 2, ST * P])
        shift = sb("shift", [P, 2, SLOTS, G])
        rel = sb("rel", [P, SLOTS * G])
        src_i = sb("src_i", [P, SLOTS * G], I32)

        sort_scope = ExitStack()

        def grid_sb(name, shape, dt=F32):
            return sort_scope.enter_context(nc.sbuf_tensor(name, shape, dt))

        idx_i = grid_sb("idx_i", [P, 2, ET, P], I32)
        idx_f = grid_sb("idx_f", [P, 2, ET, P])
        keys = grid_sb("keys", [P, 2, EC])
        pair_i = grid_sb("pair_i", [P, EC, 2], I32)
        buck_i = grid_sb("buck_i", [P, EC], I32)
        lo_i = grid_sb("lo_i", [P, EC], I32)
        lo_f = grid_sb("lo_f", [P, EC])
        buck = grid_sb("buck", [P, EC])
        hot = grid_sb("hot", [P, NK, EC], BF16)
        ranks = grid_sb("ranks", [P, EC])
        picked = grid_sb("picked", [P, EC])
        pos = grid_sb("pos", [P, EC])
        pos_i = grid_sb("pos_i", [P, 2, EC], I32)
        cnt = grid_sb("cnt", [P, NK])
        tot = grid_sb("tot", [P, NK])
        first = grid_sb("first", [P, NK])
        offs = grid_sb("offs", [P, NK])
        need_i = grid_sb("need_i", [P, NB], I32)
        need = grid_sb("need", [P, NB])
        ends = grid_sb("ends", [P, NB])
        slack = grid_sb("slack", [P, NB])
        passed = grid_sb("passed", [P, ST, NB])
        past = grid_sb("past", [P, ST, NB])
        blk = grid_sb("blk", [P, ST])
        start = grid_sb("start", [P, ST])
        tab_i = grid_sb("tab_i", [P, 2, ST], I32)
        tab_f = grid_sb("tab_f", [P, 2, ST])
        hot_lo = grid_sb("hot_lo", [P, 4, P], BF16)
        posq = grid_sb("posq", [P, 2, BUF, KC], I32)
        srow = grid_sb("srow", [P, BUF, KC, RW])

        acc = ctx.enter_context(nc.psum_tensor("acc", [P, BANKS * BANK], F32))

        loaded = signal("loaded")
        iotas = signal("iotas")
        vec = signal("vec")
        vec2 = signal("vec2")
        turned_in = signal("turned_in")
        sums = signal("sums")
        tabs_out = signal("tabs_out")
        tabs_in = signal("tabs_in")
        cnt_ready = signal("cnt_ready")
        tab_ready = signal("tab_ready")
        lo_hot = signal("lo_hot")
        lo_used = signal("lo_used")
        cleared = signal("cleared")
        rooted = signal("rooted")

        def bank_pair(i):
            return acc[:, BANK * i:BANK * i + BANK]

        with nc.Block() as block:
            @block.sync
            def _(sp):

                def load(to, of):
                    sp.dma_start(to, of).then_inc(loaded.h, 16)

                full = (EC - 1) // P * P
                for k, of in ((0, src), (1, dst)):
                    load(idx_i[:, k, 0:full // P, :], of[0:full * P].rearrange("(t c e) -> c t e", t=full // P, e=P))
                load(x_nm[:, 0:NB - 1, :], x[0:(NB - 1) * P, :].rearrange("(b p) f -> p b f", p=P))
                sp.wait_ge(vec.h, vec.at(3))
                for k, of in ((0, src), (1, dst)):
                    load(idx_i[0:EC - 1 - full, k, ET - 1, :], of[full * P:(EC - 1) * P].rearrange("(c e) -> c e", e=P))
                    load(idx_i[EC - 1 - full:EC - full, k, ET - 1, 0:ELAST], of[(EC - 1) * P:E].rearrange("(c e) -> c e", c=1))
                load(x_nm[0:NLAST, NB - 1, :], x[(NB - 1) * P:N, :])
                for to, of in ((w_l0, l0[0]), (w_l1, l1[0]), (w_msg, l3[0]), (w_upd, l3[4])):
                    load(to[:, :, :], of.rearrange("(k p) f -> p k f", p=P))
                for to, of in ((w2_l0, l0[2]), (w2_l1, l1[2]), (w1_g, l2[0]), (w2_g, l2[2]), (w2_msg, l3[2]), (w2_upd, l3[6])):
                    load(to[:, :], of)
                for k, of in enumerate((l0[1], l1[1], l2[1], l3[5])):
                    load(b_cols[0:of.shape[0], k:k + 1], of.rearrange("(p a) -> p a", a=1))
                for k, of in enumerate((l0[3], l1[3], l2[3], l3[7], l3[1], l3[3])):
                    load(b_rows[:, k, :], of.rearrange("(a f) -> a f", a=1))
                sp.wait_ge(loaded.h, loaded.at(16 * 28))

            @block.gpsimd
            def _(pool):
                pool.iota(iota_i[:, :], [[1, P]], base=0, channel_multiplier=0)
                pool.iota(part_i[:, :], [[1, 1]], base=0, channel_multiplier=1)
                pool.iota(slot_i[:, :], [[P, ST]], base=0, channel_multiplier=1)
                pool.iota(place_i[:, :], [[1, G]], base=0, channel_multiplier=G).then_inc(iotas.h, 1)

            @block.vector
            def _(dve):
                dve.memset(x_nm[:, NB - 1, :], 0.0).then_inc(vec.h, 1)
                dve.memset(idx_i[:, :, ET - 1, :], NP).then_inc(vec.h, 1)
                dve.memset(b_cols[:, :], 0.0).then_inc(vec.h, 1)
                dve.memset(ones[:, :], 1.0)
                dve.memset(zeros[:, :], 0.0)
                dve.wait_ge(iotas.h, iotas.at(1))
                dve.tensor_copy(iota[:, :], iota_i[:, :]).then_inc(vec.h, 1)
                dve.tensor_copy(iota_b[:, :], iota_i[:, :])
                dve.tensor_copy(part[:, :], part_i[:, :]).then_inc(vec.h, 1)
                dve.tensor_copy(slot_id[:, :], slot_i[:, :])
                dve.tensor_copy(place[:, :], place_i[:, :])
                dve.wait_ge(vec.h, vec.at(5))
                dve.tensor_scalar(ident[:, :], iota[:, :], part[:, :], None, ALU.is_equal)
                dve.tensor_scalar(lower[:, :], iota[:, :], part[:, :], None, ALU.is_gt)
        vec.passed(5)
        loaded.passed(16 * 28)
        iotas.passed(1)

        with nc.Block() as block:
            @block.vector
            def _(dve):
                dve.tensor_copy(idx_f[:, :, :, :], idx_i[:, :, :, :]).then_inc(vec.h, 1)
                for k in range(2):
                    dve.wait_ge(turned_in.h, turned_in.at(k + 1))
                    dve.tensor_copy(keys[:, k, :], acc[:, BANK * k:BANK * k + EC])
                    dve.tensor_copy(pair_i[:, :, k], acc[:, BANK * k:BANK * k + EC])

            @block.tensor
            def _(pe):
                pe.wait_ge(vec.h, vec.at(1))
                for k in range(2):
                    for t in range(ET):
                        w = min(P, EC - t * P)
                        last = pe.transpose(acc[:, BANK * k + t * P:BANK * k + t * P + w], idx_f[0:w, k, t, :], ident[0:w, 0:w])
                    last.then_inc(turned_in.h, 1)
        vec.passed(1)
        turned_in.passed(2)

        def order(which):
            with nc.Block() as block:
                @block.vector
                def _(dve):
                    n = [0]

                    def step(ins):
                        n[0] += 1
                        ins.then_inc(vec.h, 1)
                        dve.wait_ge(vec.h, vec.at(n[0]))

                    step(dve.tensor_copy(lo_i[:, :], keys[:, which, :]))
                    dve.tensor_scalar(buck_i[:, :], lo_i[:, :], 7, None, ALU.logical_shift_right).then_inc(vec.h, 1)
                    n[0] += 1
                    dve.wait_ge(vec.h, vec.at(n[0]))
                    step(dve.tensor_copy(buck[:, :], buck_i[:, :]))
                    for b in range(NK):
                        ins = dve.tensor_scalar(hot[:, b, :], buck[:, :], float(b), 0.0, ALU.is_equal, ALU.add,
                                                accum_out=cnt[:, b:b + 1])
                    n[0] += 1
                    ins.then_inc(vec.h, 1)
                    ins2 = dve.memset(pos[:, :], 0.0)
                    ins2.then_inc(cnt_ready.h, 1)
                    dve.wait_ge(sums.h, sums.at(1))
                    step(dve.tensor_copy(tot[:, :], acc[:, BANK:BANK + NK]))
                    step(dve.tensor_tensor_scan(first[:, :], ones[:, 0:NK], tot[:, :], 0.0, ALU.mult, ALU.add))
                    step(dve.tensor_tensor(first[:, :], first[:, :], tot[:, :], ALU.subtract))
                    step(dve.scalar_tensor_tensor(offs[:, :], acc[:, 0:NK], -1.0, first[:, :], ALU.add, ALU.add))
                    for b in range(NK):
                        step(dve.tensor_tensor_scan(ranks[:, :], ones[:, :], hot[:, b, :], offs[:, b:b + 1], ALU.mult, ALU.add))
                        step(dve.tensor_tensor(picked[:, :], ranks[:, :], hot[:, b, :], ALU.mult))
                        step(dve.tensor_tensor(pos[:, :], pos[:, :], picked[:, :], ALU.add))
                    dve.tensor_copy(pos_i[:, which, :], pos[:, :])
                    step(dve.tensor_scalar(need[:, :], tot[:, 0:NB], float(SLOT - 1), None, ALU.add))
                    step(dve.tensor_copy(need_i[:, :], need[:, :]))
                    step(dve.tensor_scalar(need_i[:, :], need_i[:, :], SLOT.bit_length() - 1, None, ALU.logical_shift_right))
                    step(dve.tensor_copy(need[:, :], need_i[:, :]))
                    step(dve.tensor_tensor_scan(ends[:, :], ones[:, 0:NB], need[:, :], 0.0, ALU.mult, ALU.add))
                    step(dve.scalar_tensor_tensor(slack[:, :], need[:, :], -float(SLOT), tot[:, 0:NB], ALU.mult, ALU.add))
                    for j in range(ST):
                        step(dve.tensor_scalar(passed[:, j, :], ends[:, :], slot_id[:, j:j + 1], None, ALU.is_le))
                        step(dve.tensor_tensor(past[:, j, :], passed[:, j, :], slack[:, :], ALU.mult))
                    step(dve.tensor_reduce(blk[:, :], passed[:, :, :], AX.X, ALU.add))
                    step(dve.tensor_reduce(start[:, :], past[:, :, :], AX.X, ALU.add))
                    step(dve.scalar_tensor_tensor(start[:, :], slot_id[:, :], float(SLOT), start[:, :], ALU.mult, ALU.add))
                    step(dve.tensor_scalar(past[:, 0, 0:ST], start[:, :], float(E - SLOT), None, ALU.min))
                    step(dve.tensor_tensor(tab_f[:, 0, :], start[:, :], past[:, 0, 0:ST], ALU.subtract))
                    step(dve.tensor_copy(tab_i[:, 0, :], past[:, 0, 0:ST]))
                    step(dve.tensor_scalar(tab_f[:, 1, :], blk[:, :], float(NB - 1), float(P), ALU.min, ALU.mult))
                    dve.tensor_copy(tab_i[:, 1, :], tab_f[:, 1, :]).then_inc(tab_ready.h, 1)
                    dve.wait_ge(tabs_in.h, tabs_in.at(32))
                    for j in range(G):
                        step(dve.tensor_scalar(shift[:, which, :, j], tab_bc[:, which, 0, 0:SLOTS], place[:, j:j + 1], MASKED,
                                               ALU.is_gt, ALU.mult))
                        step(dve.tensor_tensor(shift[:, which, :, j], shift[:, which, :, j], tab_bc[:, which, 1, 0:SLOTS], ALU.subtract))
                    order.steps = n[0]

                @block.tensor
                def _(pe):
                    pe.wait_ge(cnt_ready.h, cnt_ready.at(1))
                    pe.matmul(acc[:, 0:NK], lower[:, :], cnt[:, :], start=True, stop=True)
                    pe.matmul(acc[:, BANK:BANK + NK], ones[:, 0:P], cnt[:, :], start=True, stop=True).then_inc(sums.h, 1)

                @block.sync
                def _(sp):
                    sp.wait_ge(tab_ready.h, tab_ready.at(1))
                    sp.dma_start(tab_i_dram[which].rearrange("f (j p) -> p f j", p=P), tab_i[:, :, :]).then_inc(tabs_out.h, 16)
                    sp.dma_start(tab_f_dram[which].rearrange("f (j p) -> p f j", p=P), tab_f[:, :, :]).then_inc(tabs_out.h, 16)
                    sp.wait_ge(tabs_out.h, tabs_out.at(32))
                    sp.dma_start(tab_row[:, which, :, :], tab_i_dram[which].rearrange("(a f) s -> a f s", a=1)).then_inc(tabs_in.h, 16)
                    sp.dma_start(tab_bc[:, which, :, :], tab_f_dram[which].partition_broadcast(P)).then_inc(tabs_in.h, 16)
                    sp.wait_ge(tabs_in.h, tabs_in.at(32))
            vec.passed(order.steps)
            for s, k in ((cnt_ready, 1), (sums, 1), (tab_ready, 1), (tabs_out, 32), (tabs_in, 32)):
                s.passed(k)

        order(0)
        order(1)

        LB = 4
        with nc.Block() as block:
            @block.vector
            def _(dve):
                dve.tensor_scalar(buck_i[:, :], lo_i[:, :], P - 1, None, ALU.bitwise_and).then_inc(vec.h, 1)
                dve.wait_ge(vec.h, vec.at(1))
                dve.tensor_copy(lo_f[:, :], buck_i[:, :]).then_inc(vec.h, 1)
                dve.wait_ge(vec.h, vec.at(2))
                with dve.Fori(0, EC // LB) as it:
                    for q in range(LB):
                        dve.wait_ge(lo_used.h, it * LB + q + lo_used.at(1))
                        dve.tensor_scalar(hot_lo[:, q, :], iota_b[:, :], lo_f[:, bass.ds(it * LB + q, 1)], None,
                                          ALU.is_equal).then_inc(lo_hot.h, 1)
                dve.wait_ge(sums.h, sums.at(1))
                def step(ins, k):
                    ins.then_inc(vec.h, 1)
                    dve.wait_ge(vec.h, vec.at(k))
                cn = acc[:, 0:NB]
                step(dve.tensor_scalar(deg[:, 0, :], cn, 1.0, None, ALU.add), 3)
                step(dve.tensor_scalar(deg[:, 2, :], cn, 1.0, None, ALU.max), 4)
                step(dve.reciprocal(deg[:, 1, :], deg[:, 2, :]), 5)
                step(dve.tensor_scalar(deg[:, 2, :], cn, 0.0, None, ALU.is_gt), 6)
                dve.wait_ge(rooted.h, rooted.at(1))
                step(dve.reciprocal(deg[:, 0, :], deg_root[:, :]), 7)

            @block.tensor
            def _(pe):
                for q in range(LB):
                    pe.sem_inc(lo_used.h, 1)
                pe.matmul(acc[:, 0:BANK], zeros[0:1, 0:P], zeros[0:1, :], start=True, stop=False)
                with pe.Fori(0, EC // LB) as it:
                    for q in range(LB):
                        pe.wait_ge(lo_hot.h, it * LB + q + lo_hot.at(1))
                        pe.matmul(acc[:, 0:NB], hot_lo[:, q, :], hot[:, 0:NB, bass.ds(it * LB + q, 1)].rearrange("p b c -> p (b c)"),
                                  start=False, stop=False).then_inc(lo_used.h, 1)
                pe.matmul(acc[:, 0:BANK], zeros[0:1, 0:P], zeros[0:1, :], start=False, stop=True).then_inc(sums.h, 1)

            @block.scalar
            def _(act):
                act.wait_ge(vec.h, vec.at(3))
                act.activation(deg_root[:, :], deg[:, 0, :], ACT.Sqrt).then_inc(rooted.h, 1)

            @block.sync
            def _(sp):
                sp.wait_ge(vec.h, vec.at(7))
                sp.dma_start(deg_dram.rearrange("f (b p) -> p f b", p=P), deg[:, :, :]).then_inc(tabs_out.h, 16)
                sp.wait_ge(tabs_out.h, tabs_out.at(16))
                sp.dma_start(node_bc[:, :, :], deg_dram.partition_broadcast(P)).then_inc(tabs_in.h, 16)
                sp.wait_ge(tabs_in.h, tabs_in.at(16))
        vec.passed(7)
        sums.passed(1)
        rooted.passed(1)
        tabs_out.passed(16)
        tabs_in.passed(16)
        lo_used.passed(EC + LB)
        lo_hot.passed(EC)

        row_in = [signal(f"row_in{q}") for q in range(BUF)]
        staged = signal("staged")
        scattered = [signal(f"scattered{q}") for q in range(BUF)]
        GROUPS = EC // KC
        ROUNDS = GROUPS // BUF
        orders = ((0, rows_by_src), (1, rows_by_dst))
        with nc.Block() as block:
            def rounds(eng, body):
                body(0, True, False)
                with eng.Fori(1, ROUNDS - 1) as it:
                    body(it, False, False)
                body(ROUNDS - 1, False, True)

            @block.sync
            def _(sp):
                def body(it, fresh, ends_here):
                    for q in range(BUF):
                        c = (it * BUF + q) * KC
                        if not fresh:
                            sp.wait_ge(scattered[q].h, scattered[q].at(0) + it * (16 * KC * 2))
                        if ends_here and q == BUF - 1:
                            sp.dma_start(srow[:, q, 0:KC - 1, 0:D],
                                         ea[c * P:(c + KC - 1) * P, :].rearrange("(c p) f -> p c f", p=P)).then_inc(row_in[q].h, 16)
                            sp.dma_start(srow[0:ELAST, q, KC - 1, 0:D], ea[(EC - 1) * P:E, :]).then_inc(row_in[q].h, 16)
                        else:
                            sp.dma_start(srow[:, q, :, 0:D],
                                         ea[bass.ds(c * P, KC * P), :].rearrange("(c p) f -> p c f", p=P)).then_inc(row_in[q].h, 16)
                rounds(sp, body)
                for q in range(BUF):
                    sp.wait_ge(scattered[q].h, scattered[q].at(ROUNDS * 16 * KC * 2))

            @block.vector
            def _(dve):
                def body(it, fresh, ends_here):
                    for q in range(BUF):
                        c = (it * BUF + q) * KC
                        if not fresh:
                            dve.wait_ge(scattered[q].h, scattered[q].at(0) + it * (16 * KC * 2))
                        dve.tensor_copy(srow[:, q, :, D:RW].bitcast(I32), pair_i[:, bass.ds(c, KC), :])
                        dve.tensor_copy(posq[:, :, q, :], pos_i[:, :, bass.ds(c, KC)]).then_inc(staged.h, 1)
                rounds(dve, body)

            @block.gpsimd
            def _(pool):
                def body(it, fresh, ends_here):
                    for q in range(BUF):
                        pool.wait_ge(staged.h, staged.at(q + 1) + it * BUF)
                        pool.wait_ge(row_in[q].h, row_in[q].at(16 + 16 * (ends_here and q == BUF - 1)) + it * 16)
                        pool.sem_inc(cleared.h, 1)
                        for j in range(KC):
                            for k, rows_out in orders:
                                pool.indirect_dma_start(rows_out, bass.IndirectOffsetOnAxis(ap=posq[:, k, q, j:j + 1], axis=0),
                                                        srow[:, q, j, :], None).then_inc(scattered[q].h, 16)
                rounds(pool, body)
        staged.passed(GROUPS)
        for q in range(BUF):
            row_in[q].passed(16 * (ROUNDS + (q == BUF - 1)))
            scattered[q].passed(ROUNDS * 16 * KC * 2)

        sort_scope.close()

        hid_t = sb("hid_t", [P, NP])
        h_t = sb("h_t", [P, NP])
        n_nm = sb("n_nm", [P, NB, D])
        rows = sb("rows", [P, BUF, G, RW])
        relq = sb("relq", [P, BUF, G])
        onehot = sb("onehot", [P, BUF * G, P])
        idxq = sb("idxq", [P, BUF, G], I32)
        got = sb("got", [P, BUF * G, D])
        got_z = sb("got_z", [P, BUF * G, H2])
        turned = sb("turned", [P, 2, 2 * P])
        msg = sb("msg", [P, 2, D])
        relued = sb("relued", [P, 2, D])

        slot_in = [signal(f"slot_in{q}") for q in range(BUF)]
        hot_ready = signal("hot_ready")
        hot_used = signal("hot_used")
        rel_ready = signal("rel_ready")
        evac = signal("evac")
        LOOPS = SLOTS // BUF

        def open_banks(pe, m=P):
            for k in range(BANKS):
                pe.matmul(acc[0:m, BANK * k:BANK * k + BANK], zeros[0:1, 0:m], zeros[0:1, :], start=True, stop=False)

        def close_banks(pe, m=P):
            for k in range(BANKS):
                last = pe.matmul(acc[0:m, BANK * k:BANK * k + BANK], zeros[0:1, 0:m], zeros[0:1, :], start=False, stop=True)
            return last

        def column(eng, which, slot):
            return eng.value_load(tab_row[0:1, which, 1, bass.ds(slot, 1)], min_val=0, max_val=NP - P)

        def first_row(eng, which, slot):
            return eng.value_load(tab_row[0:1, which, 0, bass.ds(slot, 1)], min_val=0, max_val=E - SLOT)

        def sum_edges(which, rows_in, keep):
            with nc.Block() as block:
                @block.sync
                def _(sp):
                    def body(it, fresh):
                        for q in range(BUF):
                            row = first_row(sp, which, it * BUF + q)
                            if not fresh:
                                sp.wait_ge(hot_used.h, hot_used.at(q + 1 - BUF) + it * BUF)
                            sp.dma_start(rows[:, q, :, :], rows_in[bass.ds(row, SLOT), :].rearrange("(p j) w -> p j w", j=G))\
                              .then_inc(slot_in[q].h, 16)
                    body(0, True)
                    with sp.Fori(1, LOOPS) as it:
                        body(it, False)

                @block.vector
                def _(dve):
                    def body(it, fresh):
                        for q in range(BUF):
                            slot = it * BUF + q
                            dve.wait_ge(slot_in[q].h, slot_in[q].at(16) + it * 16)
                            if not fresh:
                                dve.wait_ge(hot_used.h, hot_used.at(q + 1 - BUF) + it * BUF)
                            key = rows[:, q, :, D + which:D + which + 1].bitcast(I32).rearrange("p j a -> p (j a)")
                            dve.tensor_tensor(relq[:, q, :], key, shift[:, which, bass.ds(slot, 1), :].rearrange("p s j -> p (s j)"), ALU.add)\
                               .then_inc(rel_ready.h, 1)
                            if keep:
                                dve.tensor_tensor(rel[:, bass.ds(slot * G, G)], key, shift[:, which, bass.ds(slot, 1), :].rearrange("p s j -> p (s j)"), ALU.add)
                                dve.tensor_copy(src_i[:, bass.ds(slot * G, G)], rows[:, q, :, D:D + 1].bitcast(I32).rearrange("p j a -> p (j a)"))
                            dve.wait_ge(rel_ready.h, rel_ready.at(q + 1) + it * BUF)
                            for j in range(G):
                                ins = dve.tensor_scalar(onehot[:, q * G + j, :], iota[:, :], relq[:, q, j:j + 1], None, ALU.is_equal)
                            ins.then_inc(hot_ready.h, 1)
                    body(0, True)
                    with dve.Fori(1, LOOPS) as it:
                        body(it, False)
                    dve.wait_ge(evac.h, evac.at(1))
                    if which == 1:
                        for k, c, w in banks():
                            dve.tensor_copy(agg_dst[:, c:c + w], acc[:, c:c + w])
                    else:
                        for k, c, w in banks():
                            dve.tensor_tensor(agg_sum[:, c:c + w], acc[:, c:c + w], agg_dst[:, c:c + w], ALU.add)

                @block.tensor
                def _(pe):
                    open_banks(pe)

                    def body(it):
                        for q in range(BUF):
                            col = column(pe, which, it * BUF + q)
                            pe.wait_ge(hot_ready.h, hot_ready.at(q + 1) + it * BUF)
                            pe.wait_ge(slot_in[q].h, slot_in[q].at(16) + it * 16)
                            for j in range(G):
                                last = pe.matmul(acc[:, bass.ds(col, P)], rows[:, q, j, 0:D], onehot[:, q * G + j, :],
                                                 start=False, stop=False)
                            last.then_inc(hot_used.h, 1)
                    with pe.Fori(0, LOOPS) as it:
                        body(it)
                    close_banks(pe).then_inc(evac.h, 1)
            for q in range(BUF):
                slot_in[q].passed(16 * LOOPS)
            for s in (hot_ready, hot_used, rel_ready):
                s.passed(SLOTS)
            evac.passed(1)

        sum_edges(1, rows_by_dst, True)
        sum_edges(0, rows_by_src, False)

        mean_done = signal("mean_done")
        turned_out = signal("turned_out")
        relu_done = signal("relu_done")
        first_mm = signal("first_mm")
        hidden = signal("hidden")
        second_mm = signal("second_mm")
        added = signal("added")

        def norm():
            with nc.Block() as block:
                @block.vector
                def _(dve):
                    for b in range(NB):
                        ins = dve.bn_stats(stats[:, b, :], x_nm[:, b, :])
                    ins.then_inc(vec.h, 1)
                    dve.wait_ge(vec.h, vec.at(1))
                    for b in range(NB):
                        ins = dve.bn_aggr(mv[:, b, :], stats[:, b, :])
                    ins.then_inc(vec.h, 1)
                    dve.wait_ge(vec.h, vec.at(2))
                    dve.tensor_scalar(rstd[:, :], mv[:, :, 1:2].rearrange("p b a -> p (b a)"), EPS, None, ALU.add).then_inc(vec.h, 1)
                    dve.wait_ge(rooted.h, rooted.at(1))
                    dve.reciprocal(rstd[:, :], std[:, :]).then_inc(vec.h, 1)
                    dve.wait_ge(vec.h, vec.at(4))
                    for b in range(NB):
                        ins = dve.tensor_scalar(n_nm[:, b, :], x_nm[:, b, :], mv[:, b, 0:1], rstd[:, b:b + 1], ALU.subtract, ALU.mult)
                        if b % 4 == 3 or b == NB - 1:
                            ins.then_inc(mean_done.h, 1)


                @block.tensor
                def _(pe):
                    for k, c, w in banks():
                        pe.wait_ge(mean_done.h, mean_done.at(k + 1))
                        for b in range(w // P):
                            last = pe.transpose(acc[:, c + b * P:c + b * P + P], n_nm[:, 4 * k + b, :], ident[:, :])
                        last.then_inc(turned_out.h, 1)

                @block.scalar
                def _(act):
                    act.wait_ge(vec.h, vec.at(3))
                    act.activation(std[:, :], rstd[:, :], ACT.Sqrt).then_inc(rooted.h, 1)
                    for k, c, w in banks():
                        act.wait_ge(turned_out.h, turned_out.at(k + 1))
                        act.activation(h_t[:, c:c + w], acc[:, c:c + w], ACT.Relu)
            vec.passed(4)
            rooted.passed(1)
            mean_done.passed(BANKS)
            turned_out.passed(BANKS)

        def dense(parts, bias, w2, row, rows_in, to_x=True):
            with nc.Block() as block:
                @block.tensor
                def _(pe):
                    for k, c, w in banks():
                        if k >= 2:
                            pe.wait_ge(hidden.h, hidden.at(k - 1))
                        for i, (wt, t) in enumerate(parts):
                            last = pe.matmul(acc[:, BANK * (k % 2):BANK * (k % 2) + w], wt, t[:, c:c + w],
                                             start=i == 0, stop=i == len(parts) - 1)
                        last.then_inc(first_mm.h, 1)
                        pe.wait_ge(hidden.h, hidden.at(k + 1))
                        if k >= 2:
                            pe.wait_ge(added.h, added.at(k - 1))
                        o = BANK * (2 + k % 2)
                        pe.matmul(acc[:, o:o + w], ones[0:1, 0:P], b_rows[0:1, row:row + 1, :].broadcast_to([1, w // P, D]),
                                  start=True, stop=False)
                        for b in range(w // P):
                            last = pe.matmul(acc[:, o + b * P:o + b * P + P], hid_t[:, c + b * P:c + b * P + P], w2,
                                             start=False, stop=b == w // P - 1)
                        last.then_inc(second_mm.h, 1)

                @block.scalar
                def _(act):
                    for k, c, w in banks():
                        act.wait_ge(first_mm.h, first_mm.at(k + 1))
                        act.activation(hid_t[:, c:c + w], acc[:, BANK * (k % 2):BANK * (k % 2) + w], ACT.Relu, bias=bias)\
                           .then_inc(hidden.h, 1)

                @block.vector
                def _(dve):
                    for k, c, w in banks():
                        dve.wait_ge(second_mm.h, second_mm.at(k + 1))
                        o = BANK * (2 + k % 2)
                        xb = x_nm[:, 4 * k:4 * k + w // P, :].rearrange("p b f -> p (b f)")
                        dve.tensor_tensor(xb, xb, acc[:, o:o + w], ALU.add).then_inc(added.h, 1)
            for s in (first_mm, hidden, second_mm, added):
                s.passed(BANKS)

        norm()
        dense([(w_l0[:, 0, :], h_t), (w_l0[:, 1, :], agg_sum)], b_cols[:, 0:1], w2_l0[:, :], 0, None)
        norm()
        dense([(w_l1[:, 0, :], h_t), (w_l1[:, 1, :], agg_dst)], b_cols[:, 1:2], w2_l1[:, :], 1, None)
        norm()

        table_out = signal("table_out")
        gathered = [signal(f"gathered{q}") for q in range(BUF)]
        idx_ready = signal("idx_ready")
        z_nm = n_nm[:, :, 0:H2]

        def store_table(sp, table, tile):
            sp.dma_start(table.rearrange("(b p) f -> p b f", p=P), tile).then_inc(table_out.h, 16)
            sp.wait_ge(table_out.h, table_out.at(16))

        with nc.Block() as block:
            @block.tensor
            def _(pe):
                for b in range(NB):
                    last = pe.matmul(acc[:, b * H2:b * H2 + H2], h_t[:, b * P:b * P + P], w1_g[:, :], start=True, stop=True)
                last.then_inc(first_mm.h, 1)

            @block.vector
            def _(dve):
                dve.wait_ge(first_mm.h, first_mm.at(1))
                dve.tensor_tensor(z_nm, acc[:, 0:NB * H2].rearrange("p (b f) -> p b f", f=H2),
                                  deg[:, 0, :].rearrange("p (b a) -> p b a", a=1).broadcast_to([P, NB, H2]), ALU.mult).then_inc(added.h, 1)

            @block.sync
            def _(sp):
                sp.wait_ge(added.h, added.at(1))
                store_table(sp, z_table[0], z_nm)
        first_mm.passed(1)
        added.passed(1)
        table_out.passed(16)

        def gather_z(table):
            with nc.Block() as block:
                @block.vector
                def _(dve):
                    def body(it, fresh):
                        for q in range(BUF):
                            slot = it * BUF + q
                            if not fresh:
                                dve.wait_ge(gathered[q].h, gathered[q].at(0) + it * (16 * G))
                            dve.tensor_copy(idxq[:, q, :], src_i[:, bass.ds(slot * G, G)]).then_inc(idx_ready.h, 1)
                            if not fresh:
                                dve.wait_ge(hot_used.h, hot_used.at(q + 1 - BUF) + it * BUF)
                            for j in range(G):
                                ins = dve.tensor_scalar(onehot[:, q * G + j, :], iota[:, :], rel[:, bass.ds(slot * G + j, 1)], None, ALU.is_equal)
                            ins.then_inc(hot_ready.h, 1)
                    body(0, True)
                    with dve.Fori(1, LOOPS) as it:
                        body(it, False)

                @block.gpsimd
                def _(pool):
                    def body(it, fresh):
                        for q in range(BUF):
                            pool.wait_ge(idx_ready.h, idx_ready.at(q + 1) + it * BUF)
                            if not fresh:
                                pool.wait_ge(hot_used.h, hot_used.at(q + 1 - BUF) + it * BUF)
                            pool.sem_inc(cleared.h, 1)
                            for j in range(G):
                                pool.indirect_dma_start(got_z[:, q * G + j, :], None, table,
                                                        bass.IndirectOffsetOnAxis(ap=idxq[:, q, j:j + 1], axis=0)).then_inc(gathered[q].h, 16)
                    body(0, True)
                    with pool.Fori(1, LOOPS) as it:
                        body(it, False)

                @block.tensor
                def _(pe):
                    open_banks(pe, H2)
                    for b in range(NB):
                        pe.matmul(acc[0:H2, b * P:b * P + P], z_nm[:, b, :], ident[:, :], start=False, stop=False)
                    with pe.Fori(0, LOOPS) as it:
                        for q in range(BUF):
                            col = column(pe, 1, it * BUF + q)
                            pe.wait_ge(hot_ready.h, hot_ready.at(q + 1) + it * BUF)
                            pe.wait_ge(gathered[q].h, gathered[q].at(16 * G) + it * (16 * G))
                            for j in range(G):
                                last = pe.matmul(acc[0:H2, bass.ds(col, P)], got_z[:, q * G + j, :], onehot[:, q * G + j, :],
                                                 start=False, stop=False)
                            last.then_inc(hot_used.h, 1)
                    close_banks(pe, H2)
            for s in (idx_ready, hot_ready, hot_used):
                s.passed(SLOTS)
            for q in range(BUF):
                gathered[q].passed(16 * G * LOOPS)

        gather_z(z_table[0])

        with nc.Block() as block:
            @block.vector
            def _(dve):
                for k, c, w in banks():
                    dve.tensor_tensor(hid_t[0:H2, c:c + w], acc[0:H2, c:c + w], node_bc[0:H2, 0, c:c + w], ALU.mult).then_inc(first_mm.h, 1)
                for k, c, w in banks():
                    dve.wait_ge(hidden.h, hidden.at(k + 1))
                    dve.tensor_tensor(agg_sum[0:H2, c:c + w], agg_sum[0:H2, c:c + w], node_bc[0:H2, 0, c:c + w], ALU.mult).then_inc(added.h, 1)
                for h in range(2):
                    dve.wait_ge(turned_out.h, turned_out.at(h + 1))
                    b0, b1 = (0, 16) if h == 0 else (16, NB)
                    dve.tensor_copy(z_nm[:, b0:b1, :], acc[:, b0 * H2:b1 * H2].rearrange("p (b f) -> p b f", f=H2)).then_inc(second_mm.h, 1)

            @block.scalar
            def _(act):
                for k, c, w in banks():
                    act.wait_ge(first_mm.h, first_mm.at(k + 1))
                    act.activation(agg_sum[0:H2, c:c + w], hid_t[0:H2, c:c + w], ACT.Relu, bias=b_cols[0:H2, 2:3]).then_inc(hidden.h, 1)

            @block.tensor
            def _(pe):
                pe.wait_ge(added.h, added.at(BANKS))
                for b in range(NB):
                    last = pe.transpose(acc[:, b * H2:b * H2 + H2], agg_sum[0:H2, b * P:b * P + P], ident[0:H2, 0:H2])
                    if b in (15, NB - 1):
                        last.then_inc(turned_out.h, 1)

            @block.sync
            def _(sp):
                sp.wait_ge(second_mm.h, second_mm.at(2))
                store_table(sp, z_table[1], z_nm)
        for s, k in ((first_mm, BANKS), (hidden, BANKS), (added, BANKS), (turned_out, 2), (second_mm, 2), (table_out, 16)):
            s.passed(k)

        gather_z(z_table[1])

        with nc.Block() as block:
            @block.vector
            def _(dve):
                for k, c, w in banks():
                    dve.tensor_tensor(hid_t[0:H2, c:c + w], acc[0:H2, c:c + w], node_bc[0:H2, 0, c:c + w], ALU.mult).then_inc(hidden.h, 1)
                for k, c, w in banks():
                    dve.wait_ge(second_mm.h, second_mm.at(k + 1))
                    xb = x_nm[:, 4 * k:4 * k + w // P, :].rearrange("p b f -> p (b f)")
                    dve.tensor_tensor(xb, xb, acc[:, c:c + w], ALU.add)

            @block.tensor
            def _(pe):
                pe.wait_ge(hidden.h, hidden.at(BANKS))
                for k, c, w in banks():
                    pe.matmul(acc[:, c:c + w], ones[0:1, 0:P], b_rows[0:1, 2:3, :].broadcast_to([1, w // P, D]), start=True, stop=False)
                    for b in range(w // P):
                        last = pe.matmul(acc[:, c + b * P:c + b * P + P], hid_t[0:H2, c + b * P:c + b * P + P], w2_g[:, :],
                                         start=False, stop=b == w // P - 1)
                    last.then_inc(second_mm.h, 1)
        hidden.passed(BANKS)
        second_mm.passed(BANKS)
        norm()

        p_nm = n_nm
        q_nm = hid_t[:, :].rearrange("p (b f) -> p b f", f=D)
        with nc.Block() as block:
            @block.tensor
            def _(pe):
                for k, c, w in banks():
                    for b in range(w // P):
                        last = pe.matmul(acc[:, c + b * P:c + b * P + P], h_t[:, c + b * P:c + b * P + P], w_msg[:, 0, :], start=True, stop=True)
                    last.then_inc(first_mm.h, 1)
                for k, c, w in banks():
                    pe.wait_ge(added.h, added.at(k + 1))
                    pe.matmul(acc[:, c:c + w], ones[0:1, 0:P], b_rows[0:1, 4:5, :].broadcast_to([1, w // P, D]), start=True, stop=False)
                    for b in range(w // P):
                        last = pe.matmul(acc[:, c + b * P:c + b * P + P], h_t[:, c + b * P:c + b * P + P], w_msg[:, 1, :],
                                         start=False, stop=b == w // P - 1)
                    last.then_inc(second_mm.h, 1)

            @block.vector
            def _(dve):
                for k, c, w in banks():
                    dve.wait_ge(first_mm.h, first_mm.at(k + 1))
                    dve.tensor_copy(p_nm[:, :, :].rearrange("p b f -> p (b f)")[:, c:c + w], acc[:, c:c + w]).then_inc(added.h, 1)

            @block.scalar
            def _(act):
                for k, c, w in banks():
                    act.wait_ge(second_mm.h, second_mm.at(k + 1))
                    act.activation(hid_t[:, c:c + w], acc[:, c:c + w], ACT.Copy)

            @block.sync
            def _(sp):
                sp.wait_ge(added.h, added.at(BANKS))
                store_table(sp, p_table, p_nm[:, :, :])
        for s, k in ((first_mm, BANKS), (added, BANKS), (second_mm, BANKS), (table_out, 16)):
            s.passed(k)

        turn = signal("turn")
        turn_out = signal("turn_out")
        made = signal("made")
        plus = signal("plus")
        cut = signal("cut")
        collected = signal("collected")
        summed = signal("summed")
        CH = BUF * G
        TOTAL = SLOTS * G
        with nc.Block() as block:
            def chunk(i):
                return (i % CH) // G, i % G

            def body_rounds(eng, step):
                def body(it, n0):
                    for i in range(CH):
                        step(it, i, n0)
                body(0, 0)
                with eng.Fori(1, LOOPS) as it:
                    body(it, None)

            @block.sync
            def _(sp):
                def body(it, fresh):
                    for q in range(BUF):
                        row = first_row(sp, 1, it * BUF + q)
                        if not fresh:
                            sp.wait_ge(turn.h, turn.at((q + 1) * G - CH) + it * CH)
                        sp.dma_start(rows[:, q, :, 0:D], rows_by_dst[bass.ds(row, SLOT), 0:D].rearrange("(p j) w -> p j w", j=G))\
                          .then_inc(slot_in[q].h, 16)
                body(0, True)
                with sp.Fori(1, LOOPS) as it:
                    body(it, False)

            @block.gpsimd
            def _(pool):
                def body(it, fresh):
                    for q in range(BUF):
                        pool.wait_ge(idx_ready.h, idx_ready.at(q + 1) + it * BUF)
                        if not fresh:
                            pool.wait_ge(plus.h, plus.at((q + 1) * G - CH) + it * CH)
                        pool.sem_inc(cleared.h, 1)
                        for j in range(G):
                            pool.indirect_dma_start(got[:, q * G + j, :], None, p_table,
                                                    bass.IndirectOffsetOnAxis(ap=idxq[:, q, j:j + 1], axis=0)).then_inc(gathered[q].h, 16)
                body(0, True)
                with pool.Fori(1, LOOPS) as it:
                    body(it, False)

            @block.vector
            def _(dve):
                def add(it, i):
                    q, j = chunk(i)
                    dve.wait_ge(made.h, made.at(i + 1) + it * CH)
                    dve.wait_ge(gathered[q].h, gathered[q].at(16 * G) + it * (16 * G))
                    if not (isinstance(it, int) and it == 0 and i < 2):
                        dve.wait_ge(cut.h, cut.at(i - 1) + it * CH)
                    dve.tensor_tensor(msg[:, i % 2, :], acc[:, (2 + i % 2) * BANK:(2 + i % 2) * BANK + P], got[:, i, :], ALU.add).then_inc(plus.h, 1)

                def collect(it, q):
                    col = column(dve, 1, it * BUF + q)
                    dve.wait_ge(summed.h, summed.at((q + 1) * G) + it * CH)
                    if not (isinstance(it, int) and it == 0 and q == 0):
                        dve.wait_ge(collected.h, collected.at(q) + it * BUF)
                    o = (4 + q % 2) * BANK
                    dve.tensor_tensor(agg_sum[:, bass.ds(col, P)], agg_sum[:, bass.ds(col, P)], acc[:, o:o + P], ALU.add)\
                       .then_inc(collected.h, 1)

                dve.memset(agg_sum[:, :], 0.0).then_inc(vec.h, 1)
                dve.wait_ge(vec.h, vec.at(1))

                def body(it, fresh):
                    for q in range(BUF):
                        slot = it * BUF + q
                        if not fresh:
                            dve.wait_ge(gathered[q].h, gathered[q].at(0) + it * (16 * G))
                        dve.tensor_copy(idxq[:, q, :], src_i[:, bass.ds(slot * G, G)]).then_inc(idx_ready.h, 1)
                        if q >= BEHIND:
                            collect(it, q - BEHIND)
                        elif not fresh:
                            collect(it - 1, q - BEHIND + BUF)
                        for j in range(G):
                            if not fresh:
                                dve.wait_ge(summed.h, summed.at(q * G + j + 1 - CH) + it * CH)
                            dve.tensor_scalar(onehot[:, q * G + j, :], iota[:, :], rel[:, bass.ds(slot * G + j, 1)], None, ALU.is_equal)\
                               .then_inc(hot_ready.h, 1)
                            i = q * G + j - HEAD
                            if i >= 0:
                                add(it, i)
                            elif not fresh:
                                add(it - 1, i + CH)
                HEAD, BEHIND = 2 * G, 3
                body(0, True)
                with dve.Fori(1, LOOPS) as it:
                    body(it, False)
                for q in range(BUF, BUF + BEHIND):
                    collect(LOOPS - 1, q - BEHIND)
                    for i in range(q * G - HEAD, min((q + 1) * G - HEAD, CH)):
                        add(LOOPS - 1, i)

            @block.scalar
            def _(act):
                def out_of_psum(it, i):
                    act.wait_ge(turn.h, turn.at(i + 1) + it * CH)
                    if not (isinstance(it, int) and it == 0 and i < 2):
                        act.wait_ge(made.h, made.at(i - 1) + it * CH)
                    act.activation(turned[:, i % 2, :], acc[:, i % 2 * BANK:i % 2 * BANK + 2 * P], ACT.Copy).then_inc(turn_out.h, 1)

                def relu(it, i):
                    act.wait_ge(plus.h, plus.at(i + 1) + it * CH)
                    if not (isinstance(it, int) and it == 0 and i < 2):
                        act.wait_ge(summed.h, summed.at(i - 1) + it * CH)
                    act.activation(relued[:, i % 2, :], msg[:, i % 2, :], ACT.Relu).then_inc(cut.h, 1)

                def body(it, fresh):
                    for i in range(CH):
                        out_of_psum(it, i)
                        if i >= 1:
                            relu(it, i - 1)
                        elif not fresh:
                            relu(it - 1, CH - 1)
                body(0, True)
                with act.Fori(1, LOOPS) as it:
                    body(it, False)
                relu(LOOPS - 1, CH - 1)

            @block.tensor
            def _(pe):
                def turn_chunk(it, i):
                    q, j = chunk(i)
                    pe.wait_ge(hot_ready.h, hot_ready.at(i + 1) + it * CH)
                    if j == 0:
                        pe.wait_ge(slot_in[q].h, slot_in[q].at(16) + it * 16)
                    if not (isinstance(it, int) and it == 0 and i < 2):
                        pe.wait_ge(turn_out.h, turn_out.at(i - 1) + it * CH)
                    o = i % 2 * BANK
                    pe.transpose(acc[:, o:o + P], rows[:, q, j, 0:D], ident[:, :])
                    pe.transpose(acc[:, o + P:o + 2 * P], onehot[:, i, :], ident[:, :]).then_inc(turn.h, 1)

                def product(it, i, col):
                    pe.wait_ge(turn_out.h, turn_out.at(i + 1) + it * CH)
                    if not (isinstance(it, int) and it == 0 and i < 2):
                        pe.wait_ge(plus.h, plus.at(i - 1) + it * CH)
                    o = (2 + i % 2) * BANK
                    pe.matmul(acc[:, o:o + P], turned[:, i % 2, 0:P], w_msg[:, 2, :], start=True, stop=False)
                    pe.matmul(acc[:, o:o + P], turned[:, i % 2, P:2 * P], hid_t[:, bass.ds(col, P)], start=False, stop=True)\
                      .then_inc(made.h, 1)

                def total(it, i):
                    q, j = chunk(i)
                    pe.wait_ge(cut.h, cut.at(i + 1) + it * CH)
                    if j == 0 and not (isinstance(it, int) and it == 0 and q < 2):
                        pe.wait_ge(collected.h, collected.at(q - 1) + it * BUF)
                    o = (4 + q % 2) * BANK
                    pe.matmul(acc[:, o:o + P], relued[:, i % 2, :], onehot[:, i, :], start=j == 0, stop=j == G - 1)\
                      .then_inc(summed.h, 1)

                def body(it, fresh):
                    if not fresh:
                        product_col = column(pe, 1, it * BUF - 1)
                    for i in range(CH):
                        turn_chunk(it, i)
                        if i >= 1:
                            product(it, i - 1, product_col)
                        elif not fresh:
                            product(it - 1, CH - 1, product_col)
                        if i % G == 0:
                            product_col = column(pe, 1, it * BUF + i // G)
                        if i >= 3:
                            total(it, i - 3)
                        elif not fresh:
                            total(it - 1, CH + i - 3)
                body(0, True)
                with pe.Fori(1, LOOPS) as it:
                    body(it, False)
                product(LOOPS - 1, CH - 1, column(pe, 1, SLOTS - 1))
                for i in range(CH - 3, CH):
                    total(LOOPS - 1, i)
        for s in (turn, turn_out, made, plus, cut, summed, hot_ready):
            s.passed(TOTAL)
        idx_ready.passed(SLOTS)
        collected.passed(SLOTS)
        vec.passed(1)
        for q in range(BUF):
            gathered[q].passed(16 * G * LOOPS)
            slot_in[q].passed(16 * LOOPS)

        with nc.Block() as block:
            @block.vector
            def _(dve):
                for k, c, w in banks():
                    dve.tensor_tensor(hid_t[:, c:c + w], agg_sum[:, c:c + w], node_bc[:, 1, c:c + w], ALU.mult).then_inc(first_mm.h, 1)

            @block.tensor
            def _(pe):
                pe.wait_ge(first_mm.h, first_mm.at(BANKS))
                for k, c, w in banks():
                    pe.matmul(acc[:, c:c + w], w2_msg[:, :], hid_t[:, c:c + w], start=True, stop=False)
                    pe.matmul(acc[:, c:c + w], b_rows[0:1, 5, :], node_bc[0:1, 2, c:c + w], start=False, stop=True).then_inc(second_mm.h, 1)

            @block.scalar
            def _(act):
                for k, c, w in banks():
                    act.wait_ge(second_mm.h, second_mm.at(k + 1))
                    act.activation(agg_dst[:, c:c + w], acc[:, c:c + w], ACT.Copy)
        first_mm.passed(BANKS)
        second_mm.passed(BANKS)
        dense([(w_upd[:, 0, :], h_t), (w_upd[:, 1, :], agg_dst)], b_cols[:, 3:4], w2_upd[:, :], 3, None)

        out_done = signal("out_done")
        with nc.Block() as block:
            @block.sync
            def _(sp):
                sp.dma_start(out[0:(NB - 1) * P, :].rearrange("(b p) f -> p b f", p=P), x_nm[:, 0:NB - 1, :]).then_inc(out_done.h, 16)
                sp.dma_start(out[(NB - 1) * P:N, :], x_nm[0:NLAST, NB - 1, :]).then_inc(out_done.h, 16)
                sp.wait_ge(out_done.h, out_done.at(32))


_INS = ["x", "src", "dst", "edge_attr_128"] + [f"L0_gnn_{n}" for n in ("W1", "b1", "W2", "b2")] \
    + [f"L1_gnn_{n}" for n in ("W1", "b1", "W2", "b2")] + [f"L2_gnn_{n}" for n in ("W1", "b1", "W2", "b2")] \
    + [f"L3_gnn_{a}_{n}" for a in ("msg", "upd") for n in ("w1", "b1", "w2", "b2")]


def kernel(**inputs):
    import numpy as _np
    import concourse.bacc as _bacc
    from concourse import mybir as _mybir
    from concourse.bass_utils import run_bass_kernel_spmd as _run

    nc = _bacc.Bacc("TRN2", target_bir_lowering=False, num_devices=1)
    arrays, args = {}, []
    for name in _INS:
        a = _np.ascontiguousarray(inputs[name])
        arrays[f"in_{name}"] = a
        args.append(nc.dram_tensor(f"in_{name}", a.shape, _mybir.dt.from_np(a.dtype), kind="ExternalInput").ap())
    out = nc.dram_tensor("out", (N, D), F32, kind="ExternalOutput").ap()
    build(nc, *args[0:4], args[4:8], args[8:12], args[12:16], args[16:24], out)
    r = _run(nc, [arrays], core_ids=[0])
    return r.results[0]["out"]
```

```python
import numpy as np
import concourse.bass as bass
from concourse import mybir
from contextlib import ExitStack, contextmanager

F32 = mybir.dt.float32
I32 = mybir.dt.int32
BF16 = mybir.dt.bfloat16
F16 = mybir.dt.float16
U8 = mybir.dt.uint8
BYTES = {F32: 4, I32: 4, BF16: 2, F16: 2, U8: 1}
ALU = mybir.AluOpType
ACT = mybir.ActivationFunctionType
AX = mybir.AxisListType

P = 128
N, E, D, H2 = 3125, 53125, 128, 64
NB = -(-N // P)
NP = NB * P
NLAST = N - (NB - 1) * P
EC = -(-E // P)
EP = EC * P
ELAST = E - (EC - 1) * P
ET = -(-EC // P)
NK = NB + 1
G = 2
SLOT = G * P
SLOTS = (E + NB * (SLOT - 1)) // SLOT
BUF = 8
SLOTS = -(-SLOTS // BUF) * BUF
ST = -(-SLOTS // P)
RW = D + 2
BANK = 512
BANKS = -(-NP // BANK)
MB = 4
UB = 6
MASKED = 4096.0
EPS = 1e-5
KC = 4
W = 24
PAIRS = EC // 2
HW = NB * W
HBLOCKS = 16
WS = BANK // HBLOCKS
LIMIT = 254.0
FAST, GENERAL = 0, 1
ROWB = 4
HOTB = 4


class Signal:
    path = None

    def __init__(self, make):
        self.make, self.on_path, self.base = make, {}, {}

    @property
    def h(self):
        if Signal.path not in self.on_path:
            self.on_path[Signal.path] = self.make()
        return self.on_path[Signal.path]

    def at(self, n):
        return self.base.get(Signal.path, 0) + n

    def passed(self, n):
        self.base[Signal.path] = self.at(n)


@contextmanager
def path(which):
    Signal.path = which
    yield
    Signal.path = None


class Space:

    def __init__(self, flat, dt):
        self.flat, self.unit, self.used = flat, BYTES[dt], 0

    def again(self):
        self.used = 0

    def take(self, shape, dt=F32):
        size = -(-int(np.prod(shape[1:])) * BYTES[dt] // 4) * 4
        first, self.used = self.used, self.used + size
        assert self.used <= self.flat.shape[1] * self.unit
        ap = self.flat[0:shape[0], first // self.unit:self.used // self.unit]
        if BYTES[dt] * ap.shape[1] != size or dt not in (F32, U8) or BYTES[dt] != self.unit:
            ap = ap.bitcast(dt)
        ap = ap[:, 0:int(np.prod(shape[1:]))]
        names = "abc"[:len(shape) - 1]
        if len(names) > 1:
            ap = ap.rearrange(f"p ({' '.join(names)}) -> p {' '.join(names)}", **dict(zip(names, shape[1:])))
        return ap


def banks():
    return [(k, BANK * k, min(BANK, NP - BANK * k)) for k in range(BANKS)]


def build(nc, x, src, dst, ea, l0, l1, l2, l3, out):
    ctx = ExitStack()
    with ctx:
        nc_ctx = ctx.enter_context(nc.allow_non_contiguous_dma(reason="small tables and bias columns"))

        def sb(name, shape, dt=F32):
            return ctx.enter_context(nc.sbuf_tensor(name, shape, dt))

        made_signals = [0]

        def signal(name):
            def make():
                made_signals[0] += 1
                return ctx.enter_context(nc.semaphore(f"{name}_{made_signals[0]}"))
            return Signal(make)

        def on(register):
            def wrap(f):
                @register
                def _(eng):
                    if Signal.path is None:
                        f(eng)
                    else:
                        with eng.If(eng.value_load(flags[0:1, Signal.path:Signal.path + 1], min_val=0, max_val=1)):
                            f(eng)
            return wrap

        def dram(name, shape, dt=F32):
            return nc.dram_tensor(name, shape, dt, kind="Internal").ap()

        rows_by_src = dram("rows_by_src", (EP, RW))
        rows_by_dst = dram("rows_by_dst", (EP, RW))
        tab_i_dram = [dram(f"tab_i{k}", (2, ST * P), I32) for k in range(2)]
        tab_f_dram = [dram(f"tab_f{k}", (2, ST * P)) for k in range(2)]
        z_table = dram("z_table", (NP, H2))
        p_table = dram("p_table", (NP, D))
        q_table = dram("q_table", (NP, D))
        cnt_dram = dram("cnt_dram", (NP,))

        x_nm = sb("x_nm", [P, NB, D])
        h_t = sb("h_t", [P, NP])
        n_nm = sb("n_nm", [P, NB, D])
        n_flat = n_nm[:, :, :].rearrange("p b f -> p (b f)")
        hid_t = n_flat
        by_dst = sb("by_dst", [P, 2, NP])
        agg_dst, cnt_bc = by_dst[:, 0, :], by_dst[:, 1, :]
        agg_sum = sb("agg_sum", [P, NP])
        dinv_bc = sb("dinv_bc", [P, NP])
        dinv_nm = sb("dinv_nm", [P, NB])
        stats = sb("stats", [P, NB, 6])
        mv = sb("mv", [P, NB, 2])
        rstd = sb("rstd", [P, NB])
        std = sb("std", [P, NB])
        between = sb("between", [P, NB, NP], U8)
        flags = sb("flags", [1, 2], I32)

        iota_i = sb("iota_i", [P, P], I32)
        part_i = sb("part_i", [P, 1], I32)
        slot_i = sb("slot_i", [P, ST], I32)
        place_i = sb("place_i", [P, G], I32)
        iota = sb("iota", [P, P])
        iota_b = sb("iota_b", [P, P], BF16)
        iota_w = sb("iota_w", [P, HW], F16)
        part = sb("part", [P, 1])
        slot_id = sb("slot_id", [P, ST])
        place = sb("place", [P, G])
        ident = sb("ident", [P, P])
        lower = sb("lower", [P, P])
        ones = sb("ones", [P, EC])
        zeros = sb("zeros", [1, BANK])

        w_l0 = sb("w_l0", [P, 2, D])
        w_l1 = sb("w_l1", [P, 2, D])
        w2_l0 = sb("w2_l0", [P, D])
        w2_l1 = sb("w2_l1", [P, D])
        w1_g = sb("w1_g", [P, H2])
        w2_g = sb("w2_g", [H2, D])
        w_msg = sb("w_msg", [P, 3, D])
        w2_msg = sb("w2_msg", [P, D])
        w_upd = sb("w_upd", [P, 2, D])
        w2_upd = sb("w2_upd", [P, D])
        b_cols = sb("b_cols", [P, 4])
        b_rows = sb("b_rows", [1, 6, D])
        b1_row = sb("b1_row", [1, H2])

        tab_row = sb("tab_row", [1, 2, 2, ST * P], I32)
        tab_bc = sb("tab_bc", [P, 2, 2, ST * P])
        shift = sb("shift", [P, 2, SLOTS, G])

        win_f = sb("win_f", [1, PAIRS])
        win_i = sb("win_i", [1, PAIRS], I32)
        place_w = sb("place_w", [P, EC])
        src_g = sb("src_g", [P, EC], I32)

        grid_space = Space(dinv_bc[:, :], F32)
        keys = grid_space.take([P, 2, EC])
        pair_i = grid_space.take([P, EC, 2], I32)
        pos_i = grid_space.take([P, 2, EC], I32)
        posq = sb("posq", [P, ROWB, KC], I32)

        space = Space(between[:, :, :].rearrange("p b n -> p (b n)"), U8)
        idx_i = space.take([P, 2, ET * P], I32)
        idx_f = space.take([P, 2, ET * P])
        buck_i = space.take([P, EC], I32)
        lo_i = space.take([P, EC], I32)
        lo_f = space.take([P, EC])
        buck = space.take([P, EC])
        hot = space.take([P, NK, EC], BF16)
        ranks = space.take([P, EC])
        picked = space.take([P, EC])
        pos = space.take([P, EC])
        cnt = space.take([P, NK])
        tot = space.take([P, NK])
        first = space.take([P, NK])
        offs = space.take([P, NK])
        need_i = space.take([P, NB], I32)
        need = space.take([P, NB])
        ends = space.take([P, NB])
        slack = space.take([P, NB])
        passed = space.take([P, ST, NB])
        past = space.take([P, ST, NB])
        blk = space.take([P, ST])
        start = space.take([P, ST])
        tab_i = space.take([P, 2, ST], I32)
        tab_f = space.take([P, 2, ST])
        hot_lo = space.take([P, 4, P], BF16)
        wide_i = space.take([P, HW], I32)
        cnt_nm = space.take([P, NB])
        rel = space.take([P, SLOTS * G])
        src_i = space.take([P, SLOTS * G], I32)
        slot_space = Space(space.flat[:, space.used:NB * NP], U8)
        rows_space = Space(h_t[:, :], F32)
        hots_space = Space(n_flat, F32)
        srow = rows_space.take([P, ROWB, KC, RW])
        lo_s = rows_space.take([P, EC])
        key_w = rows_space.take([P, EC])
        wide_hot = hots_space.take([P, 2 * HOTB, HW], BF16)
        low_hot = hots_space.take([P, 2 * HOTB, P], BF16)
        win_hot = hots_space.take([P, 2 * HOTB, W])

        acc = ctx.enter_context(nc.psum_tensor("acc", [P, 8 * BANK], F32))

        loaded = signal("loaded")
        iotas = signal("iotas")
        vec = signal("vec")
        vec2 = signal("vec2")
        turned_in = signal("turned_in")
        sums = signal("sums")
        tabs_out = signal("tabs_out")
        tabs_in = signal("tabs_in")
        cnt_ready = signal("cnt_ready")
        tab_ready = signal("tab_ready")
        lo_hot = signal("lo_hot")
        lo_used = signal("lo_used")
        cleared = signal("cleared")
        rooted = signal("rooted")

        def bank_pair(i):
            return acc[:, BANK * i:BANK * i + BANK]

        full = (EC - 1) // P * P
        with nc.Block() as block:
            @on(block.sync)
            def _(sp):

                def load(to, of):
                    sp.dma_start(to, of).then_inc(loaded.h, 16)

                for k, of in ((0, src), (1, dst)):
                    load(idx_i[:, k, 0:full].rearrange("c (t e) -> c t e", e=P), of[0:full * P].rearrange("(t c e) -> c t e", t=full // P, e=P))
                load(x_nm[:, 0:NB - 1, :], x[0:(NB - 1) * P, :].rearrange("(b p) f -> p b f", p=P))
                sp.wait_ge(vec.h, vec.at(3))
                for k, of in ((0, src), (1, dst)):
                    load(idx_i[0:EC - 1 - full, k, full:full + P], of[full * P:(EC - 1) * P].rearrange("(c e) -> c e", e=P))
                    load(idx_i[EC - 1 - full:EC - full, k, full:full + ELAST], of[(EC - 1) * P:E].rearrange("(c e) -> c e", c=1))
                load(x_nm[0:NLAST, NB - 1, :], x[(NB - 1) * P:N, :])
                for to, of in ((w_l0, l0[0]), (w_l1, l1[0]), (w_msg, l3[0]), (w_upd, l3[4])):
                    load(to[:, :, :], of.rearrange("(k p) f -> p k f", p=P))
                for to, of in ((w2_l0, l0[2]), (w2_l1, l1[2]), (w1_g, l2[0]), (w2_g, l2[2]), (w2_msg, l3[2]), (w2_upd, l3[6])):
                    load(to[:, :], of)
                for k, of in enumerate((l0[1], l1[1], l2[1], l3[5])):
                    load(b_cols[0:of.shape[0], k:k + 1], of.rearrange("(p a) -> p a", a=1))
                for k, of in enumerate((l0[3], l1[3], l2[3], l3[7], l3[1], l3[3])):
                    load(b_rows[:, k, :], of.rearrange("(a f) -> a f", a=1))
                load(b1_row[:, :], l2[1].rearrange("(a f) -> a f", a=1))
                sp.wait_ge(loaded.h, loaded.at(16 * 29))

            @on(block.gpsimd)
            def _(pool):
                pool.iota(iota_i[:, :], [[1, P]], base=0, channel_multiplier=0)
                pool.iota(wide_i[:, :], [[1, HW]], base=0, channel_multiplier=0)
                pool.iota(part_i[:, :], [[1, 1]], base=0, channel_multiplier=1)
                pool.iota(slot_i[:, :], [[P, ST]], base=0, channel_multiplier=1)
                pool.iota(place_i[:, :], [[1, G]], base=0, channel_multiplier=G).then_inc(iotas.h, 1)

            @on(block.vector)
            def _(dve):
                dve.memset(x_nm[:, NB - 1, :], 0.0).then_inc(vec.h, 1)
                dve.memset(idx_i[:, :, full:full + P], NP).then_inc(vec.h, 1)
                dve.memset(b_cols[:, :], 0.0).then_inc(vec.h, 1)
                dve.memset(ones[:, :], 1.0)
                dve.memset(zeros[:, :], 0.0)
                dve.wait_ge(iotas.h, iotas.at(1))
                dve.tensor_copy(iota[:, :], iota_i[:, :]).then_inc(vec.h, 1)
                dve.tensor_copy(iota_b[:, :], iota_i[:, :])
                dve.tensor_copy(iota_w[:, :], wide_i[:, :])
                dve.tensor_copy(part[:, :], part_i[:, :]).then_inc(vec.h, 1)
                dve.tensor_copy(slot_id[:, :], slot_i[:, :])
                dve.tensor_copy(place[:, :], place_i[:, :])
                dve.wait_ge(vec.h, vec.at(5))
                dve.tensor_scalar(ident[:, :], iota[:, :], part[:, :], None, ALU.is_equal)
                dve.tensor_scalar(lower[:, :], iota[:, :], part[:, :], None, ALU.is_gt)
        vec.passed(5)
        loaded.passed(16 * 29)
        iotas.passed(1)

        with nc.Block() as block:
            @on(block.vector)
            def _(dve):
                dve.tensor_copy(idx_f[:, :, :], idx_i[:, :, :]).then_inc(vec.h, 1)
                for k in range(2):
                    dve.wait_ge(turned_in.h, turned_in.at(k + 1))
                    dve.tensor_copy(keys[:, k, :], acc[:, BANK * k:BANK * k + EC])
                    dve.tensor_copy(pair_i[:, :, k], acc[:, BANK * k:BANK * k + EC])

            @on(block.tensor)
            def _(pe):
                pe.wait_ge(vec.h, vec.at(1))
                for k in range(2):
                    for t in range(ET):
                        w = min(P, EC - t * P)
                        last = pe.transpose(acc[:, BANK * k + t * P:BANK * k + t * P + w], idx_f[0:w, k, t * P:t * P + P], ident[0:w, 0:w])
                    last.then_inc(turned_in.h, 1)
        vec.passed(1)
        turned_in.passed(2)

        def order(which):
            with nc.Block() as block:
                @on(block.vector)
                def _(dve):
                    n = [0]

                    def step(ins):
                        n[0] += 1
                        ins.then_inc(vec.h, 1)
                        dve.wait_ge(vec.h, vec.at(n[0]))

                    step(dve.tensor_copy(lo_i[:, :], keys[:, which, :]))
                    dve.tensor_scalar(buck_i[:, :], lo_i[:, :], 7, None, ALU.logical_shift_right).then_inc(vec.h, 1)
                    n[0] += 1
                    dve.wait_ge(vec.h, vec.at(n[0]))
                    step(dve.tensor_copy(buck[:, :], buck_i[:, :]))
                    for b in range(NK):
                        ins = dve.tensor_scalar(hot[:, b, :], buck[:, :], float(b), 0.0, ALU.is_equal, ALU.add,
                                                accum_out=cnt[:, b:b + 1])
                    n[0] += 1
                    ins.then_inc(vec.h, 1)
                    ins2 = dve.memset(pos[:, :], 0.0)
                    ins2.then_inc(cnt_ready.h, 1)
                    dve.wait_ge(sums.h, sums.at(1))
                    step(dve.tensor_copy(tot[:, :], acc[:, BANK:BANK + NK]))
                    step(dve.tensor_tensor_scan(first[:, :], ones[:, 0:NK], tot[:, :], 0.0, ALU.mult, ALU.add))
                    step(dve.tensor_tensor(first[:, :], first[:, :], tot[:, :], ALU.subtract))
                    step(dve.scalar_tensor_tensor(offs[:, :], acc[:, 0:NK], -1.0, first[:, :], ALU.add, ALU.add))
                    for b in range(NK):
                        step(dve.tensor_tensor_scan(ranks[:, :], ones[:, :], hot[:, b, :], offs[:, b:b + 1], ALU.mult, ALU.add))
                        step(dve.tensor_tensor(picked[:, :], ranks[:, :], hot[:, b, :], ALU.mult))
                        step(dve.tensor_tensor(pos[:, :], pos[:, :], picked[:, :], ALU.add))
                    dve.tensor_copy(pos_i[:, which, :], pos[:, :])
                    step(dve.tensor_scalar(need[:, :], tot[:, 0:NB], float(SLOT - 1), None, ALU.add))
                    step(dve.tensor_copy(need_i[:, :], need[:, :]))
                    step(dve.tensor_scalar(need_i[:, :], need_i[:, :], SLOT.bit_length() - 1, None, ALU.logical_shift_right))
                    step(dve.tensor_copy(need[:, :], need_i[:, :]))
                    step(dve.tensor_tensor_scan(ends[:, :], ones[:, 0:NB], need[:, :], 0.0, ALU.mult, ALU.add))
                    step(dve.scalar_tensor_tensor(slack[:, :], need[:, :], -float(SLOT), tot[:, 0:NB], ALU.mult, ALU.add))
                    for j in range(ST):
                        step(dve.tensor_scalar(passed[:, j, :], ends[:, :], slot_id[:, j:j + 1], None, ALU.is_le))
                        step(dve.tensor_tensor(past[:, j, :], passed[:, j, :], slack[:, :], ALU.mult))
                    step(dve.tensor_reduce(blk[:, :], passed[:, :, :], AX.X, ALU.add))
                    step(dve.tensor_reduce(start[:, :], past[:, :, :], AX.X, ALU.add))
                    step(dve.scalar_tensor_tensor(start[:, :], slot_id[:, :], float(SLOT), start[:, :], ALU.mult, ALU.add))
                    step(dve.tensor_scalar(past[:, 0, 0:ST], start[:, :], float(E - SLOT), None, ALU.min))
                    step(dve.tensor_tensor(tab_f[:, 0, :], start[:, :], past[:, 0, 0:ST], ALU.subtract))
                    step(dve.tensor_copy(tab_i[:, 0, :], past[:, 0, 0:ST]))
                    step(dve.tensor_scalar(tab_f[:, 1, :], blk[:, :], float(NB - 1), float(P), ALU.min, ALU.mult))
                    dve.tensor_copy(tab_i[:, 1, :], tab_f[:, 1, :]).then_inc(tab_ready.h, 1)
                    dve.wait_ge(tabs_in.h, tabs_in.at(32))
                    for j in range(G):
                        step(dve.tensor_scalar(shift[:, which, :, j], tab_bc[:, which, 0, 0:SLOTS], place[:, j:j + 1], MASKED,
                                               ALU.is_gt, ALU.mult))
                        step(dve.tensor_tensor(shift[:, which, :, j], shift[:, which, :, j], tab_bc[:, which, 1, 0:SLOTS], ALU.subtract))
                    order.steps = n[0]

                @on(block.tensor)
                def _(pe):
                    pe.wait_ge(cnt_ready.h, cnt_ready.at(1))
                    pe.matmul(acc[:, 0:NK], lower[:, :], cnt[:, :], start=True, stop=True)
                    pe.matmul(acc[:, BANK:BANK + NK], ones[:, 0:P], cnt[:, :], start=True, stop=True).then_inc(sums.h, 1)

                @on(block.sync)
                def _(sp):
                    sp.wait_ge(tab_ready.h, tab_ready.at(1))
                    sp.dma_start(tab_i_dram[which].rearrange("f (j p) -> p f j", p=P), tab_i[:, :, :]).then_inc(tabs_out.h, 16)
                    sp.dma_start(tab_f_dram[which].rearrange("f (j p) -> p f j", p=P), tab_f[:, :, :]).then_inc(tabs_out.h, 16)
                    sp.wait_ge(tabs_out.h, tabs_out.at(32))
                    sp.dma_start(tab_row[:, which, :, :], tab_i_dram[which].rearrange("(a f) s -> a f s", a=1)).then_inc(tabs_in.h, 16)
                    sp.dma_start(tab_bc[:, which, :, :], tab_f_dram[which].partition_broadcast(P)).then_inc(tabs_in.h, 16)
                    sp.wait_ge(tabs_in.h, tabs_in.at(32))
            vec.passed(order.steps)
            for s, k in ((cnt_ready, 1), (sums, 1), (tab_ready, 1), (tabs_out, 32), (tabs_in, 32)):
                s.passed(k)

        order(0)

        low_bound = sb("low_bound", [P, 1])
        odd = sb("odd", [P, 3])
        with nc.Block() as block:
            @on(block.vector)
            def _(dve):
                n = [0]

                def step(ins):
                    n[0] += 1
                    ins.then_inc(vec.h, 1)
                    dve.wait_ge(vec.h, vec.at(n[0]))

                dve.memset(low_bound[:, :], -LIMIT)
                step(dve.tensor_scalar(win_f[:, :], keys[0:1, 1, :].rearrange("p (m j) -> p m j", j=2)[:, :, 0:1].rearrange("p m a -> p (m a)"),
                                       float(NP - W), None, ALU.min))
                dve.tensor_copy(win_i[:, :], win_f[:, :])
                dve.wait_ge(sums.h, sums.at(1))
                step(dve.tensor_tensor(place_w[:, :].rearrange("p (m j) -> p m j", j=2), keys[:, 1, :].rearrange("p (m j) -> p m j", j=2),
                                       acc[:, 0:PAIRS].rearrange("p (m a) -> p m a", a=1).broadcast_to([P, PAIRS, 2]), ALU.subtract))
                step(dve.tensor_scalar(picked[:, :], place_w[:, :], 0.0, 0.0, ALU.is_lt, ALU.add, accum_out=odd[:, 0:1]))
                step(dve.tensor_scalar(picked[:, :], place_w[:, :], float(W), 0.0, ALU.is_ge, ALU.add, accum_out=odd[:, 1:2]))
                step(dve.scalar_tensor_tensor(lo_s[:, :], buck[:, :], -float(P), keys[:, 0, :], ALU.mult, ALU.add))
                step(dve.scalar_tensor_tensor(key_w[:, :], buck[:, :], float(W), place_w[:, :], ALU.mult, ALU.add))
                step(dve.tensor_scalar(src_g[:, :], keys[:, 0, :], float(NP - 1), None, ALU.min))
                ins = dve.memset(by_dst[:, :, :], 0.0)
                ins.then_inc(vec.h, 1)
                dve.memset(between[:, 16:NB, :].rearrange("p b n -> p (b n)").bitcast(F32), 0.0)

            @on(block.gpsimd)
            def _(pool):
                pool.wait_ge(vec.h, vec.at(7))
                pool.memset(between[:, 0:16, :].rearrange("p b n -> p (b n)").bitcast(F32), 0.0)

            @on(block.tensor)
            def _(pe):
                pe.wait_ge(vec.h, vec.at(1))
                pe.matmul(acc[:, 0:PAIRS], ones[0:1, 0:P], win_f[:, :], start=True, stop=True).then_inc(sums.h, 1)
        vec.passed(8)
        sums.passed(1)

        row_in = [signal(f"row_in{q}") for q in range(ROWB)]
        staged = signal("staged")
        scattered = [signal(f"scattered{q}") for q in range(ROWB)]
        hots_made = signal("hots_made")
        pair_done = signal("pair_done")
        taken = signal("taken")
        GROUPS = EC // KC
        ROUNDS = GROUPS // ROWB
        SC = 16 * KC
        PG = KC // 2

        def scatter_rows(which, rows_out, with_windows):
            def rounds(eng, body):
                body(0, True, False)
                with eng.Fori(1, ROUNDS - 1) as it:
                    body(it, False, False)
                body(ROUNDS - 1, False, True)

            with nc.Block() as block:
                @on(block.sync)
                def _(sp):
                    def body(it, fresh, ends_here):
                        for q in range(ROWB):
                            c = (it * ROWB + q) * KC
                            e = c * P
                            if not fresh:
                                def wait_scattered():
                                    sp.wait_ge(scattered[q].h, scattered[q].at(0) + it * SC)

                                if q == 0:
                                    wait_scattered()
                                if with_windows:
                                    sp.wait_ge(pair_done.h, pair_done.at((q + 1 - ROWB) * PG) + it * (ROWB * PG))
                                if q > 0:
                                    wait_scattered()
                            if ends_here and q == ROWB - 1:
                                sp.dma_start(srow[:, q, 0:KC - 1, 0:D],
                                             ea[e:e + (KC - 1) * P, :].rearrange("(c p) f -> p c f", p=P)).then_inc(row_in[q].h, 16)
                                sp.dma_start(srow[0:ELAST, q, KC - 1, 0:D], ea[(EC - 1) * P:E, :]).then_inc(row_in[q].h, 16)
                            else:
                                sp.dma_start(srow[:, q, :, 0:D],
                                             ea[bass.ds(e, KC * P), :].rearrange("(c p) f -> p c f", p=P)).then_inc(row_in[q].h, 16)
                    rounds(sp, body)
                    for q in range(ROWB):
                        sp.wait_ge(scattered[q].h, scattered[q].at(ROUNDS * SC))

                @on(block.gpsimd)
                def _(pool):
                    def body(it, fresh, ends_here):
                        for q in range(ROWB):
                            pool.wait_ge(staged.h, staged.at(q + 1) + it * ROWB)
                            pool.wait_ge(row_in[q].h, row_in[q].at(16 + 16 * (ends_here and q == ROWB - 1)) + it * 16)
                            pool.sem_inc(cleared.h, 1)
                            for j in range(KC):
                                pool.indirect_dma_start(rows_out, bass.IndirectOffsetOnAxis(ap=posq[:, q, j:j + 1], axis=0),
                                                        srow[:, q, j, :], None).then_inc(scattered[q].h, 16)
                    rounds(pool, body)

                def is_first(it, i):
                    return isinstance(it, int) and it == 0 and i < 0

                @on(block.vector)
                def _(dve):
                    def collect(it, i):
                        first = dve.value_load(win_i[0:1, bass.ds(it * (ROWB * PG) + i, 1)], min_val=0, max_val=NP - W)
                        dve.wait_ge(pair_done.h, pair_done.at(i + 1) + it * (ROWB * PG))
                        if not is_first(it, i - 1):
                            dve.wait_ge(taken.h, taken.at(i) + it * (ROWB * PG))
                        o = i % 4 * 2 * BANK
                        dve.tensor_tensor(between[:, :, bass.ds(first, W)], between[:, :, bass.ds(first, W)],
                                          acc[:, o:o + NB * WS].rearrange("p (b w) -> p b w", w=WS)[:, :, 0:W], ALU.add)
                        dve.tensor_tensor(by_dst[:, :, bass.ds(first, W)], by_dst[:, :, bass.ds(first, W)],
                                          acc[:, o + NB * WS:o + NB * WS + 2 * W].rearrange("p (k w) -> p k w", w=W), ALU.add)\
                           .then_inc(taken.h, 1)

                    def body(it, fresh, ends_here):
                        for q in range(ROWB):
                            c = (it * ROWB + q) * KC
                            if not fresh:
                                dve.wait_ge(scattered[q].h, scattered[q].at(0) + it * SC)
                            dve.tensor_copy(srow[:, q, :, D:RW].bitcast(I32), pair_i[:, bass.ds(c, KC), :])
                            dve.tensor_copy(posq[:, q, :], pos_i[:, which, bass.ds(c, KC)]).then_inc(staged.h, 1)
                            if not with_windows:
                                continue
                            for i in range(q * PG, q * PG + PG):
                                if not is_first(it, i - HOTB):
                                    dve.wait_ge(pair_done.h, pair_done.at(i + 1 - HOTB) + it * (ROWB * PG))
                                for j in range(2):
                                    at, h = bass.ds(it * (ROWB * KC) + 2 * i + j, 1), i % HOTB * 2 + j
                                    dve.tensor_scalar(low_hot[:, h, :], iota_b[:, :], lo_s[:, at], None, ALU.is_equal)
                                    dve.tensor_scalar(wide_hot[:, h, :], iota_w[:, :], key_w[:, at], None, ALU.is_equal)
                                    ins = dve.tensor_scalar(win_hot[:, h, :], iota[:, 0:W], place_w[:, at], None, ALU.is_equal)
                                ins.then_inc(hots_made.h, 1)
                                if i >= 2:
                                    collect(it, i - 2)
                                elif not fresh:
                                    collect(it - 1, i - 2 + ROWB * PG)
                    rounds(dve, body)
                    if with_windows:
                        for i in (ROWB * PG - 2, ROWB * PG - 1):
                            collect(ROUNDS - 1, i)

                if with_windows:
                    @on(block.tensor)
                    def _(pe):
                        def body(it, fresh, ends_here):
                            for i in range(ROWB * PG):
                                q, c = i // PG, i % PG * 2
                                pe.wait_ge(hots_made.h, hots_made.at(i + 1) + it * (ROWB * PG))
                                if c == 0:
                                    pe.wait_ge(row_in[q].h, row_in[q].at(16 + 16 * (ends_here and q == ROWB - 1)) + it * 16)
                                if not is_first(it, i - 4):
                                    pe.wait_ge(taken.h, taken.at(i - 3) + it * (ROWB * PG))
                                o, h, o2 = i % 4 * 2 * BANK, i % HOTB * 2, i % 4 * 2 * BANK + NB * WS
                                for to, b0, b1 in ((o, 0, HBLOCKS), (o + BANK, HBLOCKS, NB)):
                                    for j in range(2):
                                        pe.matmul(acc[:, to:to + (b1 - b0) * WS].rearrange("p (b w) -> p b w", w=WS)[:, :, 0:W],
                                                  low_hot[:, h + j, :], wide_hot[:, h + j, b0 * W:b1 * W].rearrange("p (b w) -> p b w", w=W),
                                                  start=j == 0, stop=j == 1)
                                for j in range(2):
                                    pe.matmul(acc[:, o2:o2 + W], srow[:, q, c + j, 0:D], win_hot[:, h + j, :], start=j == 0, stop=j == 1)
                                for j in range(2):
                                    last = pe.matmul(acc[:, o2 + W:o2 + 2 * W], ones[:, 0:P], win_hot[:, h + j, :], start=j == 0, stop=j == 1)
                                last.then_inc(pair_done.h, 1)
                        rounds(pe, body)
            staged.passed(GROUPS)
            for q in range(ROWB):
                row_in[q].passed(16 * (ROUNDS + (q == ROWB - 1)))
                scattered[q].passed(ROUNDS * SC)
            if with_windows:
                for s in (hots_made, pair_done, taken):
                    s.passed(PAIRS)

        scatter_rows(0, rows_by_src, True)

        rows_space.again()
        hots_space.again()
        rows = rows_space.take([P, BUF, G, RW])
        onehot = hots_space.take([P, BUF * G, P])
        relq = hots_space.take([P, BUF, G])
        excess = rows_space.take([P, NB])
        junk = rows_space.take([P, NP], U8)
        odd_all = sb("odd_all", [1, 4])


        slot_in = [signal(f"slot_in{q}") for q in range(BUF)]
        hot_ready = signal("hot_ready")
        hot_used = signal("hot_used")
        rel_ready = signal("rel_ready")
        evac = signal("evac")
        LOOPS = SLOTS // BUF
        MLOOPS = SLOTS // MB

        def open_banks(pe, m=P):
            for k in range(BANKS):
                pe.matmul(acc[0:m, BANK * k:BANK * k + BANK], zeros[0:1, 0:m], zeros[0:1, :], start=True, stop=False)

        def close_banks(pe, m=P):
            for k in range(BANKS):
                last = pe.matmul(acc[0:m, BANK * k:BANK * k + BANK], zeros[0:1, 0:m], zeros[0:1, :], start=False, stop=True)
            return last

        def column(eng, which, slot):
            return eng.value_load(tab_row[0:1, which, 1, bass.ds(slot, 1)], min_val=0, max_val=NP - P)

        def first_row(eng, which, slot):
            return eng.value_load(tab_row[0:1, which, 0, bass.ds(slot, 1)], min_val=0, max_val=E - SLOT)

        def sum_edges(which, rows_in, keep, to, on_act=None):
            with nc.Block() as block:
                @on(block.sync)
                def _(sp):
                    def body(it, fresh):
                        for q in range(BUF):
                            row = first_row(sp, which, it * BUF + q)
                            if not fresh:
                                sp.wait_ge(hot_used.h, hot_used.at(q + 1 - BUF) + it * BUF)
                            sp.dma_start(rows[:, q, :, :], rows_in[bass.ds(row, SLOT), :].rearrange("(p j) w -> p j w", j=G))\
                              .then_inc(slot_in[q].h, 16)
                    body(0, True)
                    with sp.Fori(1, LOOPS) as it:
                        body(it, False)

                @on(block.vector)
                def _(dve):
                    def body(it, fresh):
                        for q in range(BUF):
                            slot = it * BUF + q
                            dve.wait_ge(slot_in[q].h, slot_in[q].at(16) + it * 16)
                            if not fresh:
                                dve.wait_ge(hot_used.h, hot_used.at(q + 1 - BUF) + it * BUF)
                            key = rows[:, q, :, D + which:D + which + 1].bitcast(I32).rearrange("p j a -> p (j a)")
                            dve.tensor_tensor(relq[:, q, :], key, shift[:, which, bass.ds(slot, 1), :].rearrange("p s j -> p (s j)"), ALU.add)\
                               .then_inc(rel_ready.h, 1)
                            if keep:
                                dve.tensor_tensor(rel[:, bass.ds(slot * G, G)], key, shift[:, which, bass.ds(slot, 1), :].rearrange("p s j -> p (s j)"), ALU.add)
                                dve.tensor_copy(src_i[:, bass.ds(slot * G, G)], rows[:, q, :, D:D + 1].bitcast(I32).rearrange("p j a -> p (j a)"))
                            dve.wait_ge(rel_ready.h, rel_ready.at(q + 1) + it * BUF)
                            for j in range(G):
                                ins = dve.tensor_scalar(onehot[:, q * G + j, :], iota[:, :], relq[:, q, j:j + 1], None, ALU.is_equal)
                            ins.then_inc(hot_ready.h, 1)
                    body(0, True)
                    with dve.Fori(1, LOOPS) as it:
                        body(it, False)
                    dve.wait_ge(evac.h, evac.at(1))
                    for k, c, w in banks():
                        dve.tensor_copy(to[:, c:c + w], acc[:, c:c + w])

                if on_act is not None:
                    @on(block.scalar)
                    def _(act):
                        on_act(act)

                @on(block.tensor)
                def _(pe):
                    open_banks(pe)

                    def body(it):
                        for q in range(BUF):
                            col = column(pe, which, it * BUF + q)
                            pe.wait_ge(hot_ready.h, hot_ready.at(q + 1) + it * BUF)
                            pe.wait_ge(slot_in[q].h, slot_in[q].at(16) + it * 16)
                            for j in range(G):
                                last = pe.matmul(acc[:, bass.ds(col, P)], rows[:, q, j, 0:D], onehot[:, q * G + j, :],
                                                 start=False, stop=False)
                            last.then_inc(hot_used.h, 1)
                    with pe.Fori(0, LOOPS) as it:
                        body(it)
                    close_banks(pe).then_inc(evac.h, 1)
            for q in range(BUF):
                slot_in[q].passed(16 * LOOPS)
            for s in (hot_ready, hot_used, rel_ready):
                s.passed(SLOTS)
            evac.passed(1)

        checked = signal("checked")

        def check_counts(act):
            for b in range(NB):
                act.activation(junk[:, :], between[:, b, :], ACT.Relu, bias=low_bound[:, :], accum_out=excess[:, b:b + 1])\
                   .then_inc(checked.h, 1)
                if b < NB - 1:
                    act.wait_ge(checked.h, checked.at(b + 1))

        sum_edges(0, rows_by_src, False, agg_sum, check_counts)

        with nc.Block() as block:
            @on(block.vector)
            def _(dve):
                dve.tensor_reduce(odd[:, 2:3], excess[:, :], AX.X, ALU.add).then_inc(vec.h, 1)
                dve.wait_ge(sums.h, sums.at(1))
                dve.tensor_reduce(odd_all[:, 0:1], acc[0:1, 0:3], AX.X, ALU.add).then_inc(vec.h, 1)
                dve.wait_ge(vec.h, vec.at(2))
                dve.tensor_scalar(flags[:, FAST:FAST + 1], odd_all[:, 0:1], float(EP - E), None, ALU.is_equal)
                dve.tensor_scalar(flags[:, GENERAL:GENERAL + 1], odd_all[:, 0:1], float(EP - E), None, ALU.not_equal)

            @on(block.tensor)
            def _(pe):
                pe.wait_ge(vec.h, vec.at(1))
                pe.matmul(acc[0:1, 0:3], ones[:, 0:1], odd[:, :], start=True, stop=True).then_inc(sums.h, 1)
        vec.passed(2)
        sums.passed(1)

        with path(GENERAL):
            order(1)
            LB = 4
            with nc.Block() as block:
                @on(block.vector)
                def _(dve):
                    dve.tensor_scalar(buck_i[:, :], lo_i[:, :], P - 1, None, ALU.bitwise_and).then_inc(vec.h, 1)
                    dve.wait_ge(vec.h, vec.at(1))
                    dve.tensor_copy(lo_f[:, :], buck_i[:, :]).then_inc(vec.h, 1)
                    dve.wait_ge(vec.h, vec.at(2))
                    with dve.Fori(0, EC // LB) as it:
                        for q in range(LB):
                            dve.wait_ge(lo_used.h, it * LB + q + lo_used.at(1))
                            dve.tensor_scalar(hot_lo[:, q, :], iota_b[:, :], lo_f[:, bass.ds(it * LB + q, 1)], None,
                                              ALU.is_equal).then_inc(lo_hot.h, 1)
                    dve.wait_ge(sums.h, sums.at(1))
                    def step(ins, k):
                        ins.then_inc(vec.h, 1)
                        dve.wait_ge(vec.h, vec.at(k))
                    step(dve.tensor_copy(cnt_nm[:, :], acc[:, 0:NB]), 3)

                @on(block.tensor)
                def _(pe):
                    for q in range(LB):
                        pe.sem_inc(lo_used.h, 1)
                    pe.matmul(acc[:, 0:BANK], zeros[0:1, 0:P], zeros[0:1, :], start=True, stop=False)
                    with pe.Fori(0, EC // LB) as it:
                        for q in range(LB):
                            pe.wait_ge(lo_hot.h, it * LB + q + lo_hot.at(1))
                            pe.matmul(acc[:, 0:NB], hot_lo[:, q, :], hot[:, 0:NB, bass.ds(it * LB + q, 1)].rearrange("p b c -> p (b c)"),
                                      start=False, stop=False).then_inc(lo_used.h, 1)
                    pe.matmul(acc[:, 0:BANK], zeros[0:1, 0:P], zeros[0:1, :], start=False, stop=True).then_inc(sums.h, 1)

                @on(block.sync)
                def _(sp):
                    sp.wait_ge(vec.h, vec.at(3))
                    sp.dma_start(cnt_dram.rearrange("(b p) -> p b", p=P), cnt_nm[:, :]).then_inc(tabs_out.h, 16)
                    sp.wait_ge(tabs_out.h, tabs_out.at(16))
                    sp.dma_start(cnt_bc, cnt_dram.partition_broadcast(P)).then_inc(tabs_in.h, 16)
                    sp.wait_ge(tabs_in.h, tabs_in.at(16))
            vec.passed(3)
            sums.passed(1)
            tabs_out.passed(16)
            tabs_in.passed(16)
            lo_used.passed(EC + LB)
            lo_hot.passed(EC)

            rows_space.again()
            rows_space.take([P, ROWB, KC, RW])
            scatter_rows(1, rows_by_dst, False)
            sum_edges(1, rows_by_dst, True, agg_dst)

        mean_done = signal("mean_done")
        turned_out = signal("turned_out")
        relu_done = signal("relu_done")
        first_mm = signal("first_mm")
        hidden = signal("hidden")
        second_mm = signal("second_mm")
        added = signal("added")

        def norm():
            with nc.Block() as block:
                @on(block.vector)
                def _(dve):
                    for b in range(NB):
                        ins = dve.bn_stats(stats[:, b, :], x_nm[:, b, :])
                    ins.then_inc(vec.h, 1)
                    dve.wait_ge(vec.h, vec.at(1))
                    for b in range(NB):
                        ins = dve.bn_aggr(mv[:, b, :], stats[:, b, :])
                    ins.then_inc(vec.h, 1)
                    dve.wait_ge(vec.h, vec.at(2))
                    dve.tensor_scalar(rstd[:, :], mv[:, :, 1:2].rearrange("p b a -> p (b a)"), EPS, None, ALU.add).then_inc(vec.h, 1)
                    dve.wait_ge(rooted.h, rooted.at(1))
                    dve.reciprocal(rstd[:, :], std[:, :]).then_inc(vec.h, 1)
                    dve.wait_ge(vec.h, vec.at(4))
                    for b in range(NB):
                        ins = dve.tensor_scalar(n_nm[:, b, :], x_nm[:, b, :], mv[:, b, 0:1], rstd[:, b:b + 1], ALU.subtract, ALU.mult)
                        if b % 4 == 3 or b == NB - 1:
                            ins.then_inc(mean_done.h, 1)


                @on(block.tensor)
                def _(pe):
                    for k, c, w in banks():
                        pe.wait_ge(mean_done.h, mean_done.at(k + 1))
                        for b in range(w // P):
                            last = pe.transpose(acc[:, c + b * P:c + b * P + P], n_nm[:, 4 * k + b, :], ident[:, :])
                        last.then_inc(turned_out.h, 1)

                @on(block.scalar)
                def _(act):
                    act.wait_ge(vec.h, vec.at(3))
                    act.activation(std[:, :], rstd[:, :], ACT.Sqrt).then_inc(rooted.h, 1)
                    for k, c, w in banks():
                        act.wait_ge(turned_out.h, turned_out.at(k + 1))
                        act.activation(h_t[:, c:c + w], acc[:, c:c + w], ACT.Relu)
            vec.passed(4)
            rooted.passed(1)
            mean_done.passed(BANKS)
            turned_out.passed(BANKS)

        def dense(parts, bias, w2, row, rows_in, to_x=True):
            with nc.Block() as block:
                @on(block.tensor)
                def _(pe):
                    for k, c, w in banks():
                        if k >= 2:
                            pe.wait_ge(hidden.h, hidden.at(k - 1))
                        for i, (wt, t) in enumerate(parts):
                            last = pe.matmul(acc[:, BANK * (k % 2):BANK * (k % 2) + w], wt, t[:, c:c + w],
                                             start=i == 0, stop=i == len(parts) - 1)
                        last.then_inc(first_mm.h, 1)
                        pe.wait_ge(hidden.h, hidden.at(k + 1))
                        if k >= 2:
                            pe.wait_ge(added.h, added.at(k - 1))
                        o = BANK * (2 + k % 2)
                        pe.matmul(acc[:, o:o + w], ones[0:1, 0:P], b_rows[0:1, row:row + 1, :].broadcast_to([1, w // P, D]),
                                  start=True, stop=False)
                        for b in range(w // P):
                            last = pe.matmul(acc[:, o + b * P:o + b * P + P], hid_t[:, c + b * P:c + b * P + P], w2,
                                             start=False, stop=b == w // P - 1)
                        last.then_inc(second_mm.h, 1)

                @on(block.scalar)
                def _(act):
                    for k, c, w in banks():
                        act.wait_ge(first_mm.h, first_mm.at(k + 1))
                        act.activation(hid_t[:, c:c + w], acc[:, BANK * (k % 2):BANK * (k % 2) + w], ACT.Relu, bias=bias)\
                           .then_inc(hidden.h, 1)

                @on(block.vector)
                def _(dve):
                    for k, c, w in banks():
                        dve.wait_ge(second_mm.h, second_mm.at(k + 1))
                        o = BANK * (2 + k % 2)
                        xb = x_nm[:, 4 * k:4 * k + w // P, :].rearrange("p b f -> p (b f)")
                        dve.tensor_tensor(xb, xb, acc[:, o:o + w], ALU.add).then_inc(added.h, 1)
            for s in (first_mm, hidden, second_mm, added):
                s.passed(BANKS)

        with nc.Block() as block:
            @on(block.gpsimd)
            def _(pool):
                pool.tensor_tensor(agg_sum[:, :], agg_sum[:, :], agg_dst, ALU.add)

            @on(block.vector)
            def _(dve):
                dve.tensor_scalar(h_t[:, :], cnt_bc, 1.0, None, ALU.add).then_inc(vec.h, 1)
                dve.wait_ge(rooted.h, rooted.at(1))
                dve.reciprocal(dinv_bc[:, :], hid_t).then_inc(vec.h, 1)
                dve.wait_ge(sums.h, sums.at(1))
                dve.tensor_copy(dinv_nm[:, :], acc[:, 0:NB])

            @on(block.scalar)
            def _(act):
                act.wait_ge(vec.h, vec.at(1))
                act.activation(hid_t, h_t[:, :], ACT.Sqrt).then_inc(rooted.h, 1)

            @on(block.tensor)
            def _(pe):
                pe.wait_ge(vec.h, vec.at(2))
                for b in range(NB):
                    last = pe.matmul(acc[:, b:b + 1], dinv_bc[0:1, b * P:b * P + P], ones[0:1, 0:1], start=True, stop=True)
                last.then_inc(sums.h, 1)
        vec.passed(2)
        rooted.passed(1)
        sums.passed(1)

        norm()
        dense([(w_l0[:, 0, :], h_t), (w_l0[:, 1, :], agg_sum)], b_cols[:, 0:1], w2_l0[:, :], 0, None)
        norm()
        dense([(w_l1[:, 0, :], h_t), (w_l1[:, 1, :], agg_dst)], b_cols[:, 1:2], w2_l1[:, :], 1, None)
        norm()

        table_out = signal("table_out")
        gathered = [signal(f"gathered{q}") for q in range(BUF)]
        idx_ready = signal("idx_ready")
        z_nm, z_rest = n_nm[:, :, 0:H2], n_nm[:, :, H2:2 * H2]
        y_nm = agg_dst.rearrange("p (b f) -> p b f", f=D)[:, :, 0:H2]
        parts_space = Space(agg_sum[:, :], F32)
        z_parts = parts_space.take([P, NB, 3 * H2], BF16)
        exact = Space(h_t[:, :], F32).take([P, 2, NB, P], BF16)
        cast = [signal(f"cast{h}") for h in range(2)]
        parted = signal("parted")
        summed_z = signal("summed_z")
        read_z = signal("read_z")
        dinv_z = dinv_nm[:, :].rearrange("p (b a) -> p b a", a=1).broadcast_to([P, NB, H2])

        def flight_buffers():
            slot_space.again()
            return (slot_space.take([P, MB * G, P]), slot_space.take([P, MB, G], I32), slot_space.take([P, MB * G, D]))

        def store_table(sp, table, tile):
            sp.dma_start(table.rearrange("(b p) f -> p b f", p=P), tile).then_inc(table_out.h, 16)
            sp.wait_ge(table_out.h, table_out.at(16))

        slot_onehot, idxq, got = flight_buffers()

        def gather_z(table):
            with nc.Block() as block:
                @on(block.vector)
                def _(dve):
                    def body(it, fresh):
                        for q in range(MB):
                            slot = it * MB + q
                            if not fresh:
                                dve.wait_ge(gathered[q].h, gathered[q].at(0) + it * (16 * G))
                            dve.tensor_copy(idxq[:, q, :], src_i[:, bass.ds(slot * G, G)]).then_inc(idx_ready.h, 1)
                            if not fresh:
                                dve.wait_ge(hot_used.h, hot_used.at(q + 1 - MB) + it * MB)
                            for j in range(G):
                                ins = dve.tensor_scalar(slot_onehot[:, q * G + j, :], iota[:, :], rel[:, bass.ds(slot * G + j, 1)], None, ALU.is_equal)
                            ins.then_inc(hot_ready.h, 1)
                    body(0, True)
                    with dve.Fori(1, MLOOPS) as it:
                        body(it, False)

                @on(block.gpsimd)
                def _(pool):
                    def body(it, fresh):
                        for q in range(MB):
                            pool.wait_ge(idx_ready.h, idx_ready.at(q + 1) + it * MB)
                            if not fresh:
                                pool.wait_ge(hot_used.h, hot_used.at(q + 1 - MB) + it * MB)
                            pool.sem_inc(cleared.h, 1)
                            for j in range(G):
                                pool.indirect_dma_start(got[:, q * G + j, 0:H2], None, table,
                                                        bass.IndirectOffsetOnAxis(ap=idxq[:, q, j:j + 1], axis=0)).then_inc(gathered[q].h, 16)
                    body(0, True)
                    with pool.Fori(1, MLOOPS) as it:
                        body(it, False)

                @on(block.tensor)
                def _(pe):
                    open_banks(pe, H2)
                    with pe.Fori(0, MLOOPS) as it:
                        for q in range(MB):
                            col = column(pe, 1, it * MB + q)
                            pe.wait_ge(hot_ready.h, hot_ready.at(q + 1) + it * MB)
                            pe.wait_ge(gathered[q].h, gathered[q].at(16 * G) + it * (16 * G))
                            for j in range(G):
                                last = pe.matmul(acc[0:H2, bass.ds(col, P)], got[:, q * G + j, 0:H2], slot_onehot[:, q * G + j, :],
                                                 start=False, stop=False)
                            last.then_inc(hot_used.h, 1)
                    close_banks(pe, H2)
            for s in (idx_ready, hot_ready, hot_used):
                s.passed(SLOTS)
            for q in range(MB):
                gathered[q].passed(16 * G * MLOOPS)

        def spread():
            def convert(eng, half, it, u):
                b0, b1 = ((0, NB // 2), (NB // 2, NB))[half]
                if not (isinstance(it, int) and it == 0 and u < 2):
                    eng.wait_ge(summed_z.h, summed_z.at(u - 1) + it * UB)
                of, to = between[:, b0:b1, bass.ds(it * (UB * P) + u * P, P)], exact[:, u % 2, b0:b1, :]
                if half == 0:
                    eng.activation(to, of, ACT.Copy).then_inc(cast[half].h, 1)
                else:
                    eng.tensor_copy(to, of).then_inc(cast[half].h, 1)

            with path(FAST):
                with nc.Block() as block:
                    @on(block.vector)
                    def _(dve):
                        dve.tensor_copy(z_parts[:, :, 0:H2], z_nm).then_inc(parted.h, 1)
                        dve.wait_ge(parted.h, parted.at(1))
                        dve.tensor_tensor(z_rest, z_nm, z_parts[:, :, 0:H2], ALU.subtract).then_inc(parted.h, 1)
                        dve.wait_ge(parted.h, parted.at(2))
                        dve.tensor_copy(z_parts[:, :, H2:2 * H2], z_rest).then_inc(parted.h, 1)
                        dve.wait_ge(parted.h, parted.at(3))
                        dve.tensor_tensor(z_parts[:, :, 2 * H2:3 * H2], z_rest, z_parts[:, :, H2:2 * H2], ALU.subtract).then_inc(parted.h, 1)
                        def add_up(it, u):
                            dve.wait_ge(summed_z.h, summed_z.at(u + 1) + it * UB)
                            dve.tensor_reduce(agg_dst[:, bass.ds(it * (UB * D) + u * D, H2)],
                                              acc[:, u * BANK:u * BANK + 3 * H2].rearrange("p (k f) -> p f k", f=H2), AX.X, ALU.add)\
                               .then_inc(read_z.h, 1)

                        def body(it, fresh):
                            for u in range(UB):
                                convert(dve, 1, it, u)
                                if u >= 1:
                                    add_up(it, u - 1)
                                elif not fresh:
                                    add_up(it - 1, UB - 1)
                        body(0, True)
                        with dve.Fori(1, NB // UB) as it:
                            body(it, False)
                        for u in range(NB % UB + 1):
                            if u < NB % UB:
                                convert(dve, 1, NB // UB, u)
                            add_up(NB // UB - (u == 0), (u - 1) % UB)

                    @on(block.scalar)
                    def _(act):
                        for u in range(UB):
                            convert(act, 0, 0, u)
                        with act.Fori(1, NB // UB) as it:
                            for u in range(UB):
                                convert(act, 0, it, u)
                        for u in range(NB % UB):
                            convert(act, 0, NB // UB, u)

                    @on(block.tensor)
                    def _(pe):
                        pe.wait_ge(parted.h, parted.at(4))

                        def body(it, fresh, blocks=UB):
                            for u in range(blocks):
                                for h in range(2):
                                    pe.wait_ge(cast[h].h, cast[h].at(u + 1) + it * UB)
                                if not fresh:
                                    pe.wait_ge(read_z.h, read_z.at(u + 1 - UB) + it * UB)
                                for b in range(NB):
                                    last = pe.matmul(acc[:, u * BANK:u * BANK + 3 * H2], exact[:, u % 2, b, :], z_parts[:, b, :],
                                                     start=b == 0, stop=b == NB - 1)
                                last.then_inc(summed_z.h, 1)
                        body(0, True)
                        with pe.Fori(1, NB // UB) as it:
                            body(it, False)
                        body(NB // UB, False, NB % UB)
                parted.passed(4)
                for c in (summed_z, read_z, *cast):
                    c.passed(NB)
            with path(GENERAL):
                with nc.Block() as block:
                    @on(block.sync)
                    def _(sp):
                        store_table(sp, z_table, z_nm)
                table_out.passed(16)
                gather_z(z_table)
                with nc.Block() as block:
                    @on(block.vector)
                    def _(dve):
                        for k, c, w in banks():
                            ins = dve.tensor_copy(agg_sum[0:H2, c:c + w], acc[0:H2, c:c + w])
                        ins.then_inc(first_mm.h, 1)
                        dve.wait_ge(turned_out.h, turned_out.at(1))
                        dve.tensor_copy(y_nm, acc[:, 0:NB * H2].rearrange("p (b f) -> p b f", f=H2))

                    @on(block.tensor)
                    def _(pe):
                        pe.wait_ge(first_mm.h, first_mm.at(1))
                        for b in range(NB):
                            last = pe.transpose(acc[:, b * H2:b * H2 + H2], agg_sum[0:H2, b * P:b * P + P], ident[0:H2, 0:H2])
                        last.then_inc(turned_out.h, 1)
                first_mm.passed(1)
                turned_out.passed(1)

        with nc.Block() as block:
            @on(block.vector)
            def _(dve):
                for k, c, w in banks():
                    dve.tensor_tensor(h_t[:, c:c + w], h_t[:, c:c + w], dinv_bc[:, c:c + w], ALU.mult).then_inc(added.h, 1)
                dve.wait_ge(first_mm.h, first_mm.at(1))
                dve.tensor_copy(z_nm, acc[:, 0:NB * H2].rearrange("p (b f) -> p b f", f=H2))

            @on(block.tensor)
            def _(pe):
                for k, c, w in banks():
                    pe.wait_ge(added.h, added.at(k + 1))
                    for b in range(4 * k, 4 * k + w // P):
                        last = pe.matmul(acc[:, b * H2:b * H2 + H2], h_t[:, b * P:b * P + P], w1_g[:, :], start=True, stop=True)
                last.then_inc(first_mm.h, 1)
        first_mm.passed(1)
        added.passed(BANKS)

        spread()

        with nc.Block() as block:
            @on(block.tensor)
            def _(pe):
                pe.matmul(acc[:, 0:H2], ones[0:1, 0:P], b1_row[:, :], start=True, stop=True).then_inc(first_mm.h, 1)

            @on(block.vector)
            def _(dve):
                dve.tensor_tensor(y_nm, y_nm, z_nm, ALU.add).then_inc(vec.h, 1)
                dve.wait_ge(vec.h, vec.at(1))
                dve.tensor_tensor(y_nm, y_nm, dinv_z, ALU.mult).then_inc(vec.h, 1)
                dve.wait_ge(vec.h, vec.at(2))
                dve.wait_ge(first_mm.h, first_mm.at(1))
                dve.tensor_tensor(y_nm, y_nm, acc[:, 0:H2].rearrange("p (a f) -> p a f", a=1).broadcast_to([P, NB, H2]), ALU.add)\
                   .then_inc(vec.h, 1)
                dve.wait_ge(vec.h, vec.at(3))
                dve.scalar_tensor_tensor(z_nm, y_nm, 0.0, dinv_z, ALU.max, ALU.mult)
        vec.passed(3)
        first_mm.passed(1)

        spread()

        with nc.Block() as block:
            @on(block.vector)
            def _(dve):
                dve.tensor_tensor(y_nm, y_nm, z_nm, ALU.add).then_inc(vec.h, 1)
                dve.wait_ge(vec.h, vec.at(1))
                dve.tensor_tensor(y_nm, y_nm, dinv_z, ALU.mult).then_inc(vec.h, 1)
                for k, c, w in banks():
                    dve.wait_ge(second_mm.h, second_mm.at(k + 1))
                    xb = x_nm[:, 4 * k:4 * k + w // P, :].rearrange("p b f -> p (b f)")
                    dve.tensor_tensor(xb, xb, acc[:, c:c + w], ALU.add)

            @on(block.tensor)
            def _(pe):
                pe.wait_ge(vec.h, vec.at(2))
                for k, c, w in banks():
                    for b in range(w // P):
                        last = pe.transpose(acc[0:H2, c + b * P:c + b * P + P], y_nm[:, 4 * k + b, :], ident[:, :])
                    last.then_inc(turned_out.h, 1)
                for k, c, w in banks():
                    pe.wait_ge(hidden.h, hidden.at(k + 1))
                    pe.matmul(acc[:, c:c + w], ones[0:1, 0:P], b_rows[0:1, 2:3, :].broadcast_to([1, w // P, D]), start=True, stop=False)
                    for b in range(w // P):
                        last = pe.matmul(acc[:, c + b * P:c + b * P + P], h_t[0:H2, c + b * P:c + b * P + P], w2_g[:, :],
                                         start=False, stop=b == w // P - 1)
                    last.then_inc(second_mm.h, 1)

            @on(block.scalar)
            def _(act):
                for k, c, w in banks():
                    act.wait_ge(turned_out.h, turned_out.at(k + 1))
                    act.activation(h_t[0:H2, c:c + w], acc[0:H2, c:c + w], ACT.Copy).then_inc(hidden.h, 1)
        vec.passed(2)
        for s in (turned_out, hidden, second_mm):
            s.passed(BANKS)
        norm()

        p_nm = n_nm
        q_nm = agg_dst.rearrange("p (b f) -> p b f", f=D)
        with nc.Block() as block:
            @on(block.tensor)
            def _(pe):
                for k, c, w in banks():
                    for b in range(w // P):
                        last = pe.matmul(acc[:, c + b * P:c + b * P + P], h_t[:, c + b * P:c + b * P + P], w_msg[:, 0, :], start=True, stop=True)
                    last.then_inc(first_mm.h, 1)
                for k, c, w in banks():
                    pe.wait_ge(added.h, added.at(k + 1))
                    pe.matmul(acc[:, c:c + w], ones[0:1, 0:P], b_rows[0:1, 4:5, :].broadcast_to([1, w // P, D]), start=True, stop=False)
                    for b in range(w // P):
                        last = pe.matmul(acc[:, c + b * P:c + b * P + P], h_t[:, c + b * P:c + b * P + P], w_msg[:, 1, :],
                                         start=False, stop=b == w // P - 1)
                    last.then_inc(second_mm.h, 1)

            @on(block.vector)
            def _(dve):
                for k, c, w in banks():
                    dve.wait_ge(first_mm.h, first_mm.at(k + 1))
                    dve.tensor_copy(p_nm[:, :, :].rearrange("p b f -> p (b f)")[:, c:c + w], acc[:, c:c + w]).then_inc(added.h, 1)

            @on(block.scalar)
            def _(act):
                for k, c, w in banks():
                    act.wait_ge(second_mm.h, second_mm.at(k + 1))
                    act.activation(agg_dst[:, c:c + w], acc[:, c:c + w], ACT.Copy).then_inc(hidden.h, 1)

            @on(block.sync)
            def _(sp):
                sp.wait_ge(added.h, added.at(BANKS))
                store_table(sp, p_table, p_nm[:, :, :])
                sp.wait_ge(hidden.h, hidden.at(BANKS))
                sp.dma_start(q_table.rearrange("(b p) f -> p b f", p=P), q_nm).then_inc(table_out.h, 16)
                sp.wait_ge(table_out.h, table_out.at(32))
        for s, k in ((first_mm, BANKS), (added, BANKS), (second_mm, BANKS), (hidden, BANKS), (table_out, 32)):
            s.passed(k)

        slot_space.again()
        onehot = slot_space.take([P, MB * G, P])
        idxq = slot_space.take([P, MB, G], I32)
        got = slot_space.take([P, MB * G, D])
        rows = slot_space.take([P, MB, G, D])
        turned = slot_space.take([P, 2, 2 * P])
        msg = slot_space.take([P, 2, D])
        relued = slot_space.take([P, 2, D])
        q_win = slot_space.take([W, MB, D])

        turn = signal("turn")
        turn_out = signal("turn_out")
        made = signal("made")
        plus = signal("plus")
        cut = signal("cut")
        collected = signal("collected")
        summed = signal("summed")
        win_in = [signal(f"win_in{q}") for q in range(MB)]
        CH = MB * G

        def sum_messages(windows):
            loops, width = (PAIRS // MB, W) if windows else (MLOOPS, P)

            def first_node(eng, n):
                if windows:
                    return eng.value_load(win_i[0:1, bass.ds(n, 1)], min_val=0, max_val=NP - W)
                return column(eng, 1, n)

            def chunk(i):
                return (i % CH) // G, i % G

            def is_first(it, i):
                return isinstance(it, int) and it == 0 and i < 0

            with nc.Block() as block:
                @on(block.sync)
                def _(sp):
                    def body(it, fresh, ends_here):
                        for q in range(MB):
                            if windows:
                                first = first_node(sp, it * MB + q)
                                e = (it * MB + q) * SLOT
                            else:
                                row = first_row(sp, 1, it * MB + q)
                            if not fresh:
                                sp.wait_ge(made.h, made.at((q + 1) * G - CH) + it * CH)
                            if not windows:
                                sp.dma_start(rows[:, q, :, :], rows_by_dst[bass.ds(row, SLOT), 0:D].rearrange("(p j) w -> p j w", j=G))\
                                  .then_inc(slot_in[q].h, 16)
                                continue
                            if ends_here and q == MB - 1:
                                sp.dma_start(rows[:, q, 0, :], ea[e:e + P, :]).then_inc(slot_in[q].h, 16)
                                sp.dma_start(rows[0:ELAST, q, 1, :], ea[e + P:E, :]).then_inc(slot_in[q].h, 16)
                            else:
                                sp.dma_start(rows[:, q, :, :], ea[bass.ds(e, SLOT), :].rearrange("(j p) w -> p j w", j=G))\
                                  .then_inc(slot_in[q].h, 16)
                            sp.dma_start(q_win[:, q, :], q_table[bass.ds(first, W), :]).then_inc(win_in[q].h, 16)
                    body(0, True, False)
                    with sp.Fori(1, loops - 1) as it:
                        body(it, False, False)
                    body(loops - 1, False, True)

                @on(block.gpsimd)
                def _(pool):
                    def body(it, fresh):
                        for q in range(MB):
                            pool.wait_ge(idx_ready.h, idx_ready.at(q + 1) + it * MB)
                            if not fresh:
                                pool.wait_ge(plus.h, plus.at((q + 1) * G - CH) + it * CH)
                            pool.sem_inc(cleared.h, 1)
                            for j in range(G):
                                pool.indirect_dma_start(got[:, q * G + j, :], None, p_table,
                                                        bass.IndirectOffsetOnAxis(ap=idxq[:, q, j:j + 1], axis=0)).then_inc(gathered[q].h, 16)
                    body(0, True)
                    with pool.Fori(1, loops) as it:
                        body(it, False)

                @on(block.vector)
                def _(dve):
                    places, sources = (place_w, src_g) if windows else (rel, src_i)

                    def add(it, i):
                        q, j = chunk(i)
                        dve.wait_ge(made.h, made.at(i + 1) + it * CH)
                        dve.wait_ge(gathered[q].h, gathered[q].at(16 * G) + it * (16 * G))
                        if not is_first(it, i - 2):
                            dve.wait_ge(cut.h, cut.at(i - 1) + it * CH)
                        dve.tensor_tensor(msg[:, i % 2, :], acc[:, (2 + i % 2) * BANK:(2 + i % 2) * BANK + P], got[:, i, :], ALU.add)\
                           .then_inc(plus.h, 1)

                    def collect(it, q):
                        col = first_node(dve, it * MB + q)
                        dve.wait_ge(summed.h, summed.at((q + 1) * G) + it * CH)
                        if not is_first(it, q - 1):
                            dve.wait_ge(collected.h, collected.at(q) + it * MB)
                        o = (4 + q % 2) * BANK
                        dve.tensor_tensor(agg_sum[:, bass.ds(col, width)], agg_sum[:, bass.ds(col, width)], acc[:, o:o + width], ALU.add)\
                           .then_inc(collected.h, 1)

                    dve.memset(agg_sum[:, :], 0.0).then_inc(parted.h, 1)
                    dve.wait_ge(parted.h, parted.at(1))

                    def body(it, fresh):
                        for q in range(MB):
                            n = it * MB + q
                            if not fresh:
                                dve.wait_ge(gathered[q].h, gathered[q].at(0) + it * (16 * G))
                            dve.tensor_copy(idxq[:, q, :], sources[:, bass.ds(n * G, G)]).then_inc(idx_ready.h, 1)
                            if q >= BEHIND:
                                collect(it, q - BEHIND)
                            elif not fresh:
                                collect(it - 1, q - BEHIND + MB)
                            for j in range(G):
                                if not fresh:
                                    dve.wait_ge(summed.h, summed.at(q * G + j + 1 - CH) + it * CH)
                                dve.tensor_scalar(onehot[:, q * G + j, 0:width], iota[:, 0:width], places[:, bass.ds(n * G + j, 1)], None,
                                                  ALU.is_equal).then_inc(hot_ready.h, 1)
                                i = q * G + j - HEAD
                                if i >= 0:
                                    add(it, i)
                                elif not fresh:
                                    add(it - 1, i + CH)
                    HEAD, BEHIND = 2 * G, 3
                    body(0, True)
                    with dve.Fori(1, loops) as it:
                        body(it, False)
                    for q in range(MB, MB + BEHIND):
                        collect(loops - 1, q - BEHIND)
                        for i in range(q * G - HEAD, min((q + 1) * G - HEAD, CH)):
                            add(loops - 1, i)

                @on(block.scalar)
                def _(act):
                    def out_of_psum(it, i):
                        act.wait_ge(turn.h, turn.at(i + 1) + it * CH)
                        if not is_first(it, i - 2):
                            act.wait_ge(made.h, made.at(i - 1) + it * CH)
                        o = i % 2 * BANK
                        if width < P:
                            act.activation(turned[0:width, i % 2, P:2 * P], acc[0:width, o + P:o + 2 * P], ACT.Copy)
                            act.activation(turned[:, i % 2, 0:P], acc[:, o:o + P], ACT.Copy).then_inc(turn_out.h, 1)
                        else:
                            act.activation(turned[:, i % 2, :], acc[:, o:o + 2 * P], ACT.Copy).then_inc(turn_out.h, 1)

                    def relu(it, i):
                        act.wait_ge(plus.h, plus.at(i + 1) + it * CH)
                        if not is_first(it, i - 2):
                            act.wait_ge(summed.h, summed.at(i - 1) + it * CH)
                        act.activation(relued[:, i % 2, :], msg[:, i % 2, :], ACT.Relu).then_inc(cut.h, 1)

                    def body(it, fresh):
                        for i in range(CH):
                            out_of_psum(it, i)
                            if i >= 1:
                                relu(it, i - 1)
                            elif not fresh:
                                relu(it - 1, CH - 1)
                    body(0, True)
                    with act.Fori(1, loops) as it:
                        body(it, False)
                    relu(loops - 1, CH - 1)

                @on(block.tensor)
                def _(pe):
                    def turn_chunk(it, i, ends_here):
                        q, j = chunk(i)
                        pe.wait_ge(hot_ready.h, hot_ready.at(i + 1) + it * CH)
                        if j == 0:
                            pe.wait_ge(slot_in[q].h, slot_in[q].at(16 + 16 * (windows and ends_here and q == MB - 1)) + it * 16)
                        if not is_first(it, i - 2):
                            pe.wait_ge(turn_out.h, turn_out.at(i - 1) + it * CH)
                        o = i % 2 * BANK
                        pe.transpose(acc[:, o:o + P], rows[:, q, j, :], ident[:, :])
                        pe.transpose(acc[0:width, o + P:o + 2 * P], onehot[:, i, 0:width], ident[:, :]).then_inc(turn.h, 1)

                    def product(it, i, col):
                        q, j = chunk(i)
                        pe.wait_ge(turn_out.h, turn_out.at(i + 1) + it * CH)
                        if windows and j == 0:
                            pe.wait_ge(win_in[q].h, win_in[q].at(16) + it * 16)
                        if not is_first(it, i - 2):
                            pe.wait_ge(plus.h, plus.at(i - 1) + it * CH)
                        o = (2 + i % 2) * BANK
                        pe.matmul(acc[:, o:o + P], turned[:, i % 2, 0:P], w_msg[:, 2, :], start=True, stop=False)
                        pe.matmul(acc[:, o:o + P], turned[0:width, i % 2, P:2 * P], q_win[:, q, :] if windows else agg_dst[:, bass.ds(col, P)],
                                  start=False, stop=True).then_inc(made.h, 1)

                    def total(it, i):
                        q, j = chunk(i)
                        pe.wait_ge(cut.h, cut.at(i + 1) + it * CH)
                        if j == 0 and not is_first(it, q - 2):
                            pe.wait_ge(collected.h, collected.at(q - 1) + it * MB)
                        o = (4 + q % 2) * BANK
                        pe.matmul(acc[:, o:o + width], relued[:, i % 2, :], onehot[:, i, 0:width], start=j == 0, stop=j == G - 1)\
                          .then_inc(summed.h, 1)

                    def column_of(n):
                        return None if windows else column(pe, 1, n)

                    def body(it, fresh, ends_here):
                        if not fresh:
                            product_col = column_of(it * MB - 1)
                        for i in range(CH):
                            turn_chunk(it, i, ends_here)
                            if i >= 1:
                                product(it, i - 1, product_col)
                            elif not fresh:
                                product(it - 1, CH - 1, product_col)
                            if i % G == 0:
                                product_col = column_of(it * MB + i // G)
                            if i >= 3:
                                total(it, i - 3)
                            elif not fresh:
                                total(it - 1, CH + i - 3)
                    body(0, True, False)
                    with pe.Fori(1, loops - 1) as it:
                        body(it, False, False)
                    body(loops - 1, False, True)
                    product(loops - 1, CH - 1, column_of(loops * MB - 1))
                    for i in range(CH - 3, CH):
                        total(loops - 1, i)

        with path(FAST):
            sum_messages(True)
        with path(GENERAL):
            sum_messages(False)

        with nc.Block() as block:
            @on(block.vector)
            def _(dve):
                dve.tensor_scalar(dinv_bc[0:1, :], cnt_bc[0:1, :], 1.0, None, ALU.min).then_inc(vec.h, 1)
                for k, c, w in banks():
                    dve.tensor_scalar(hid_t[:, c:c + w], cnt_bc[:, c:c + w], 1.0, None, ALU.max).then_inc(vec.h, 1)
                    dve.wait_ge(vec.h, vec.at(2 * k + 2))
                    dve.reciprocal(hid_t[:, c:c + w], hid_t[:, c:c + w]).then_inc(vec.h, 1)
                    dve.wait_ge(vec.h, vec.at(2 * k + 3))
                    dve.tensor_tensor(hid_t[:, c:c + w], agg_sum[:, c:c + w], hid_t[:, c:c + w], ALU.mult).then_inc(first_mm.h, 1)

            @on(block.tensor)
            def _(pe):
                for k, c, w in banks():
                    pe.wait_ge(first_mm.h, first_mm.at(k + 1))
                    pe.matmul(acc[:, c:c + w], w2_msg[:, :], hid_t[:, c:c + w], start=True, stop=False)
                    pe.matmul(acc[:, c:c + w], b_rows[0:1, 5, :], dinv_bc[0:1, c:c + w], start=False, stop=True).then_inc(second_mm.h, 1)

            @on(block.scalar)
            def _(act):
                for k, c, w in banks():
                    act.wait_ge(second_mm.h, second_mm.at(k + 1))
                    act.activation(agg_dst[:, c:c + w], acc[:, c:c + w], ACT.Copy)
        vec.passed(2 * BANKS + 1)
        first_mm.passed(BANKS)
        second_mm.passed(BANKS)
        dense([(w_upd[:, 0, :], h_t), (w_upd[:, 1, :], agg_dst)], b_cols[:, 3:4], w2_upd[:, :], 3, None)

        out_done = signal("out_done")
        with nc.Block() as block:
            @on(block.sync)
            def _(sp):
                sp.dma_start(out[0:(NB - 1) * P, :].rearrange("(b p) f -> p b f", p=P), x_nm[:, 0:NB - 1, :]).then_inc(out_done.h, 16)
                sp.dma_start(out[(NB - 1) * P:N, :], x_nm[0:NLAST, NB - 1, :]).then_inc(out_done.h, 16)
                sp.wait_ge(out_done.h, out_done.at(32))


_INS = ["x", "src", "dst", "edge_attr_128"] + [f"L0_gnn_{n}" for n in ("W1", "b1", "W2", "b2")] \
    + [f"L1_gnn_{n}" for n in ("W1", "b1", "W2", "b2")] + [f"L2_gnn_{n}" for n in ("W1", "b1", "W2", "b2")] \
    + [f"L3_gnn_{a}_{n}" for a in ("msg", "upd") for n in ("w1", "b1", "w2", "b2")]


def kernel(**inputs):
    import numpy as _np
    import concourse.bacc as _bacc
    from concourse import mybir as _mybir
    from concourse.bass_utils import run_bass_kernel_spmd as _run

    nc = _bacc.Bacc("TRN2", target_bir_lowering=False, num_devices=1)
    arrays, args = {}, []
    for name in _INS:
        a = _np.ascontiguousarray(inputs[name])
        arrays[f"in_{name}"] = a
        args.append(nc.dram_tensor(f"in_{name}", a.shape, _mybir.dt.from_np(a.dtype), kind="ExternalInput").ap())
    out = nc.dram_tensor("out", (N, D), F32, kind="ExternalOutput").ap()
    build(nc, *args[0:4], args[4:8], args[8:12], args[12:16], args[16:24], out)
    r = _run(nc, [arrays], core_ids=[0])
    return r.results[0]["out"]
```

```python
import numpy as np
import concourse.bass as bass
from concourse import mybir
from contextlib import ExitStack, contextmanager

F32 = mybir.dt.float32
I32 = mybir.dt.int32
BF16 = mybir.dt.bfloat16
F16 = mybir.dt.float16
U8 = mybir.dt.uint8
BYTES = {F32: 4, I32: 4, BF16: 2, F16: 2, U8: 1}
ALU = mybir.AluOpType
ACT = mybir.ActivationFunctionType
AX = mybir.AxisListType

P = 128
N, E, D, H2 = 3125, 53125, 128, 64
NB = -(-N // P)
NP = NB * P
NLAST = N - (NB - 1) * P
EC = -(-E // P)
EP = EC * P
ELAST = E - (EC - 1) * P
ET = -(-EC // P)
NK = NB + 1
G = 2
SLOT = G * P
GS = (4, G)
BUF = 8
BUFS = (BUF * G // GS[0], BUF)
SLOTS_OF = [-(-((E + NB * (g * P - 1)) // (g * P)) // BUF) * BUF for g in GS]
SLOTS = SLOTS_OF[1]
ST = -(-SLOTS // P)
RW = D + 2
BANK = 512
BANKS = -(-NP // BANK)
MB = 4
FL = 8
MR = 4
DG = 4
ACT_BLOCKS = 14
UB = 6
MASKED = 4096.0
EPS = 1e-5
KC = 4
W = 24
PAIRS = EC // 2
HW = NB * W
HBLOCKS = 16
WS = BANK // HBLOCKS
LIMIT = 254.0
FAST, GENERAL = 0, 1
ROWB = 4
HOTB = 4


class Signal:
    path = None

    def __init__(self, make):
        self.make, self.on_path, self.base = make, {}, {}

    @property
    def h(self):
        if Signal.path not in self.on_path:
            self.on_path[Signal.path] = self.make()
        return self.on_path[Signal.path]

    def at(self, n):
        return self.base.get(Signal.path, 0) + n

    def passed(self, n):
        self.base[Signal.path] = self.at(n)


@contextmanager
def path(which):
    Signal.path = which
    yield
    Signal.path = None


class Space:

    def __init__(self, flat, dt):
        self.flat, self.unit, self.used = flat, BYTES[dt], 0

    def again(self):
        self.used = 0

    def take(self, shape, dt=F32):
        size = -(-int(np.prod(shape[1:])) * BYTES[dt] // 4) * 4
        first, self.used = self.used, self.used + size
        assert self.used <= self.flat.shape[1] * self.unit
        ap = self.flat[0:shape[0], first // self.unit:self.used // self.unit]
        if BYTES[dt] * ap.shape[1] != size or dt not in (F32, U8) or BYTES[dt] != self.unit:
            ap = ap.bitcast(dt)
        ap = ap[:, 0:int(np.prod(shape[1:]))]
        names = "abc"[:len(shape) - 1]
        if len(names) > 1:
            ap = ap.rearrange(f"p ({' '.join(names)}) -> p {' '.join(names)}", **dict(zip(names, shape[1:])))
        return ap


def banks():
    return [(k, BANK * k, min(BANK, NP - BANK * k)) for k in range(BANKS)]


def build(nc, x, src, dst, ea, l0, l1, l2, l3, out):
    ctx = ExitStack()
    with ctx:
        nc_ctx = ctx.enter_context(nc.allow_non_contiguous_dma(reason="small tables and bias columns"))

        def sb(name, shape, dt=F32):
            return ctx.enter_context(nc.sbuf_tensor(name, shape, dt))

        made_signals = [0]

        def signal(name):
            def make():
                made_signals[0] += 1
                return ctx.enter_context(nc.semaphore(f"{name}_{made_signals[0]}"))
            return Signal(make)

        def on(register):
            def wrap(f):
                @register
                def _(eng):
                    if Signal.path is None:
                        f(eng)
                    else:
                        with eng.If(eng.value_load(flags[0:1, Signal.path:Signal.path + 1], min_val=0, max_val=1)):
                            f(eng)
            return wrap

        def dram(name, shape, dt=F32):
            return nc.dram_tensor(name, shape, dt, kind="Internal").ap()

        rows_by_src = dram("rows_by_src", (EP, RW))
        rows_by_dst = dram("rows_by_dst", (EP, RW))
        tab_i_dram = [dram(f"tab_i{k}", (2, ST * P), I32) for k in range(2)]
        tab_f_dram = [dram(f"tab_f{k}", (2, ST * P)) for k in range(2)]
        z_table = dram("z_table", (NP, H2))
        p_table = dram("p_table", (NP, D))
        q_table = dram("q_table", (NP * 3, D), BF16)
        cnt_dram = dram("cnt_dram", (NP,))
        factor_dram = dram("factor_dram", (2, NP))

        x_nm = sb("x_nm", [P, NB, D])
        h_t = sb("h_t", [P, NP])
        n_nm = sb("n_nm", [P, NB, D])
        n_flat = n_nm[:, :, :].rearrange("p b f -> p (b f)")
        hid_t = n_flat
        by_dst = sb("by_dst", [P, 2, NP])
        agg_dst, cnt_bc = by_dst[:, 0, :], by_dst[:, 1, :]
        agg_sum = sb("agg_sum", [P, NP])
        mean_bc = sb("mean_bc", [P, NP])
        dinv_nm = sb("dinv_nm", [P, NB])
        degree = sb("degree", [P, NB])
        root = sb("root", [P, NB])
        factors = sb("factors", [P, 2, NB])
        stats = sb("stats", [P, NB, 6])
        mv = sb("mv", [P, NB, 2])
        rstd = sb("rstd", [P, NB])
        std = sb("std", [P, NB])
        between = sb("between", [P, NB, NP], U8)
        flags = sb("flags", [1, 2], I32)

        iota_i = sb("iota_i", [P, P], I32)
        part_i = sb("part_i", [P, 1], I32)
        slot_i = sb("slot_i", [P, ST], I32)
        place_i = sb("place_i", [P, 2, GS[0]], I32)
        iota = sb("iota", [P, P])
        iota_b = sb("iota_b", [P, P], BF16)
        iota_w = sb("iota_w", [P, HW], F16)
        part = sb("part", [P, 1])
        slot_id = sb("slot_id", [P, ST])
        place = sb("place", [P, 2, GS[0]])
        ident = sb("ident", [P, P])
        lower = sb("lower", [P, P])
        ones = sb("ones", [P, EC])
        ones_b = sb("ones_b", [P, P], BF16)
        zeros = sb("zeros", [1, BANK])

        w_l0 = sb("w_l0", [P, 2, D])
        w_l1 = sb("w_l1", [P, 2, D])
        w2_l0 = sb("w2_l0", [P, D])
        w2_l1 = sb("w2_l1", [P, D])
        w1_g = sb("w1_g", [P, H2])
        w2_g = sb("w2_g", [H2, D])
        w_msg = sb("w_msg", [P, 3, D])
        w2_msg = sb("w2_msg", [P, D])
        w_upd = sb("w_upd", [P, 2, D])
        w2_upd = sb("w2_upd", [P, D])
        b_cols = sb("b_cols", [P, 4])
        b_rows = sb("b_rows", [1, 6, D])
        b1_row = sb("b1_row", [1, H2])

        tab_row = sb("tab_row", [1, 2, 2, ST * P], I32)
        tab_bc = sb("tab_bc", [P, 2, 2, ST * P])
        shifts = [sb(f"shift{k}", [P, SLOTS_OF[k], GS[k]]) for k in range(2)]

        win_f = sb("win_f", [1, PAIRS])
        win_i = sb("win_i", [1, PAIRS], I32)
        place_w = sb("place_w", [P, EC])
        win_nodes = sb("win_nodes", [3 * W, PAIRS])
        in_win = sb("in_win", [3 * W, 1])
        in_win_i = sb("in_win_i", [3 * W, 1], I32)
        src_g = sb("src_g", [P, EC], I32)

        grid_space = Space(mean_bc[:, :], F32)
        keys = grid_space.take([P, 2, EC])
        pair_i = grid_space.take([P, EC, 2], I32)
        pos_i = grid_space.take([P, 2, EC], I32)
        posq = sb("posq", [P, ROWB, KC], I32)

        space = Space(between[:, :, :].rearrange("p b n -> p (b n)"), U8)
        rel = space.take([P, SLOTS * G])
        src_i = space.take([P, SLOTS * G], I32)
        slot_space = Space(space.flat[:, space.used:NB * NP], U8)
        buck_i = space.take([P, EC], I32)
        lo_i = space.take([P, EC], I32)
        lo_f = space.take([P, EC])
        buck = space.take([P, EC])
        hot = space.take([P, NK, EC], BF16)
        ranks = space.take([P, NK, EC])
        picked = space.take([P, EC])
        pos = space.take([P, EC])
        cnt = space.take([P, NK])
        tot = space.take([P, NK])
        first = space.take([P, NK])
        offs = space.take([P, NK])
        need_i = space.take([P, NB], I32)
        need = space.take([P, NB])
        ends = space.take([P, NB])
        slack = space.take([P, NB])
        passed = space.take([P, ST, NB])
        past = space.take([P, ST, NB])
        blk = space.take([P, ST])
        start = space.take([P, ST])
        tab_i = space.take([P, 2, ST], I32)
        tab_f = space.take([P, 2, ST])
        early_space = Space(n_flat, F32)
        hot_lo = early_space.take([P, 4, P], BF16)
        idx_i = early_space.take([P, 2, ET * P], I32)
        idx_f = early_space.take([P, 2, ET * P])
        wide_i = early_space.take([P, HW], I32)
        cnt_nm = space.take([P, NB])
        rows_space = Space(h_t[:, :], F32)
        hots_space = Space(n_flat, F32)
        srow = rows_space.take([P, ROWB, KC, RW])
        lo_s = rows_space.take([P, EC])
        key_w = rows_space.take([P, EC])
        wide_hot = hots_space.take([P, 2 * HOTB, HW], BF16)
        low_hot = hots_space.take([P, 2 * HOTB, P], BF16)
        win_hot = hots_space.take([P, 2 * HOTB, W])
        away = sb("away", [P, 2 * HOTB, P], BF16)

        acc = ctx.enter_context(nc.psum_tensor("acc", [P, 8 * BANK], F32))

        loaded = signal("loaded")
        iotas = signal("iotas")
        vec = signal("vec")
        vec2 = signal("vec2")
        turned_in = signal("turned_in")
        sums = signal("sums")
        tabs_out = signal("tabs_out")
        tabs_in = signal("tabs_in")
        cnt_ready = signal("cnt_ready")
        tab_ready = signal("tab_ready")
        lo_hot = signal("lo_hot")
        lo_used = signal("lo_used")
        cleared = signal("cleared")
        rooted = signal("rooted")

        def bank_pair(i):
            return acc[:, BANK * i:BANK * i + BANK]

        full = (EC - 1) // P * P
        with nc.Block() as block:
            @on(block.sync)
            def _(sp):

                def load(to, of):
                    sp.dma_start(to, of).then_inc(loaded.h, 16)

                for k, of in ((0, src), (1, dst)):
                    load(idx_i[:, k, 0:full].rearrange("c (t e) -> c t e", e=P), of[0:full * P].rearrange("(t c e) -> c t e", t=full // P, e=P))
                sp.wait_ge(vec.h, vec.at(3))
                for k, of in ((0, src), (1, dst)):
                    load(idx_i[0:EC - 1 - full, k, full:full + P], of[full * P:(EC - 1) * P].rearrange("(c e) -> c e", e=P))
                    load(idx_i[EC - 1 - full:EC - full, k, full:full + ELAST], of[(EC - 1) * P:E].rearrange("(c e) -> c e", c=1))
                sp.wait_ge(loaded.h, loaded.at(16 * 6))

            @on(block.gpsimd)
            def _(pool):
                pool.iota(iota_i[:, :], [[1, P]], base=0, channel_multiplier=0)
                pool.iota(wide_i[:, :], [[1, HW]], base=0, channel_multiplier=0)
                pool.iota(part_i[:, :], [[1, 1]], base=0, channel_multiplier=1)
                pool.iota(slot_i[:, :], [[P, ST]], base=0, channel_multiplier=1)
                for k in range(2):
                    last = pool.iota(place_i[:, k, :], [[1, GS[0]]], base=0, channel_multiplier=GS[k])
                last.then_inc(iotas.h, 1)

            @on(block.vector)
            def _(dve):
                dve.memset(x_nm[:, NB - 1, :], 0.0).then_inc(vec.h, 1)
                dve.memset(idx_i[:, :, full:full + P], NP).then_inc(vec.h, 1)
                dve.memset(b_cols[:, :], 0.0).then_inc(vec.h, 1)
                dve.memset(ones[:, :], 1.0)
                dve.memset(ones_b[:, :], 1.0)
                dve.memset(zeros[:, :], 0.0)
                dve.wait_ge(iotas.h, iotas.at(1))
                dve.tensor_copy(iota[:, :], iota_i[:, :]).then_inc(vec.h, 1)
                dve.tensor_copy(iota_b[:, :], iota_i[:, :])
                dve.tensor_copy(iota_w[:, :], wide_i[:, :])
                dve.tensor_copy(part[:, :], part_i[:, :]).then_inc(vec.h, 1)
                dve.tensor_copy(slot_id[:, :], slot_i[:, :])
                dve.tensor_copy(place[:, :, :], place_i[:, :, :])
                dve.wait_ge(vec.h, vec.at(5))
                dve.tensor_scalar(ident[:, :], iota[:, :], part[:, :], None, ALU.is_equal)
                dve.tensor_scalar(lower[:, :], iota[:, :], part[:, :], None, ALU.is_gt)
        vec.passed(5)
        loaded.passed(16 * 6)
        iotas.passed(1)

        with nc.Block() as block:
            @on(block.vector)
            def _(dve):
                dve.tensor_copy(idx_f[:, :, :], idx_i[:, :, :]).then_inc(vec.h, 1)
                for k in range(2):
                    dve.wait_ge(turned_in.h, turned_in.at(k + 1))
                    dve.tensor_copy(keys[:, k, :], acc[:, BANK * k:BANK * k + EC])
                    dve.tensor_copy(pair_i[:, :, k], acc[:, BANK * k:BANK * k + EC])

            @on(block.tensor)
            def _(pe):
                pe.wait_ge(vec.h, vec.at(1))
                for k in range(2):
                    for t in range(ET):
                        w = min(P, EC - t * P)
                        last = pe.transpose(acc[:, BANK * k + t * P:BANK * k + t * P + w], idx_f[0:w, k, t * P:t * P + P], ident[0:w, 0:w])
                    last.then_inc(turned_in.h, 1)
        vec.passed(1)
        turned_in.passed(2)

        def load_rest(sp):
            def load(to, of):
                sp.dma_start(to, of).then_inc(loaded.h, 16)

            load(x_nm[:, 0:NB - 1, :], x[0:(NB - 1) * P, :].rearrange("(b p) f -> p b f", p=P))
            load(x_nm[0:NLAST, NB - 1, :], x[(NB - 1) * P:N, :])
            for to, of in ((w_l0, l0[0]), (w_l1, l1[0]), (w_msg, l3[0]), (w_upd, l3[4])):
                load(to[:, :, :], of.rearrange("(k p) f -> p k f", p=P))
            for to, of in ((w2_l0, l0[2]), (w2_l1, l1[2]), (w1_g, l2[0]), (w2_g, l2[2]), (w2_msg, l3[2]), (w2_upd, l3[6])):
                load(to[:, :], of)
            for k, of in enumerate((l0[1], l1[1], l2[1], l3[5])):
                load(b_cols[0:of.shape[0], k:k + 1], of.rearrange("(p a) -> p a", a=1))
            for k, of in enumerate((l0[3], l1[3], l2[3], l3[7], l3[1], l3[3])):
                load(b_rows[:, k, :], of.rearrange("(a f) -> a f", a=1))
            load(b1_row[:, :], l2[1].rearrange("(a f) -> a f", a=1))

        def order(which, at_start=None):
            slot = GS[which] * P
            with nc.Block() as block:
                @on(block.vector)
                def _(dve):
                    n = [0]

                    def step(ins):
                        n[0] += 1
                        ins.then_inc(vec.h, 1)
                        dve.wait_ge(vec.h, vec.at(n[0]))

                    step(dve.tensor_copy(lo_i[:, :], keys[:, which, :]))
                    dve.tensor_scalar(buck_i[:, :], lo_i[:, :], 7, None, ALU.logical_shift_right).then_inc(vec.h, 1)
                    n[0] += 1
                    dve.wait_ge(vec.h, vec.at(n[0]))
                    step(dve.tensor_copy(buck[:, :], buck_i[:, :]))
                    for b in range(NK):
                        ins = dve.tensor_scalar(hot[:, b, :], buck[:, :], float(b), 0.0, ALU.is_equal, ALU.add,
                                                accum_out=cnt[:, b:b + 1])
                    n[0] += 1
                    ins.then_inc(vec.h, 1)
                    ins2 = dve.memset(pos[:, :], 0.0)
                    ins2.then_inc(cnt_ready.h, 1)
                    dve.wait_ge(sums.h, sums.at(1))
                    step(dve.tensor_copy(tot[:, :], acc[:, BANK:BANK + NK]))
                    step(dve.tensor_tensor_scan(first[:, :], ones[:, 0:NK], tot[:, :], 0.0, ALU.mult, ALU.add))
                    step(dve.tensor_tensor(first[:, :], first[:, :], tot[:, :], ALU.subtract))
                    step(dve.scalar_tensor_tensor(offs[:, :], acc[:, 0:NK], -1.0, first[:, :], ALU.add, ALU.add))
                    for b in range(NK):
                        ins = dve.tensor_tensor_scan(ranks[:, b, :], ones[:, :], hot[:, b, :], offs[:, b:b + 1], ALU.mult, ALU.add)
                    step(ins)
                    step(dve.tensor_tensor(ranks[:, :, :], ranks[:, :, :], hot[:, :, :], ALU.mult))
                    step(dve.tensor_reduce(pos[:, :], ranks[:, :, :].rearrange("p b c -> p c b"), AX.X, ALU.add))
                    dve.tensor_copy(pos_i[:, which, :], pos[:, :])
                    step(dve.tensor_scalar(need[:, :], tot[:, 0:NB], float(slot - 1), None, ALU.add))
                    step(dve.tensor_copy(need_i[:, :], need[:, :]))
                    step(dve.tensor_scalar(need_i[:, :], need_i[:, :], slot.bit_length() - 1, None, ALU.logical_shift_right))
                    step(dve.tensor_copy(need[:, :], need_i[:, :]))
                    step(dve.tensor_tensor_scan(ends[:, :], ones[:, 0:NB], need[:, :], 0.0, ALU.mult, ALU.add))
                    step(dve.scalar_tensor_tensor(slack[:, :], need[:, :], -float(slot), tot[:, 0:NB], ALU.mult, ALU.add))
                    for j in range(ST):
                        step(dve.tensor_scalar(passed[:, j, :], ends[:, :], slot_id[:, j:j + 1], None, ALU.is_le))
                        step(dve.tensor_tensor(past[:, j, :], passed[:, j, :], slack[:, :], ALU.mult))
                    step(dve.tensor_reduce(blk[:, :], passed[:, :, :], AX.X, ALU.add))
                    step(dve.tensor_reduce(start[:, :], past[:, :, :], AX.X, ALU.add))
                    step(dve.scalar_tensor_tensor(start[:, :], slot_id[:, :], float(slot), start[:, :], ALU.mult, ALU.add))
                    step(dve.tensor_scalar(past[:, 0, 0:ST], start[:, :], float(E - slot), None, ALU.min))
                    step(dve.tensor_tensor(tab_f[:, 0, :], start[:, :], past[:, 0, 0:ST], ALU.subtract))
                    step(dve.tensor_copy(tab_i[:, 0, :], past[:, 0, 0:ST]))
                    step(dve.tensor_scalar(tab_f[:, 1, :], blk[:, :], float(NB - 1), float(P), ALU.min, ALU.mult))
                    dve.tensor_copy(tab_i[:, 1, :], tab_f[:, 1, :]).then_inc(tab_ready.h, 1)
                    dve.wait_ge(tabs_in.h, tabs_in.at(32))
                    for j in range(GS[which]):
                        step(dve.tensor_scalar(shifts[which][:, :, j], tab_bc[:, which, 0, 0:SLOTS_OF[which]], place[:, which, j:j + 1], MASKED,
                                               ALU.is_gt, ALU.mult))
                        step(dve.tensor_tensor(shifts[which][:, :, j], shifts[which][:, :, j], tab_bc[:, which, 1, 0:SLOTS_OF[which]], ALU.subtract))
                    order.steps = n[0]

                @on(block.tensor)
                def _(pe):
                    pe.wait_ge(cnt_ready.h, cnt_ready.at(1))
                    pe.matmul(acc[:, 0:NK], lower[:, :], cnt[:, :], start=True, stop=True)
                    pe.matmul(acc[:, BANK:BANK + NK], ones[:, 0:P], cnt[:, :], start=True, stop=True).then_inc(sums.h, 1)

                @on(block.sync)
                def _(sp):
                    if at_start is not None:
                        at_start(sp)
                    sp.wait_ge(tab_ready.h, tab_ready.at(1))
                    sp.dma_start(tab_i_dram[which].rearrange("f (j p) -> p f j", p=P), tab_i[:, :, :]).then_inc(tabs_out.h, 16)
                    sp.dma_start(tab_f_dram[which].rearrange("f (j p) -> p f j", p=P), tab_f[:, :, :]).then_inc(tabs_out.h, 16)
                    sp.wait_ge(tabs_out.h, tabs_out.at(32))
                    sp.dma_start(tab_row[:, which, :, :], tab_i_dram[which].rearrange("(a f) s -> a f s", a=1)).then_inc(tabs_in.h, 16)
                    sp.dma_start(tab_bc[:, which, :, :], tab_f_dram[which].partition_broadcast(P)).then_inc(tabs_in.h, 16)
                    sp.wait_ge(tabs_in.h, tabs_in.at(32))
            vec.passed(order.steps)
            for s, k in ((cnt_ready, 1), (sums, 1), (tab_ready, 1), (tabs_out, 32), (tabs_in, 32)):
                s.passed(k)

        order(0, load_rest)

        low_bound = sb("low_bound", [P, 1])
        odd = sb("odd", [P, 3])
        with nc.Block() as block:
            @on(block.vector)
            def _(dve):
                n = [0]

                def step(ins):
                    n[0] += 1
                    ins.then_inc(vec.h, 1)
                    dve.wait_ge(vec.h, vec.at(n[0]))

                dve.memset(low_bound[:, :], -LIMIT)
                step(dve.tensor_scalar(win_f[:, :], keys[0:1, 1, :].rearrange("p (m j) -> p m j", j=2)[:, :, 0:1].rearrange("p m a -> p (m a)"),
                                       float(NP - W), None, ALU.min))
                dve.tensor_copy(win_i[:, :], win_f[:, :])
                dve.wait_ge(sums.h, sums.at(1))
                step(dve.tensor_tensor(place_w[:, :].rearrange("p (m j) -> p m j", j=2), keys[:, 1, :].rearrange("p (m j) -> p m j", j=2),
                                       acc[:, 0:PAIRS].rearrange("p (m a) -> p m a", a=1).broadcast_to([P, PAIRS, 2]), ALU.subtract))
                dve.tensor_scalar(in_win_i[:, :], part[0:3 * W, :], 43.0, None, ALU.mult)
                step(dve.tensor_scalar(picked[:, :], place_w[:, :], 0.0, 0.0, ALU.is_lt, ALU.add, accum_out=odd[:, 0:1]))
                dve.tensor_scalar(in_win_i[:, :], in_win_i[:, :], 7, None, ALU.logical_shift_right)
                step(dve.tensor_scalar(picked[:, :], place_w[:, :], float(W), 0.0, ALU.is_ge, ALU.add, accum_out=odd[:, 1:2]))
                step(dve.scalar_tensor_tensor(lo_s[:, :], buck[:, :], -float(P), keys[:, 0, :], ALU.mult, ALU.add))
                dve.tensor_copy(in_win[:, :], in_win_i[:, :])
                step(dve.scalar_tensor_tensor(key_w[:, :], buck[:, :], float(W), place_w[:, :], ALU.mult, ALU.add))
                dve.tensor_scalar(win_nodes[:, :], acc[0:3 * W, 0:PAIRS], in_win[:, :], None, ALU.add)
                step(dve.tensor_scalar(src_g[:, :], keys[:, 0, :], float(NP - 1), None, ALU.min))
                ins = dve.memset(by_dst[:, :, :], 0.0)
                ins.then_inc(vec.h, 1)
                dve.memset(between[:, 16:NB, :].rearrange("p b n -> p (b n)").bitcast(F32), 0.0)

            @on(block.sync)
            def _(sp):
                sp.wait_ge(loaded.h, loaded.at(16 * 23))

            @on(block.gpsimd)
            def _(pool):
                pool.wait_ge(vec.h, vec.at(7))
                pool.memset(between[:, 0:16, :].rearrange("p b n -> p (b n)").bitcast(F32), 0.0)

            @on(block.tensor)
            def _(pe):
                pe.wait_ge(vec.h, vec.at(1))
                pe.matmul(acc[:, 0:PAIRS], ones[0:1, 0:P], win_f[:, :], start=True, stop=True).then_inc(sums.h, 1)
        vec.passed(8)
        sums.passed(1)

        row_in = [signal(f"row_in{q}") for q in range(ROWB)]
        staged = signal("staged")
        scattered = [signal(f"scattered{q}") for q in range(ROWB)]
        hots_made = signal("hots_made")
        lows_made = signal("lows_made")
        away_made = signal("away_made")
        pair_done = signal("pair_done")
        taken = signal("taken")
        GROUPS = EC // KC
        ROUNDS = GROUPS // ROWB
        SC = 16 * KC
        PG = KC // 2

        def scatter_rows(which, rows_out, with_windows):
            def rounds(eng, body):
                body(0, True, False)
                with eng.Fori(1, ROUNDS - 1) as it:
                    body(it, False, False)
                body(ROUNDS - 1, False, True)

            with nc.Block() as block:
                @on(block.sync)
                def _(sp):
                    def body(it, fresh, ends_here):
                        for q in range(ROWB):
                            c = (it * ROWB + q) * KC
                            e = c * P
                            if not fresh:
                                def wait_scattered():
                                    sp.wait_ge(scattered[q].h, scattered[q].at(0) + it * SC)

                                if q == 0:
                                    wait_scattered()
                                if with_windows:
                                    sp.wait_ge(pair_done.h, pair_done.at((q + 1 - ROWB) * PG) + it * (ROWB * PG))
                                if q > 0:
                                    wait_scattered()
                            if ends_here and q == ROWB - 1:
                                sp.dma_start(srow[:, q, 0:KC - 1, 0:D],
                                             ea[e:e + (KC - 1) * P, :].rearrange("(c p) f -> p c f", p=P)).then_inc(row_in[q].h, 16)
                                sp.dma_start(srow[0:ELAST, q, KC - 1, 0:D], ea[(EC - 1) * P:E, :]).then_inc(row_in[q].h, 16)
                            else:
                                sp.dma_start(srow[:, q, :, 0:D],
                                             ea[bass.ds(e, KC * P), :].rearrange("(c p) f -> p c f", p=P)).then_inc(row_in[q].h, 16)
                    rounds(sp, body)
                    for q in range(ROWB):
                        sp.wait_ge(scattered[q].h, scattered[q].at(ROUNDS * SC))

                @on(block.gpsimd)
                def _(pool):
                    def body(it, fresh, ends_here):
                        for q in range(ROWB):
                            pool.wait_ge(staged.h, staged.at(q + 1) + it * ROWB)
                            pool.wait_ge(row_in[q].h, row_in[q].at(16 + 16 * (ends_here and q == ROWB - 1)) + it * 16)
                            pool.sem_inc(cleared.h, 1)
                            for j in range(KC):
                                pool.indirect_dma_start(rows_out, bass.IndirectOffsetOnAxis(ap=posq[:, q, j:j + 1], axis=0),
                                                        srow[:, q, j, :], None).then_inc(scattered[q].h, 16)
                    rounds(pool, body)

                def is_first(it, i):
                    return isinstance(it, int) and it == 0 and i < 0

                @on(block.scalar)
                def _(act):
                    def body(it, fresh, ends_here):
                        for q in range(ROWB):
                            c = (it * ROWB + q) * KC
                            if not fresh:
                                act.wait_ge(scattered[q].h, scattered[q].at(0) + it * SC)
                            act.activation(srow[:, q, :, D:RW].bitcast(I32), pair_i[:, bass.ds(c, KC), :], ACT.Copy)
                            act.activation(posq[:, q, :], pos_i[:, which, bass.ds(c, KC)], ACT.Copy).then_inc(staged.h, 1)
                            for i in range(q * PG, q * PG + PG) if with_windows else ():
                                if not is_first(it, i - HOTB):
                                    act.wait_ge(pair_done.h, pair_done.at(i + 1 - HOTB) + it * (ROWB * PG))
                                h = i % HOTB * 2
                                for j in range(2):
                                    act.activation(away[:, h + j, :], iota_b[:, :], ACT.Abs, scale=-1.0,
                                                   bias=lo_s[:, bass.ds(it * (ROWB * KC) + 2 * i + j, 1)]).then_inc(away_made.h, 1)
                                act.wait_ge(away_made.h, away_made.at(2 * i + 2) + it * (2 * ROWB * PG))
                                act.activation(low_hot[:, h:h + 2, :], away[:, h:h + 2, :], ACT.Relu, scale=-1.0, bias=ones[:, 0:1])\
                                   .then_inc(lows_made.h, 1)
                    rounds(act, body)

                if with_windows:
                    @on(block.vector)
                    def _(dve):
                        def collect(it, i):
                            first = dve.value_load(win_i[0:1, bass.ds(it * (ROWB * PG) + i, 1)], min_val=0, max_val=NP - W)
                            dve.wait_ge(pair_done.h, pair_done.at(i + 1) + it * (ROWB * PG))
                            if not is_first(it, i - 1):
                                dve.wait_ge(taken.h, taken.at(i) + it * (ROWB * PG))
                            o = i % 4 * 2 * BANK
                            dve.tensor_tensor(between[:, :, bass.ds(first, W)], between[:, :, bass.ds(first, W)],
                                              acc[:, o:o + NB * WS].rearrange("p (b w) -> p b w", w=WS)[:, :, 0:W], ALU.add)
                            dve.tensor_tensor(by_dst[:, :, bass.ds(first, W)], by_dst[:, :, bass.ds(first, W)],
                                              acc[:, o + NB * WS:o + NB * WS + 2 * W].rearrange("p (k w) -> p k w", w=W), ALU.add)\
                               .then_inc(taken.h, 1)

                        def body(it, fresh, ends_here):
                            for i in range(ROWB * PG):
                                if not is_first(it, i - HOTB):
                                    dve.wait_ge(pair_done.h, pair_done.at(i + 1 - HOTB) + it * (ROWB * PG))
                                for j in range(2):
                                    at, h = bass.ds(it * (ROWB * KC) + 2 * i + j, 1), i % HOTB * 2 + j
                                    dve.tensor_scalar(wide_hot[:, h, :], iota_w[:, :], key_w[:, at], None, ALU.is_equal)
                                    ins = dve.tensor_scalar(win_hot[:, h, :], iota[:, 0:W], place_w[:, at], None, ALU.is_equal)
                                ins.then_inc(hots_made.h, 1)
                                if i >= 2:
                                    collect(it, i - 2)
                                elif not fresh:
                                    collect(it - 1, i - 2 + ROWB * PG)
                        rounds(dve, body)
                        for i in (ROWB * PG - 2, ROWB * PG - 1):
                            collect(ROUNDS - 1, i)

                    @on(block.tensor)
                    def _(pe):
                        def body(it, fresh, ends_here):
                            for i in range(ROWB * PG):
                                q, c = i // PG, i % PG * 2
                                pe.wait_ge(hots_made.h, hots_made.at(i + 1) + it * (ROWB * PG))
                                pe.wait_ge(lows_made.h, lows_made.at(i + 1) + it * (ROWB * PG))
                                if c == 0:
                                    pe.wait_ge(row_in[q].h, row_in[q].at(16 + 16 * (ends_here and q == ROWB - 1)) + it * 16)
                                if not is_first(it, i - 4):
                                    pe.wait_ge(taken.h, taken.at(i - 3) + it * (ROWB * PG))
                                o, h, o2 = i % 4 * 2 * BANK, i % HOTB * 2, i % 4 * 2 * BANK + NB * WS
                                for to, b0, b1 in ((o, 0, HBLOCKS), (o + BANK, HBLOCKS, NB)):
                                    for j in range(2):
                                        pe.matmul(acc[:, to:to + (b1 - b0) * WS].rearrange("p (b w) -> p b w", w=WS)[:, :, 0:W],
                                                  low_hot[:, h + j, :], wide_hot[:, h + j, b0 * W:b1 * W].rearrange("p (b w) -> p b w", w=W),
                                                  start=j == 0, stop=j == 1)
                                for j in range(2):
                                    pe.matmul(acc[:, o2:o2 + W], srow[:, q, c + j, 0:D], win_hot[:, h + j, :], start=j == 0, stop=j == 1)
                                for j in range(2):
                                    last = pe.matmul(acc[:, o2 + W:o2 + 2 * W], ones_b[:, :],
                                                     win_hot[:, h + j, :].bitcast(BF16).rearrange("p (w k) -> p w k", k=2)[:, :, 1:2],
                                                     start=j == 0, stop=j == 1)
                                last.then_inc(pair_done.h, 1)
                        rounds(pe, body)
            staged.passed(GROUPS)
            for q in range(ROWB):
                row_in[q].passed(16 * (ROUNDS + (q == ROWB - 1)))
                scattered[q].passed(ROUNDS * SC)
            if with_windows:
                for s in (hots_made, lows_made, pair_done, taken):
                    s.passed(PAIRS)
                away_made.passed(EC)

        scatter_rows(0, rows_by_src, True)

        rows_space.again()
        hots_space.again()
        rows_flat = rows_space.take([P, BUF * G, RW])
        onehot = hots_space.take([P, BUF * G, P])
        relq_flat = hots_space.take([P, BUF * G])
        excess = rows_space.take([P, NB])
        junk = rows_space.take([P, NP], U8)
        odd_all = sb("odd_all", [1, 4])


        slot_in = [signal(f"slot_in{q}") for q in range(BUF)]
        hot_ready = signal("hot_ready")
        hot_used = signal("hot_used")
        rel_ready = signal("rel_ready")
        evac = signal("evac")
        MLOOPS = SLOTS // MB

        def open_banks(pe, m=P):
            for k in range(BANKS):
                pe.matmul(acc[0:m, BANK * k:BANK * k + BANK], zeros[0:1, 0:m], zeros[0:1, :], start=True, stop=False)

        def close_banks(pe, m=P):
            for k in range(BANKS):
                last = pe.matmul(acc[0:m, BANK * k:BANK * k + BANK], zeros[0:1, 0:m], zeros[0:1, :], start=False, stop=True)
            return last

        def column(eng, which, slot):
            return eng.value_load(tab_row[0:1, which, 1, bass.ds(slot, 1)], min_val=0, max_val=NP - P)

        def first_row(eng, which, slot):
            return eng.value_load(tab_row[0:1, which, 0, bass.ds(slot, 1)], min_val=0, max_val=E - GS[which] * P)

        def sum_edges(which, rows_in, keep, to, on_act=None):
            g, bufs = GS[which], BUFS[which]
            loops = SLOTS_OF[which] // bufs
            rows = rows_flat.rearrange("p (q j) w -> p q j w", j=g)
            relq = relq_flat.rearrange("p (q j) -> p q j", j=g)
            with nc.Block() as block:
                @on(block.sync)
                def _(sp):
                    def body(it, fresh):
                        for q in range(bufs):
                            row = first_row(sp, which, it * bufs + q)
                            if not fresh:
                                sp.wait_ge(hot_used.h, hot_used.at(q + 1 - bufs) + it * bufs)
                            sp.dma_start(rows[:, q, :, :], rows_in[bass.ds(row, g * P), :].rearrange("(p j) w -> p j w", j=g))\
                              .then_inc(slot_in[q].h, 16)
                    body(0, True)
                    with sp.Fori(1, loops) as it:
                        body(it, False)

                @on(block.vector)
                def _(dve):
                    def body(it, fresh):
                        for q in range(bufs):
                            slot = it * bufs + q
                            dve.wait_ge(slot_in[q].h, slot_in[q].at(16) + it * 16)
                            if not fresh:
                                dve.wait_ge(hot_used.h, hot_used.at(q + 1 - bufs) + it * bufs)
                            key = rows[:, q, :, D + which:D + which + 1].bitcast(I32).rearrange("p j a -> p (j a)")
                            dve.tensor_tensor(relq[:, q, :], key, shifts[which][:, bass.ds(slot, 1), :].rearrange("p s j -> p (s j)"), ALU.add)\
                               .then_inc(rel_ready.h, 1)
                            if keep:
                                dve.tensor_tensor(rel[:, bass.ds(slot * g, g)], key, shifts[which][:, bass.ds(slot, 1), :].rearrange("p s j -> p (s j)"), ALU.add)
                                dve.tensor_copy(src_i[:, bass.ds(slot * g, g)], rows[:, q, :, D:D + 1].bitcast(I32).rearrange("p j a -> p (j a)"))
                            dve.wait_ge(rel_ready.h, rel_ready.at(q + 1) + it * bufs)
                            for j in range(g):
                                ins = dve.tensor_scalar(onehot[:, q * g + j, :], iota[:, :], relq[:, q, j:j + 1], None, ALU.is_equal)
                            ins.then_inc(hot_ready.h, 1)
                    body(0, True)
                    with dve.Fori(1, loops) as it:
                        body(it, False)
                    dve.wait_ge(evac.h, evac.at(1))
                    for k, c, w in banks():
                        dve.tensor_copy(to[:, c:c + w], acc[:, c:c + w])

                if on_act is not None:
                    @on(block.scalar)
                    def _(act):
                        on_act(act)

                @on(block.tensor)
                def _(pe):
                    open_banks(pe)

                    def body(it):
                        for q in range(bufs):
                            col = column(pe, which, it * bufs + q)
                            pe.wait_ge(hot_ready.h, hot_ready.at(q + 1) + it * bufs)
                            for j in range(g):
                                last = pe.matmul(acc[:, bass.ds(col, P)], rows[:, q, j, 0:D], onehot[:, q * g + j, :],
                                                 start=False, stop=False)
                            last.then_inc(hot_used.h, 1)
                    with pe.Fori(0, loops) as it:
                        body(it)
                    close_banks(pe).then_inc(evac.h, 1)
            for q in range(bufs):
                slot_in[q].passed(16 * loops)
            for s in (hot_ready, hot_used, rel_ready):
                s.passed(SLOTS_OF[which])
            evac.passed(1)

        checked = signal("checked")

        def check_counts(act):
            for b in range(NB):
                act.activation(junk[:, :], between[:, b, :], ACT.Relu, bias=low_bound[:, :], accum_out=excess[:, b:b + 1])\
                   .then_inc(checked.h, 1)
                if b < NB - 1:
                    act.wait_ge(checked.h, checked.at(b + 1))

        sum_edges(0, rows_by_src, False, agg_sum, check_counts)

        with nc.Block() as block:
            @on(block.vector)
            def _(dve):
                dve.tensor_reduce(odd[:, 2:3], excess[:, :], AX.X, ALU.add).then_inc(vec.h, 1)
                dve.wait_ge(sums.h, sums.at(1))
                dve.tensor_reduce(odd_all[:, 0:1], acc[0:1, 0:3], AX.X, ALU.add).then_inc(vec.h, 1)
                dve.wait_ge(vec.h, vec.at(2))
                dve.tensor_scalar(flags[:, FAST:FAST + 1], odd_all[:, 0:1], float(EP - E), None, ALU.is_equal)
                dve.tensor_scalar(flags[:, GENERAL:GENERAL + 1], odd_all[:, 0:1], float(EP - E), None, ALU.not_equal)

            @on(block.tensor)
            def _(pe):
                pe.wait_ge(vec.h, vec.at(1))
                pe.matmul(acc[0:1, 0:3], ones[:, 0:1], odd[:, :], start=True, stop=True).then_inc(sums.h, 1)
        vec.passed(2)
        sums.passed(1)

        with path(GENERAL):
            order(1)
            LB = 4
            with nc.Block() as block:
                @on(block.vector)
                def _(dve):
                    dve.tensor_scalar(buck_i[:, :], lo_i[:, :], P - 1, None, ALU.bitwise_and).then_inc(vec.h, 1)
                    dve.wait_ge(vec.h, vec.at(1))
                    dve.tensor_copy(lo_f[:, :], buck_i[:, :]).then_inc(vec.h, 1)
                    dve.wait_ge(vec.h, vec.at(2))
                    with dve.Fori(0, EC // LB) as it:
                        for q in range(LB):
                            dve.wait_ge(lo_used.h, it * LB + q + lo_used.at(1))
                            dve.tensor_scalar(hot_lo[:, q, :], iota_b[:, :], lo_f[:, bass.ds(it * LB + q, 1)], None,
                                              ALU.is_equal).then_inc(lo_hot.h, 1)
                    dve.wait_ge(sums.h, sums.at(1))
                    def step(ins, k):
                        ins.then_inc(vec.h, 1)
                        dve.wait_ge(vec.h, vec.at(k))
                    step(dve.tensor_copy(cnt_nm[:, :], acc[:, 0:NB]), 3)

                @on(block.tensor)
                def _(pe):
                    for q in range(LB):
                        pe.sem_inc(lo_used.h, 1)
                    pe.matmul(acc[:, 0:BANK], zeros[0:1, 0:P], zeros[0:1, :], start=True, stop=False)
                    with pe.Fori(0, EC // LB) as it:
                        for q in range(LB):
                            pe.wait_ge(lo_hot.h, it * LB + q + lo_hot.at(1))
                            pe.matmul(acc[:, 0:NB], hot_lo[:, q, :], hot[:, 0:NB, bass.ds(it * LB + q, 1)].rearrange("p b c -> p (b c)"),
                                      start=False, stop=False).then_inc(lo_used.h, 1)
                    pe.matmul(acc[:, 0:BANK], zeros[0:1, 0:P], zeros[0:1, :], start=False, stop=True).then_inc(sums.h, 1)

                @on(block.sync)
                def _(sp):
                    sp.wait_ge(vec.h, vec.at(3))
                    sp.dma_start(cnt_dram.rearrange("(b p) -> p b", p=P), cnt_nm[:, :]).then_inc(tabs_out.h, 16)
                    sp.wait_ge(tabs_out.h, tabs_out.at(16))
                    sp.dma_start(cnt_bc, cnt_dram.partition_broadcast(P)).then_inc(tabs_in.h, 16)
                    sp.wait_ge(tabs_in.h, tabs_in.at(16))
            vec.passed(3)
            sums.passed(1)
            tabs_out.passed(16)
            tabs_in.passed(16)
            lo_used.passed(EC + LB)
            lo_hot.passed(EC)

            rows_space.again()
            rows_space.take([P, ROWB, KC, RW])
            scatter_rows(1, rows_by_dst, False)
            sum_edges(1, rows_by_dst, True, agg_dst)

        mean_done = signal("mean_done")
        turned_out = signal("turned_out")
        relu_done = signal("relu_done")
        first_mm = signal("first_mm")
        hidden = signal("hidden")
        second_mm = signal("second_mm")
        added = signal("added")

        cleaned = signal("cleaned")

        def in_turn(stages):
            for k in range(BANKS + max(lag for _, lag in stages)):
                for stage, lag in stages:
                    if 0 <= k - lag < BANKS:
                        stage(*banks()[k - lag])

        def center(dve):
            for b in range(NB):
                ins = dve.bn_stats(stats[:, b, :], x_nm[:, b, :])
            ins.then_inc(vec.h, 1)
            dve.wait_ge(vec.h, vec.at(1))
            for b in range(NB):
                ins = dve.bn_aggr(mv[:, b, :], stats[:, b, :])
            ins.then_inc(vec.h, 1)
            dve.wait_ge(vec.h, vec.at(2))
            dve.tensor_scalar(rstd[:, :], mv[:, :, 1:2].rearrange("p b a -> p (b a)"), EPS, None, ALU.add).then_inc(vec.h, 1)
            dve.wait_ge(rooted.h, rooted.at(1))
            dve.reciprocal(rstd[:, :], std[:, :]).then_inc(vec.h, 1)
            dve.wait_ge(vec.h, vec.at(4))
            for b in range(NB):
                ins = dve.tensor_scalar(n_nm[:, b, :], x_nm[:, b, :], mv[:, b, 0:1], rstd[:, b:b + 1], ALU.subtract, ALU.mult)
                if b % 4 == 3 or b == NB - 1:
                    ins.then_inc(mean_done.h, 1)

        def norm_passed():
            vec.passed(4)
            rooted.passed(1)
            mean_done.passed(BANKS)
            turned_out.passed(BANKS)

        def norm():
            with nc.Block() as block:
                @on(block.vector)
                def _(dve):
                    center(dve)

                @on(block.tensor)
                def _(pe):
                    for k, c, w in banks():
                        pe.wait_ge(mean_done.h, mean_done.at(k + 1))
                        for b in range(w // P):
                            last = pe.transpose(acc[:, c + b * P:c + b * P + P], n_nm[:, 4 * k + b, :], ident[:, :])
                        last.then_inc(turned_out.h, 1)

                @on(block.scalar)
                def _(act):
                    act.wait_ge(vec.h, vec.at(3))
                    act.activation(std[:, :], rstd[:, :], ACT.Sqrt).then_inc(rooted.h, 1)
                    for k, c, w in banks():
                        act.wait_ge(turned_out.h, turned_out.at(k + 1))
                        act.activation(h_t[:, c:c + w], acc[:, c:c + w], ACT.Relu)
            norm_passed()

        def dense(parts, bias, w2, row, with_norm, on_sync=None):
            with nc.Block() as block:
                if on_sync is not None:
                    @on(block.sync)
                    def _(sp):
                        on_sync(sp)

                @on(block.tensor)
                def _(pe):
                    def first(k, c, w):
                        if with_norm:
                            pe.wait_ge(cleaned.h, cleaned.at(k + 1))
                        if k >= 2:
                            pe.wait_ge(hidden.h, hidden.at(k - 1))
                        for i, (wt, t) in enumerate(parts):
                            last = pe.matmul(acc[:, BANK * (k % 2):BANK * (k % 2) + w], wt, t[:, c:c + w],
                                             start=i == 0, stop=i == len(parts) - 1)
                        last.then_inc(first_mm.h, 1)

                    def second(k, c, w):
                        pe.wait_ge(hidden.h, hidden.at(k + 1))
                        if k >= 2:
                            pe.wait_ge(added.h, added.at(k - 1))
                        o = BANK * (2 + k % 2)
                        pe.matmul(acc[:, o:o + w], ones[0:1, 0:P], b_rows[0:1, row:row + 1, :].broadcast_to([1, w // P, D]),
                                  start=True, stop=False)
                        for b in range(w // P):
                            last = pe.matmul(acc[:, o + b * P:o + b * P + P], hid_t[:, c + b * P:c + b * P + P], w2,
                                             start=False, stop=b == w // P - 1)
                        last.then_inc(second_mm.h, 1)

                    def turn(k, c, w):
                        pe.wait_ge(mean_done.h, mean_done.at(k + 1))
                        if k >= 2:
                            pe.wait_ge(cleaned.h, cleaned.at(k - 1))
                        o = BANK * (4 + k % 2)
                        for b in range(w // P):
                            last = pe.transpose(acc[:, o + b * P:o + b * P + P], n_nm[:, 4 * k + b, :], ident[:, :])
                        last.then_inc(turned_out.h, 1)
                    in_turn(((turn, 0), (first, 1), (second, 2)) if with_norm else ((first, 0), (second, 1)))

                @on(block.scalar)
                def _(act):
                    def clean(k, c, w):
                        act.wait_ge(turned_out.h, turned_out.at(k + 1))
                        o = BANK * (4 + k % 2)
                        act.activation(h_t[:, c:c + w], acc[:, o:o + w], ACT.Relu).then_inc(cleaned.h, 1)

                    def hide(k, c, w):
                        act.wait_ge(first_mm.h, first_mm.at(k + 1))
                        act.activation(hid_t[:, c:c + w], acc[:, BANK * (k % 2):BANK * (k % 2) + w], ACT.Relu, bias=bias)\
                           .then_inc(hidden.h, 1)
                    if with_norm:
                        act.wait_ge(vec.h, vec.at(3))
                        act.activation(std[:, :], rstd[:, :], ACT.Sqrt).then_inc(rooted.h, 1)
                    in_turn(((clean, 0), (hide, 1)) if with_norm else ((hide, 0),))

                @on(block.vector)
                def _(dve):
                    if with_norm:
                        center(dve)
                    for k, c, w in banks():
                        dve.wait_ge(second_mm.h, second_mm.at(k + 1))
                        o = BANK * (2 + k % 2)
                        xb = x_nm[:, 4 * k:4 * k + w // P, :].rearrange("p b f -> p (b f)")
                        dve.tensor_tensor(xb, xb, acc[:, o:o + w], ALU.add).then_inc(added.h, 1)
            for s in (first_mm, hidden, second_mm, added):
                s.passed(BANKS)
            if with_norm:
                norm_passed()
                cleaned.passed(BANKS)

        with nc.Block() as block:
            @on(block.gpsimd)
            def _(pool):
                pool.tensor_tensor(agg_sum[:, :], agg_sum[:, :], agg_dst, ALU.add)

            @on(block.tensor)
            def _(pe):
                for b in range(NB):
                    last = pe.matmul(acc[:, b:b + 1], cnt_bc[0:1, b * P:b * P + P], ones[0:1, 0:1], start=True, stop=True)
                last.then_inc(sums.h, 1)

            @on(block.vector)
            def _(dve):
                dve.wait_ge(sums.h, sums.at(1))
                dve.tensor_scalar(degree[:, :], acc[:, 0:NB], 1.0, None, ALU.add).then_inc(vec.h, 1)
                dve.tensor_scalar(factors[:, 1, :], acc[:, 0:NB], 1.0, None, ALU.min)
                dve.tensor_scalar(factors[:, 0, :], acc[:, 0:NB], 1.0, None, ALU.max).then_inc(vec.h, 1)
                dve.wait_ge(vec.h, vec.at(2))
                dve.reciprocal(factors[:, 0, :], factors[:, 0, :]).then_inc(vec.h, 1)
                dve.wait_ge(rooted.h, rooted.at(1))
                dve.reciprocal(dinv_nm[:, :], root[:, :])

            @on(block.scalar)
            def _(act):
                act.wait_ge(vec.h, vec.at(1))
                act.activation(root[:, :], degree[:, :], ACT.Sqrt).then_inc(rooted.h, 1)
        vec.passed(3)
        rooted.passed(1)
        sums.passed(1)

        def spread_factors(sp):
            sp.dma_start(factor_dram.rearrange("k (b p) -> p k b", p=P), factors[:, :, :]).then_inc(tabs_out.h, 16)
            sp.wait_ge(tabs_out.h, tabs_out.at(16))
            sp.dma_start(mean_bc[:, :], factor_dram[0].partition_broadcast(P)).then_inc(tabs_in.h, 16)
            sp.dma_start(cnt_bc[0:1, :], factor_dram[1:2, :]).then_inc(tabs_in.h, 16)
            sp.wait_ge(tabs_in.h, tabs_in.at(32))

        dense([(w_l0[:, 0, :], h_t), (w_l0[:, 1, :], agg_sum)], b_cols[:, 0:1], w2_l0[:, :], 0, True, spread_factors)
        tabs_out.passed(16)
        tabs_in.passed(32)
        dense([(w_l1[:, 0, :], h_t), (w_l1[:, 1, :], agg_dst)], b_cols[:, 1:2], w2_l1[:, :], 1, True)
        norm()

        table_out = signal("table_out")
        gathered = [signal(f"gathered{q}") for q in range(BUF)]
        idx_ready = signal("idx_ready")
        z_nm, z_rest = n_nm[:, :, 0:H2], n_nm[:, :, H2:2 * H2]
        y_nm = agg_dst.rearrange("p (b f) -> p b f", f=D)[:, :, 0:H2]
        parts_space = Space(agg_sum[:, :], F32)
        z_parts = parts_space.take([P, NB, 3 * H2], BF16)
        exact = Space(h_t[:, :], F32).take([P, 2, NB, P], BF16)
        cast = [signal(f"cast{h}") for h in range(2)]
        parted = signal("parted")
        summed_z = signal("summed_z")
        read_z = signal("read_z")
        dinv_z = dinv_nm[:, :].rearrange("p (b a) -> p b a", a=1).broadcast_to([P, NB, H2])

        def flight_buffers():
            slot_space.again()
            return (slot_space.take([P, MB * G, P]), slot_space.take([P, MB, G], I32), slot_space.take([P, MB * G, D]))

        def store_table(sp, table, tile):
            sp.dma_start(table.rearrange("(b p) f -> p b f", p=P), tile).then_inc(table_out.h, 16)
            sp.wait_ge(table_out.h, table_out.at(16))

        slot_onehot, idxq, got = flight_buffers()

        def gather_z(table):
            with nc.Block() as block:
                @on(block.vector)
                def _(dve):
                    def body(it, fresh):
                        for q in range(MB):
                            slot = it * MB + q
                            if not fresh:
                                dve.wait_ge(gathered[q].h, gathered[q].at(0) + it * (16 * G))
                            dve.tensor_copy(idxq[:, q, :], src_i[:, bass.ds(slot * G, G)]).then_inc(idx_ready.h, 1)
                            if not fresh:
                                dve.wait_ge(hot_used.h, hot_used.at(q + 1 - MB) + it * MB)
                            for j in range(G):
                                ins = dve.tensor_scalar(slot_onehot[:, q * G + j, :], iota[:, :], rel[:, bass.ds(slot * G + j, 1)], None, ALU.is_equal)
                            ins.then_inc(hot_ready.h, 1)
                    body(0, True)
                    with dve.Fori(1, MLOOPS) as it:
                        body(it, False)

                @on(block.gpsimd)
                def _(pool):
                    def body(it, fresh):
                        for q in range(MB):
                            pool.wait_ge(idx_ready.h, idx_ready.at(q + 1) + it * MB)
                            if not fresh:
                                pool.wait_ge(hot_used.h, hot_used.at(q + 1 - MB) + it * MB)
                            pool.sem_inc(cleared.h, 1)
                            for j in range(G):
                                pool.indirect_dma_start(got[:, q * G + j, 0:H2], None, table,
                                                        bass.IndirectOffsetOnAxis(ap=idxq[:, q, j:j + 1], axis=0)).then_inc(gathered[q].h, 16)
                    body(0, True)
                    with pool.Fori(1, MLOOPS) as it:
                        body(it, False)

                @on(block.tensor)
                def _(pe):
                    open_banks(pe, H2)
                    with pe.Fori(0, MLOOPS) as it:
                        for q in range(MB):
                            col = column(pe, 1, it * MB + q)
                            pe.wait_ge(hot_ready.h, hot_ready.at(q + 1) + it * MB)
                            pe.wait_ge(gathered[q].h, gathered[q].at(16 * G) + it * (16 * G))
                            for j in range(G):
                                last = pe.matmul(acc[0:H2, bass.ds(col, P)], got[:, q * G + j, 0:H2], slot_onehot[:, q * G + j, :],
                                                 start=False, stop=False)
                            last.then_inc(hot_used.h, 1)
                    close_banks(pe, H2)
            for s in (idx_ready, hot_ready, hot_used):
                s.passed(SLOTS)
            for q in range(MB):
                gathered[q].passed(16 * G * MLOOPS)

        def spread():
            def convert(eng, half, it, u):
                b0, b1 = ((0, ACT_BLOCKS), (ACT_BLOCKS, NB))[half]
                if not (isinstance(it, int) and it == 0 and u < 2):
                    eng.wait_ge(summed_z.h, summed_z.at(u - 1) + it * UB)
                of, to = between[:, b0:b1, bass.ds(it * (UB * P) + u * P, P)], exact[:, u % 2, b0:b1, :]
                if half == 0:
                    eng.activation(to, of, ACT.Copy).then_inc(cast[half].h, 1)
                else:
                    eng.tensor_copy(to, of).then_inc(cast[half].h, 1)

            with path(FAST):
                with nc.Block() as block:
                    @on(block.vector)
                    def _(dve):
                        dve.tensor_copy(z_parts[:, :, 0:H2], z_nm).then_inc(parted.h, 1)
                        dve.wait_ge(parted.h, parted.at(1))
                        dve.tensor_tensor(z_rest, z_nm, z_parts[:, :, 0:H2], ALU.subtract).then_inc(parted.h, 1)
                        dve.wait_ge(parted.h, parted.at(2))
                        dve.tensor_copy(z_parts[:, :, H2:2 * H2], z_rest).then_inc(parted.h, 1)
                        dve.wait_ge(parted.h, parted.at(3))
                        dve.tensor_tensor(z_parts[:, :, 2 * H2:3 * H2], z_rest, z_parts[:, :, H2:2 * H2], ALU.subtract).then_inc(parted.h, 1)
                        def add_up(it, u):
                            dve.wait_ge(summed_z.h, summed_z.at(u + 1) + it * UB)
                            dve.tensor_reduce(agg_dst[:, bass.ds(it * (UB * D) + u * D, H2)],
                                              acc[:, u * BANK:u * BANK + 3 * H2].rearrange("p (k f) -> p f k", f=H2), AX.X, ALU.add)\
                               .then_inc(read_z.h, 1)

                        def body(it, fresh):
                            for u in range(UB):
                                convert(dve, 1, it, u)
                                if u >= 1:
                                    add_up(it, u - 1)
                                elif not fresh:
                                    add_up(it - 1, UB - 1)
                        body(0, True)
                        with dve.Fori(1, NB // UB) as it:
                            body(it, False)
                        for u in range(NB % UB + 1):
                            if u < NB % UB:
                                convert(dve, 1, NB // UB, u)
                            add_up(NB // UB - (u == 0), (u - 1) % UB)

                    @on(block.scalar)
                    def _(act):
                        for u in range(UB):
                            convert(act, 0, 0, u)
                        with act.Fori(1, NB // UB) as it:
                            for u in range(UB):
                                convert(act, 0, it, u)
                        for u in range(NB % UB):
                            convert(act, 0, NB // UB, u)

                    @on(block.tensor)
                    def _(pe):
                        pe.wait_ge(parted.h, parted.at(4))

                        def body(it, fresh, blocks=UB):
                            for u in range(blocks):
                                for h in range(2):
                                    pe.wait_ge(cast[h].h, cast[h].at(u + 1) + it * UB)
                                if not fresh:
                                    pe.wait_ge(read_z.h, read_z.at(u + 1 - UB) + it * UB)
                                for b in range(NB):
                                    last = pe.matmul(acc[:, u * BANK:u * BANK + 3 * H2], exact[:, u % 2, b, :], z_parts[:, b, :],
                                                     start=b == 0, stop=b == NB - 1)
                                last.then_inc(summed_z.h, 1)
                        body(0, True)
                        with pe.Fori(1, NB // UB) as it:
                            body(it, False)
                        body(NB // UB, False, NB % UB)
                parted.passed(4)
                for c in (summed_z, read_z, *cast):
                    c.passed(NB)
            with path(GENERAL):
                with nc.Block() as block:
                    @on(block.sync)
                    def _(sp):
                        store_table(sp, z_table, z_nm)
                table_out.passed(16)
                gather_z(z_table)
                with nc.Block() as block:
                    @on(block.vector)
                    def _(dve):
                        for k, c, w in banks():
                            ins = dve.tensor_copy(agg_sum[0:H2, c:c + w], acc[0:H2, c:c + w])
                        ins.then_inc(first_mm.h, 1)
                        dve.wait_ge(turned_out.h, turned_out.at(1))
                        dve.tensor_copy(y_nm, acc[:, 0:NB * H2].rearrange("p (b f) -> p b f", f=H2))

                    @on(block.tensor)
                    def _(pe):
                        pe.wait_ge(first_mm.h, first_mm.at(1))
                        for b in range(NB):
                            last = pe.transpose(acc[:, b * H2:b * H2 + H2], agg_sum[0:H2, b * P:b * P + P], ident[0:H2, 0:H2])
                        last.then_inc(turned_out.h, 1)
                first_mm.passed(1)
                turned_out.passed(1)

        with nc.Block() as block:
            @on(block.vector)
            def _(dve):
                dve.wait_ge(first_mm.h, first_mm.at(1))
                dve.tensor_tensor(z_nm, acc[:, 0:NB * H2].rearrange("p (b f) -> p b f", f=H2), dinv_z, ALU.mult)

            @on(block.tensor)
            def _(pe):
                for b in range(NB):
                    last = pe.matmul(acc[:, b * H2:b * H2 + H2], h_t[:, b * P:b * P + P], w1_g[:, :], start=True, stop=True)
                last.then_inc(first_mm.h, 1)
        first_mm.passed(1)

        spread()

        with nc.Block() as block:
            @on(block.tensor)
            def _(pe):
                pe.matmul(acc[:, 0:H2], ones[0:1, 0:P], b1_row[:, :], start=True, stop=True).then_inc(first_mm.h, 1)

            @on(block.vector)
            def _(dve):
                dve.tensor_tensor(y_nm, y_nm, z_nm, ALU.add).then_inc(vec.h, 1)
                dve.wait_ge(vec.h, vec.at(1))
                dve.tensor_tensor(y_nm, y_nm, dinv_z, ALU.mult).then_inc(vec.h, 1)
                dve.wait_ge(vec.h, vec.at(2))
                dve.wait_ge(first_mm.h, first_mm.at(1))
                dve.tensor_tensor(y_nm, y_nm, acc[:, 0:H2].rearrange("p (a f) -> p a f", a=1).broadcast_to([P, NB, H2]), ALU.add)\
                   .then_inc(vec.h, 1)
                dve.wait_ge(vec.h, vec.at(3))
                dve.scalar_tensor_tensor(z_nm, y_nm, 0.0, dinv_z, ALU.max, ALU.mult)
        vec.passed(3)
        first_mm.passed(1)

        spread()

        with nc.Block() as block:
            @on(block.vector)
            def _(dve):
                dve.tensor_tensor(y_nm, y_nm, z_nm, ALU.add).then_inc(vec.h, 1)
                dve.wait_ge(vec.h, vec.at(1))
                dve.tensor_tensor(y_nm, y_nm, dinv_z, ALU.mult).then_inc(vec.h, 1)
                for k, c, w in banks():
                    dve.wait_ge(second_mm.h, second_mm.at(k + 1))
                    xb = x_nm[:, 4 * k:4 * k + w // P, :].rearrange("p b f -> p (b f)")
                    dve.tensor_tensor(xb, xb, acc[:, c:c + w], ALU.add)

            @on(block.tensor)
            def _(pe):
                pe.wait_ge(vec.h, vec.at(2))
                for k, c, w in banks():
                    for b in range(w // P):
                        last = pe.transpose(acc[0:H2, c + b * P:c + b * P + P], y_nm[:, 4 * k + b, :], ident[:, :])
                    last.then_inc(turned_out.h, 1)
                for k, c, w in banks():
                    pe.wait_ge(hidden.h, hidden.at(k + 1))
                    pe.matmul(acc[:, c:c + w], ones[0:1, 0:P], b_rows[0:1, 2:3, :].broadcast_to([1, w // P, D]), start=True, stop=False)
                    for b in range(w // P):
                        last = pe.matmul(acc[:, c + b * P:c + b * P + P], h_t[0:H2, c + b * P:c + b * P + P], w2_g[:, :],
                                         start=False, stop=b == w // P - 1)
                    last.then_inc(second_mm.h, 1)

            @on(block.scalar)
            def _(act):
                for k, c, w in banks():
                    act.wait_ge(turned_out.h, turned_out.at(k + 1))
                    act.activation(h_t[0:H2, c:c + w], acc[0:H2, c:c + w], ACT.Copy).then_inc(hidden.h, 1)
        vec.passed(2)
        for s in (turned_out, hidden, second_mm):
            s.passed(BANKS)
        norm()

        p_nm = n_nm
        q_nm = agg_dst.rearrange("p (b f) -> p b f", f=D)
        with nc.Block() as block:
            @on(block.tensor)
            def _(pe):
                for k, c, w in banks():
                    for b in range(w // P):
                        last = pe.matmul(acc[:, c + b * P:c + b * P + P], h_t[:, c + b * P:c + b * P + P], w_msg[:, 0, :], start=True, stop=True)
                    last.then_inc(first_mm.h, 1)
                for k, c, w in banks():
                    pe.wait_ge(added.h, added.at(k + 1))
                    pe.matmul(acc[:, c:c + w], ones[0:1, 0:P], b_rows[0:1, 4:5, :].broadcast_to([1, w // P, D]), start=True, stop=False)
                    for b in range(w // P):
                        last = pe.matmul(acc[:, c + b * P:c + b * P + P], h_t[:, c + b * P:c + b * P + P], w_msg[:, 1, :],
                                         start=False, stop=b == w // P - 1)
                    last.then_inc(second_mm.h, 1)

            @on(block.vector)
            def _(dve):
                for k, c, w in banks():
                    dve.wait_ge(first_mm.h, first_mm.at(k + 1))
                    dve.tensor_copy(p_nm[:, :, :].rearrange("p b f -> p (b f)")[:, c:c + w], acc[:, c:c + w]).then_inc(added.h, 1)

            @on(block.scalar)
            def _(act):
                for k, c, w in banks():
                    act.wait_ge(second_mm.h, second_mm.at(k + 1))
                    act.activation(agg_dst[:, c:c + w], acc[:, c:c + w], ACT.Copy)

            @on(block.sync)
            def _(sp):
                sp.wait_ge(added.h, added.at(BANKS))
                store_table(sp, p_table, p_nm[:, :, :])
        for s, k in ((first_mm, BANKS), (added, BANKS), (second_mm, BANKS), (table_out, 16)):
            s.passed(k)

        with path(FAST):
            slot_space.again()
            q_parts = slot_space.take([P, NB, 3, D], BF16)

            def part_of(k, c, w):
                return q_parts[:, c // D:(c + w) // D, k, :]

            def by_block(flat, c, w):
                return flat[:, c:c + w].rearrange("p (b f) -> p b f", f=D)

            with nc.Block() as block:
                @on(block.scalar)
                def _(act):
                    for k, c, w in banks():
                        act.activation(part_of(0, c, w), by_block(agg_dst, c, w), ACT.Copy).then_inc(first_mm.h, 1)
                    for k, c, w in banks():
                        act.wait_ge(added.h, added.at(k + 1))
                        act.activation(part_of(1, c, w), by_block(n_flat, c, w), ACT.Copy).then_inc(second_mm.h, 1)

                @on(block.vector)
                def _(dve):
                    dve.memset(agg_sum[:, :], 0.0)
                    for k, c, w in banks():
                        dve.wait_ge(first_mm.h, first_mm.at(k + 1))
                        dve.tensor_tensor(by_block(n_flat, c, w), by_block(agg_dst, c, w), part_of(0, c, w), ALU.subtract).then_inc(added.h, 1)
                    for k, c, w in banks():
                        dve.wait_ge(second_mm.h, second_mm.at(k + 1))
                        dve.tensor_tensor(part_of(2, c, w), by_block(n_flat, c, w), part_of(1, c, w), ALU.subtract).then_inc(hidden.h, 1)

                @on(block.sync)
                def _(sp):
                    sp.wait_ge(second_mm.h, second_mm.at(BANKS))
                    sp.wait_ge(hidden.h, hidden.at(BANKS))
                    store_table(sp, q_table.rearrange("(n k) f -> n (k f)", k=3), q_parts[:, :, :, :].rearrange("p b k f -> p b (k f)"))
            for s in (first_mm, second_mm, hidden, added):
                s.passed(BANKS)
            table_out.passed(16)
        with path(GENERAL):
            with nc.Block() as block:
                @on(block.vector)
                def _(dve):
                    dve.memset(agg_sum[:, :], 0.0)

        slot_space.again()
        onehot = slot_space.take([P, FL * G, P])
        idxq = slot_space.take([P, FL, G], I32)
        got = slot_space.take([P, FL, G * D])
        rows = slot_space.take([P, FL, G, D])
        turned = slot_space.take([P, 2, 2 * G * P])
        msg = slot_space.take([P, MR, G * D])
        relued = slot_space.take([P, MR, G, D])
        q_win = slot_space.take([3 * W, FL, D], BF16)
        win_turned = slot_space.take([3 * W, FL, SLOT], BF16)
        dst_of = slot_space.take([3 * W, 2, DG * SLOT], I32)

        turn = signal("turn")
        turn_out = signal("turn_out")
        made = signal("made")
        plus = signal("plus")
        cut = signal("cut")
        collected = signal("collected")
        summed = signal("summed")
        win_in = [signal(f"win_in{q}") for q in range(FL)]
        dst_in = [signal(f"dst_in{h}") for h in range(2)]

        def sum_messages(windows):
            loops, width = (PAIRS // FL, W) if windows else (SLOTS // FL, P)
            T_AT, M_AT, S_AT = 0, 2 * BANK, (2 + MR) * BANK

            def first_node(eng, n):
                if windows:
                    return eng.value_load(win_i[0:1, bass.ds(n, 1)], min_val=0, max_val=NP - W)
                return column(eng, 1, n)

            def is_first(it, i):
                return isinstance(it, int) and it == 0 and i < 0

            def slot_of(i):
                return i % MR

            def stages(eng, *lagged, ends=False, parts=({},)):
                def body(it, fresh, **at_end):
                    for i in range(FL):
                        for stage, lag, part in ((stage, lag, part) for part in parts for stage, lag in lagged):
                            more = {**part, **(at_end if lag == 0 else {})}
                            if i >= lag:
                                stage(it, i - lag, **more)
                            elif not fresh:
                                stage(it - 1, i - lag + FL, **more)
                if ends:
                    body(0, True, ends_here=False)
                    with eng.Fori(1, loops - 1) as it:
                        body(it, False, ends_here=False)
                    body(loops - 1, False, ends_here=True)
                else:
                    body(0, True)
                    with eng.Fori(1, loops) as it:
                        body(it, False)
                for i in range(FL, FL + max(lag for _, lag in lagged)):
                    for part in parts:
                        for stage, lag in lagged:
                            if lag > i - FL:
                                stage(loops - 1, i - lag, **part)

            with nc.Block() as block:
                @on(block.sync)
                def _(sp):
                    def load(it, q, ends_here):
                        n = it * FL + q
                        if windows:
                            first, e = first_node(sp, n), n * SLOT
                        else:
                            row = first_row(sp, 1, n)
                        if not (isinstance(it, int) and it == 0):
                            sp.wait_ge(made.h, made.at(q + (DG if windows and q % DG == 0 else 1) - FL) + it * FL)
                        if not windows:
                            sp.dma_start(rows[:, q, :, :], rows_by_dst[bass.ds(row, SLOT), 0:D].rearrange("(p j) w -> p j w", j=G))\
                              .then_inc(slot_in[q].h, 16)
                            return
                        if q % DG == 0:
                            if ends_here and q + DG == FL:
                                sp.dma_start(dst_of[:, q // DG, 0:E - n * SLOT], dst[n * SLOT:E].partition_broadcast(3 * W))\
                                  .then_inc(dst_in[q // DG].h, 16)
                            else:
                                sp.dma_start(dst_of[:, q // DG, :], dst[bass.ds(e, DG * SLOT)].partition_broadcast(3 * W))\
                                  .then_inc(dst_in[q // DG].h, 16)
                        if ends_here and q == FL - 1:
                            sp.dma_start(rows[:, q, 0, :], ea[e:e + P, :]).then_inc(slot_in[q].h, 16)
                            sp.dma_start(rows[0:ELAST, q, 1, :], ea[e + P:E, :]).then_inc(slot_in[q].h, 16)
                        else:
                            sp.dma_start(rows[:, q, :, :], ea[bass.ds(e, SLOT), :].rearrange("(j p) w -> p j w", j=G))\
                              .then_inc(slot_in[q].h, 16)
                        sp.dma_start(q_win[:, q, :], q_table[bass.ds(first * 3, 3 * W), :]).then_inc(win_in[q].h, 16)
                    stages(sp, (load, 0), ends=True)

                @on(block.gpsimd)
                def _(pool):
                    def gather(it, q):
                        pool.wait_ge(idx_ready.h, idx_ready.at(q + 1) + it * FL)
                        if not (isinstance(it, int) and it == 0):
                            pool.wait_ge(plus.h, plus.at(q + 1 - FL) + it * FL)
                        pool.sem_inc(cleared.h, 1)
                        for j in range(G):
                            pool.indirect_dma_start(got[:, q, j * D:(j + 1) * D], None, p_table,
                                                    bass.IndirectOffsetOnAxis(ap=idxq[:, q, j:j + 1], axis=0)).then_inc(gathered[q].h, 16)
                    stages(pool, (gather, 0))

                @on(block.vector)
                def _(dve):
                    places, sources = (place_w, src_g) if windows else (rel, src_i)

                    def index(it, q, ends_here):
                        n = it * FL + q
                        if not (isinstance(it, int) and it == 0):
                            dve.wait_ge(gathered[q].h, gathered[q].at(0) + it * (16 * G))
                        dve.tensor_copy(idxq[:, q, :], sources[:, bass.ds(n * G, G)]).then_inc(idx_ready.h, 1)
                        if not (isinstance(it, int) and it == 0):
                            dve.wait_ge(summed.h, summed.at(q + 1 - FL) + it * FL)
                        if windows:
                            if q % DG == 0:
                                dve.wait_ge(dst_in[q // DG].h, dst_in[q // DG].at(16) + it * 16)
                            w = ELAST + P if ends_here and q == FL - 1 else SLOT
                            dve.tensor_scalar(win_turned[:, q, 0:w], dst_of[:, q // DG, q % DG * SLOT:q % DG * SLOT + w],
                                              win_nodes[:, bass.ds(n, 1)], None, ALU.is_equal)
                        for j in range(G):
                            ins = dve.tensor_scalar(onehot[:, q * G + j, 0:width], iota[:, 0:width], places[:, bass.ds(n * G + j, 1)], None,
                                                    ALU.is_equal)
                        ins.then_inc(hot_ready.h, 1)

                    def add(it, i):
                        dve.wait_ge(made.h, made.at(i + 1) + it * FL)
                        dve.wait_ge(gathered[i].h, gathered[i].at(16 * G) + it * (16 * G))
                        if not is_first(it, i - MR):
                            dve.wait_ge(cut.h, cut.at(i + 1 - MR) + it * FL)
                        o = M_AT + slot_of(i) * BANK
                        dve.tensor_tensor(msg[:, slot_of(i), :], acc[:, o:o + G * D], got[:, i, :], ALU.add).then_inc(plus.h, 1)

                    def collect(it, i):
                        col = first_node(dve, it * FL + i)
                        dve.wait_ge(summed.h, summed.at(i + 1) + it * FL)
                        if not is_first(it, i - 1):
                            dve.wait_ge(collected.h, collected.at(i) + it * FL)
                        o = S_AT + i % 2 * BANK
                        dve.tensor_tensor(agg_sum[:, bass.ds(col, width)], agg_sum[:, bass.ds(col, width)], acc[:, o:o + width], ALU.add)\
                           .then_inc(collected.h, 1)

                    stages(dve, (index, 0), (add, 4), (collect, 6), ends=True)

                @on(block.scalar)
                def _(act):
                    def out_of_psum(it, i):
                        act.wait_ge(turn.h, turn.at(i + 1) + it * FL)
                        if not is_first(it, i - 2):
                            act.wait_ge(made.h, made.at(i - 1) + it * FL)
                        o, w = T_AT + i % 2 * BANK, G * P * (1 if windows else 2)
                        act.activation(turned[:, i % 2, 0:w], acc[:, o:o + w], ACT.Copy).then_inc(turn_out.h, 1)

                    def relu(it, i):
                        act.wait_ge(plus.h, plus.at(i + 1) + it * FL)
                        if not is_first(it, i - MR):
                            act.wait_ge(summed.h, summed.at(i + 1 - MR) + it * FL)
                        act.activation(relued[:, slot_of(i), :, :].rearrange("p j f -> p (j f)"), msg[:, slot_of(i), :], ACT.Relu).then_inc(cut.h, 1)
                    stages(act, (out_of_psum, 0), (relu, 2))

                @on(block.tensor)
                def _(pe):
                    def turn_rows(it, i, j, ends_here):
                        if j == 0:
                            if not windows:
                                pe.wait_ge(hot_ready.h, hot_ready.at(i + 1) + it * FL)
                            pe.wait_ge(slot_in[i].h, slot_in[i].at(16 + 16 * (windows and ends_here and i == FL - 1)) + it * 16)
                            if not is_first(it, i - 2):
                                pe.wait_ge(turn_out.h, turn_out.at(i - 1) + it * FL)
                        o = T_AT + i % 2 * BANK + j * P
                        last = pe.transpose(acc[:, o:o + P], rows[:, i, j, :], ident[:, :])
                        if not windows:
                            last = pe.transpose(acc[:, o + G * P:o + (G + 1) * P], onehot[:, i * G + j, :], ident[:, :])
                        if j == G - 1:
                            last.then_inc(turn.h, 1)

                    def total(it, i, j):
                        if j == 0:
                            pe.wait_ge(cut.h, cut.at(i + 1) + it * FL)
                            if not is_first(it, i - 2):
                                pe.wait_ge(collected.h, collected.at(i - 1) + it * FL)
                        o = S_AT + i % 2 * BANK
                        last = pe.matmul(acc[:, o:o + width], relued[:, slot_of(i), j, :], onehot[:, i * G + j, 0:width],
                                         start=j == 0, stop=j == G - 1)
                        if j == G - 1:
                            last.then_inc(summed.h, 1)

                    def product(it, i, j):
                        if j == 0:
                            if windows:
                                pe.wait_ge(win_in[i].h, win_in[i].at(16) + it * 16)
                            pe.wait_ge(hot_ready.h, hot_ready.at(i + 1) + it * FL)
                            pe.wait_ge(turn_out.h, turn_out.at(i + 1) + it * FL)
                            if not is_first(it, i - MR):
                                pe.wait_ge(plus.h, plus.at(i + 1 - MR) + it * FL)
                        o, t = M_AT + slot_of(i) * BANK + j * P, i % 2
                        if windows:
                            pe.matmul(acc[:, o:o + P], win_turned[:, i, j * P:(j + 1) * P], q_win[:, i, :], start=True, stop=False)
                        else:
                            col = column(pe, 1, it * FL + i)
                            pe.matmul(acc[:, o:o + P], turned[:, t, (G + j) * P:(G + j + 1) * P], agg_dst[:, bass.ds(col, P)],
                                      start=True, stop=False)
                        last = pe.matmul(acc[:, o:o + P], turned[:, t, j * P:(j + 1) * P], w_msg[:, 2, :], start=False, stop=True)
                        if j == G - 1:
                            last.then_inc(made.h, 1)
                    stages(pe, (turn_rows, 0), (total, 3), (product, 1), ends=True, parts=[{"j": j} for j in range(G)])
            steps = loops * FL
            for s in (turn, turn_out, made, plus, cut, summed, hot_ready, idx_ready, collected):
                s.passed(steps)

        with path(FAST):
            sum_messages(True)
        with path(GENERAL):
            sum_messages(False)

        out_done = signal("out_done")

        def store_x(sp):
            for k, c, w in banks():
                sp.wait_ge(added.h, added.at(k + 1))
                if k < BANKS - 1:
                    sp.dma_start(out[c:c + w, :].rearrange("(b p) f -> p b f", p=P), x_nm[:, 4 * k:4 * k + 4, :]).then_inc(out_done.h, 16)
                else:
                    sp.dma_start(out[c:N, :], x_nm[0:NLAST, NB - 1, :]).then_inc(out_done.h, 16)
            sp.wait_ge(out_done.h, out_done.at(16 * BANKS))

        with nc.Block() as block:
            @on(block.vector)
            def _(dve):
                for k, c, w in banks():
                    dve.tensor_tensor(hid_t[:, c:c + w], agg_sum[:, c:c + w], mean_bc[:, c:c + w], ALU.mult).then_inc(first_mm.h, 1)

            @on(block.tensor)
            def _(pe):
                for k, c, w in banks():
                    pe.wait_ge(first_mm.h, first_mm.at(k + 1))
                    pe.matmul(acc[:, c:c + w], w2_msg[:, :], hid_t[:, c:c + w], start=True, stop=False)
                    pe.matmul(acc[:, c:c + w], b_rows[0:1, 5, :], cnt_bc[0:1, c:c + w], start=False, stop=True).then_inc(second_mm.h, 1)

            @on(block.scalar)
            def _(act):
                for k, c, w in banks():
                    act.wait_ge(second_mm.h, second_mm.at(k + 1))
                    act.activation(agg_dst[:, c:c + w], acc[:, c:c + w], ACT.Copy)
        first_mm.passed(BANKS)
        second_mm.passed(BANKS)
        dense([(w_upd[:, 0, :], h_t), (w_upd[:, 1, :], agg_dst)], b_cols[:, 3:4], w2_upd[:, :], 3, False, store_x)


_INS = ["x", "src", "dst", "edge_attr_128"] + [f"L0_gnn_{n}" for n in ("W1", "b1", "W2", "b2")] \
    + [f"L1_gnn_{n}" for n in ("W1", "b1", "W2", "b2")] + [f"L2_gnn_{n}" for n in ("W1", "b1", "W2", "b2")] \
    + [f"L3_gnn_{a}_{n}" for a in ("msg", "upd") for n in ("w1", "b1", "w2", "b2")]


def kernel(**inputs):
    import numpy as _np
    import concourse.bacc as _bacc
    from concourse import mybir as _mybir
    from concourse.bass_utils import run_bass_kernel_spmd as _run

    nc = _bacc.Bacc("TRN2", target_bir_lowering=False, num_devices=1)
    arrays, args = {}, []
    for name in _INS:
        a = _np.ascontiguousarray(inputs[name])
        arrays[f"in_{name}"] = a
        args.append(nc.dram_tensor(f"in_{name}", a.shape, _mybir.dt.from_np(a.dtype), kind="ExternalInput").ap())
    out = nc.dram_tensor("out", (N, D), F32, kind="ExternalOutput").ap()
    build(nc, *args[0:4], args[4:8], args[8:12], args[12:16], args[16:24], out)
    r = _run(nc, [arrays], core_ids=[0])
    return r.results[0]["out"]
```
